# Optimizing a Trainium2 kernel written in Bass

```python
import numpy as np
import jax
import jax.numpy as jnp

def _softmax(x, axis=-1):
    return jax.nn.softmax(x, axis=axis)

def _gelu(x):
    return jax.nn.gelu(x, approximate=True)

def _silu(x):
    return jax.nn.silu(x)

def _sigmoid(x):
    return jax.nn.sigmoid(x)

def _layernorm(x, axis=-1, eps=1e-05):
    m = jnp.mean(x, axis=axis, keepdims=True)
    v = jnp.var(x, axis=axis, keepdims=True)
    return (x - m) / jnp.sqrt(v + eps)

def _scatter_add(tgt, idx, src, axis=0):
    return tgt.at[idx].add(src)

def _segment_sum(src, seg, n):
    return jax.ops.segment_sum(src, seg, n)
kernel_name = 'mk_adj_resnorm_d1_adj_r2_e85170'

def setup_inputs(seed: int=0):
    np.random.seed(seed)
    _w = jnp.asarray

    def _rec_inputs():
        import jax
        import jax.numpy as jnp
        _gk = jax.random.key(seed)
        x = -0.000929 + 1 * jax.random.normal(jax.random.fold_in(_gk, 1), (4096, 128), jnp.float32)
        _w = (1.0 + jnp.arange(4096, dtype=jnp.float32)) ** (-0.5)
        _w = _w / _w.mean()
        _pij = jnp.clip(0.00195312 * _w[:, None] * _w[None, :], 0.0, 1.0)
        _a = jax.random.uniform(jax.random.fold_in(_gk, 2), (4096, 4096)) < _pij
        _a = jnp.logical_or(_a, jnp.eye(4096, dtype=bool))
        _af = _a.astype(jnp.float32)
        _af = _af * jax.random.uniform(jax.random.fold_in(_gk, 3), (4096, 4096), jnp.float32, 0.05, 1)
        adj = _af
        return (x, adj)
    x, adj = _rec_inputs()

    def _L0_gnn_setup():
        import jax, jax.numpy as jnp
        import numpy as np
        N, H, HEADS = (2048, 128, 3)
        ALPHA = 0.2
        NEG_INF = -9000000000000000.0

        def _sign_adj(key, n, density):
            k1, k2 = jax.random.split(key)
            mask = jax.random.uniform(k1, (n, n)) < density
            sign = jnp.where(jax.random.uniform(k2, (n, n)) < 0.5, -1.0, 1.0)
            adj = jnp.where(mask, sign, 0.0).astype(jnp.float32)
            idx = jnp.arange(n)
            return adj.at[idx, idx].set(1.0)

        def _gru_cell(x, hstate, Wih, Whh, bih, bhh):
            gi = x @ Wih.T + bih
            gh = hstate @ Whh.T + bhh
            ir, iz, inn = jnp.split(gi, 3, axis=1)
            hr, hz, hn = jnp.split(gh, 3, axis=1)
            r = jax.nn.sigmoid(ir + hr)
            z = jax.nn.sigmoid(iz + hz)
            n = jnp.tanh(inn + r * hn)
            return (1.0 - z) * n + z * hstate

        def _gat_head(h, node_adj, edge_adj, W, a):
            hW = h @ W
            hp = (node_adj > 0).astype(hW.dtype) @ hW
            hm = (node_adj < 0).astype(hW.dtype) @ hW
            e_plus = jax.nn.leaky_relu(jnp.concatenate([hp, hm], axis=1) @ a, ALPHA)[:, 0]
            e_minus = jax.nn.leaky_relu(jnp.concatenate([hm, hp], axis=1) @ a, ALPHA)[:, 0]
            att = jnp.where(edge_adj > 0, e_plus[None, :], NEG_INF)
            att = jnp.where(edge_adj < 0, e_minus[None, :], att)
            att = jax.nn.softmax(att, axis=1)
            return att * edge_adj @ hW
        key = jax.random.key(seed)
        ks = jax.random.split(key, 16)
        std = 0.01
        gain = 1.414
        return {'h': jax.random.normal(ks[0], (N, H), jnp.float32), 'node_adj': _sign_adj(ks[1], N, 0.005), 'edge_adj': _sign_adj(ks[2], N, 0.005), 'gat_W': jax.random.normal(ks[3], (HEADS, H, H), jnp.float32) * (gain / np.sqrt(H, dtype=np.float32)), 'gat_a': jax.random.normal(ks[4], (HEADS, 2 * H, 1), jnp.float32) * 0.1, 'edge_Wih': jax.random.normal(ks[5], (3 * H, H), jnp.float32) * std, 'edge_Whh': jax.random.normal(ks[6], (3 * H, H), jnp.float32) * std, 'edge_bih': jnp.zeros((3 * H,), jnp.float32), 'edge_bhh': jnp.zeros((3 * H,), jnp.float32), 'node_Wih': jax.random.normal(ks[7], (3 * H, H), jnp.float32) * std, 'node_Whh': jax.random.normal(ks[8], (3 * H, H), jnp.float32) * std, 'node_bih': jnp.zeros((3 * H,), jnp.float32), 'node_bhh': jnp.zeros((3 * H,), jnp.float32)}
    _L0_gnn_all = _L0_gnn_setup()
    _L0_gnn_in = {k: v for k, v in _L0_gnn_all.items() if k in ('gat_W', 'gat_a', 'edge_Wih', 'edge_Whh', 'edge_bih', 'edge_bhh', 'node_Wih', 'node_Whh', 'node_bih', 'node_bhh')}
    del _L0_gnn_all
    return {'x': x, 'adj': adj, 'L0_gnn_gat_W': _L0_gnn_in['gat_W'], 'L0_gnn_gat_a': _L0_gnn_in['gat_a'], 'L0_gnn_edge_Wih': _L0_gnn_in['edge_Wih'], 'L0_gnn_edge_Whh': _L0_gnn_in['edge_Whh'], 'L0_gnn_edge_bih': _L0_gnn_in['edge_bih'], 'L0_gnn_edge_bhh': _L0_gnn_in['edge_bhh'], 'L0_gnn_node_Wih': _L0_gnn_in['node_Wih'], 'L0_gnn_node_Whh': _L0_gnn_in['node_Whh'], 'L0_gnn_node_bih': _L0_gnn_in['node_bih'], 'L0_gnn_node_bhh': _L0_gnn_in['node_bhh']}

def reference(x, adj, L0_gnn_gat_W, L0_gnn_gat_a, L0_gnn_edge_Wih, L0_gnn_edge_Whh, L0_gnn_edge_bih, L0_gnn_edge_bhh, L0_gnn_node_Wih, L0_gnn_node_Whh, L0_gnn_node_bih, L0_gnn_node_bhh):
    import jax
    import jax.numpy as jnp

    def _L0_gnn_ref(h, node_adj, edge_adj, gat_W, gat_a, edge_Wih, edge_Whh, edge_bih, edge_bhh, node_Wih, node_Whh, node_bih, node_bhh):
        import jax, jax.numpy as jnp
        import numpy as np
        N, H, HEADS = (2048, 128, 3)
        ALPHA = 0.2
        NEG_INF = -9000000000000000.0

        def _sign_adj(key, n, density):
            k1, k2 = jax.random.split(key)
            mask = jax.random.uniform(k1, (n, n)) < density
            sign = jnp.where(jax.random.uniform(k2, (n, n)) < 0.5, -1.0, 1.0)
            adj = jnp.where(mask, sign, 0.0).astype(jnp.float32)
            idx = jnp.arange(n)
            return adj.at[idx, idx].set(1.0)

        def _gru_cell(x, hstate, Wih, Whh, bih, bhh):
            gi = x @ Wih.T + bih
            gh = hstate @ Whh.T + bhh
            ir, iz, inn = jnp.split(gi, 3, axis=1)
            hr, hz, hn = jnp.split(gh, 3, axis=1)
            r = jax.nn.sigmoid(ir + hr)
            z = jax.nn.sigmoid(iz + hz)
            n = jnp.tanh(inn + r * hn)
            return (1.0 - z) * n + z * hstate

        def _gat_head(h, node_adj, edge_adj, W, a):
            hW = h @ W
            hp = (node_adj > 0).astype(hW.dtype) @ hW
            hm = (node_adj < 0).astype(hW.dtype) @ hW
            e_plus = jax.nn.leaky_relu(jnp.concatenate([hp, hm], axis=1) @ a, ALPHA)[:, 0]
            e_minus = jax.nn.leaky_relu(jnp.concatenate([hm, hp], axis=1) @ a, ALPHA)[:, 0]
            att = jnp.where(edge_adj > 0, e_plus[None, :], NEG_INF)
            att = jnp.where(edge_adj < 0, e_minus[None, :], att)
            att = jax.nn.softmax(att, axis=1)
            return att * edge_adj @ hW
        dn = jnp.diag(node_adj)
        de = jnp.diag(edge_adj)
        idx = jnp.arange(node_adj.shape[0])
        node_adj_norm = node_adj.at[idx, idx].add(-dn)
        edge_adj_norm = edge_adj.at[idx, idx].add(-de)
        node_support = node_adj_norm @ h
        edge_output = _gru_cell(node_support, h, edge_Wih, edge_Whh, edge_bih, edge_bhh)
        edge_support = _gat_head(h, node_adj_norm, edge_adj_norm, gat_W[0], gat_a[0])
        for i in range(1, HEADS):
            edge_support = edge_support + _gat_head(h, node_adj_norm, edge_adj_norm, gat_W[i], gat_a[i])
        edge_support = edge_support / HEADS
        node_output = _gru_cell(edge_support, h, node_Wih, node_Whh, node_bih, node_bhh)
        return de[:, None] * edge_output + dn[:, None] * node_output
    x = _layernorm(x + _L0_gnn_ref(x, adj, adj, L0_gnn_gat_W, L0_gnn_gat_a, L0_gnn_edge_Wih, L0_gnn_edge_Whh, L0_gnn_edge_bih, L0_gnn_edge_bhh, L0_gnn_node_Wih, L0_gnn_node_Whh, L0_gnn_node_bih, L0_gnn_node_bhh), axis=-1)
    return x

_drawn_inputs = setup_inputs


def setup_inputs(seed=0):
    import zlib

    import numpy as np

    out = dict(_drawn_inputs(seed))
    spreads = {'L0_gnn_edge_bih': (0.0, 0.406),
     'L0_gnn_edge_bhh': (0.0, 0.688),
     'L0_gnn_node_bih': (0.0, 0.434),
     'L0_gnn_node_bhh': (0.0, 0.667)}
    factors = {'L0_gnn_gat_W': 6.19,
     'L0_gnn_gat_a': 7.692,
     'L0_gnn_edge_Whh': 4.191,
     'L0_gnn_node_Wih': 6.114,
     'L0_gnn_node_Whh': 4.157}
    for name, (base, spread) in spreads.items():
        noise = np.random.default_rng([zlib.crc32(name.encode()), seed]).standard_normal(out[name].shape)
        drawn = base * np.exp(spread * noise) if base else spread * noise
        out[name] = jnp.asarray(drawn.astype(out[name].dtype))
    for name, factor in factors.items():
        out[name] = (out[name] * factor).astype(out[name].dtype)
    return out
```

```python
import numpy as np
import concourse.bass as bass
from concourse import mybir
from contextlib import ExitStack

ALU = mybir.AluOpType
ACT = mybir.ActivationFunctionType
AX = mybir.AxisListType
F32 = mybir.dt.float32
BF16 = mybir.dt.bfloat16
I32 = mybir.dt.int32

N, H, HEADS = 4096, 128, 3
P = 128
TILES = N // P
GROUP = 1024
GROUPS = N // GROUP
GTILES = GROUP // P
HALF = 512
HALVES = GROUP // HALF
STEP = 8
TURNS = TILES // STEP
PAIR = 2
PW = PAIR * P
HEAD_UNITS = STEP * HEADS
RING1, MASKS = 8, 4
RING2, WEIGHTS = 4, 3
LOGIT_SLOTS = 3
ROWHALF = N // 2
PART = 512
KEEP = 2 * GROUPS - 1
MASKED = -1.0e30
LOWEST = -3.0e38
DVE_CLAMPS = [1, 2]
SLOPE = 0.2
EPS = 1e-5
EROWS = 2 * HEADS
SPLITS = 3
UCOLS = 32


def wait_apart(eng, passed, semaphore, value):
    eng.wait_ge(semaphore, value)
    eng.sem_inc(passed, 1)


def gnn_kernel(nc, x, x_t, adj, adj_t, w, w_t, a_t, edge_wih, edge_whh, node_wih, node_whh,
               biases, row_pick, bc_pick, eye, keep, out):
    x_tiles = x.rearrange("(t p) h -> p t h", p=P)
    adj_rows = adj.rearrange("(t p) j -> t p j", p=P)
    out_tiles = out.rearrange("(t p) h -> p t h", p=P)
    diagonal = bass.AP(tensor=adj.tensor, offset=0, ap=[[N + 1, P], [P * (N + 1), TILES]])

    edge_dram = nc.dram_tensor("edge_out", (P, N), F32, kind="Internal").ap()
    eminus_dram = nc.dram_tensor("e_minus", (HEADS, N), F32, kind="Internal").ap()

    whole = ExitStack()
    with whole:
        def sb(name, shape, dt=F32, ctx=whole):
            return ctx.enter_context(nc.sbuf_tensor(name, shape, dt))

        def sem(name):
            return whole.enter_context(nc.semaphore(name))

        x_sb = sb("x_sb", [P, TILES, H])
        e_bc = sb("e_bc", [P, HEADS, N])
        e_col = sb("e_col", [P, TILES * EROWS])
        w_sb = sb("w_sb", [P, HEADS, H])
        wg = sb("wg", [P, 2, 3 * H])
        bias = sb("bias", [P, 4, 3])
        half_rz = sb("half_rz", [P, 2, 2])
        eye_sb = sb("eye_sb", [P, P])
        ones_sb = sb("ones_sb", [P, P])
        zeros_sb = sb("zeros_sb", [P, HALF], BF16)
        keep_sb = sb("keep_sb", [P, KEEP, P])
        d_sb = sb("d_sb", [P, TILES])
        negatives = sb("negatives", [P, GROUPS])
        negative_max = sb("negative_max", [P, 1])
        negative_int = sb("negative_int", [P, 1], I32)

        dve_waits, pe_waits, pool_waits = sem("dve_waits"), sem("pe_waits"), sem("pool_waits")

        setup_loaded = sem("setup_loaded")
        setup_made = sem("setup_made")
        v_ready, v_copied, u_ready, u_split = (sem(n) for n in ("v_ready", "v_copied", "u_ready", "u_split"))
        chunk_loaded = [sem(f"chunk_loaded{i}") for i in range(RING1)]
        chunk_staged = sem("chunk_staged")
        masks_ready = sem("masks_ready")
        chunk_done = sem("chunk_done")
        sums_closed = sem("sums_closed")
        st_copied, pm_copied = sem("st_copied"), sem("pm_copied")
        filled = [sem(f"filled{b}") for b in range(4)]
        emptied = [sem(f"emptied{b}") for b in range(4)]
        slope_ready = sem("slope_ready")
        eminus_stored = sem("eminus_stored")
        n_ready = sem("n_ready")
        edge_ready, edge_stored = sem("edge_ready"), sem("edge_stored")
        dve_step = sem("dve_step")
        flag_made = sem("flag_made")

        with ExitStack() as one:
            def sb1(name, shape, dt=F32):
                return sb(name, shape, dt, one)

            ps_s = [one.enter_context(nc.psum_tensor(f"ps_s{i}", [P, HALF], F32)) for i in range(HALVES)]
            ps_pm = [one.enter_context(nc.psum_tensor(f"ps_pm{i}", [P, HALF], F32)) for i in range(HALVES)]
            ps_g = [one.enter_context(nc.psum_tensor(f"ps_g{i}", [P, HALF], F32)) for i in range(4)]

            xt_sb = sb1("xt_sb", [P, N])
            chunks = sb1("chunks1", [P, RING1, GROUP])
            masks = sb1("masks", [P, MASKS, 2, GROUP], BF16)
            x_ring = sb1("x_ring1", [P, RING1, H])
            u_ring = sb1("u_ring", [P, RING1, UCOLS], BF16)
            u_all = sb1("u_all", [P, TILES, UCOLS], BF16)
            u_rest = sb1("u_rest", [P, TILES, EROWS])
            wt_sb = sb1("wt_sb", [P, HEADS, H])
            at_sb = sb1("at_sb", [P, EROWS])
            v_sb = sb1("v_sb", [P, EROWS])
            row_pick_sb = sb1("row_pick_sb", [2 * UCOLS, EROWS])
            bc_pick_sb = sb1("bc_pick_sb", [2 * UCOLS, HEADS, P])
            pm_sb = sb1("pm_sb", [2 * UCOLS, HALVES, HALF])
            st_sb = sb1("st_sb", [P, HALVES, HALF])
            sloped = sb1("sloped", [P, 2, HALF])
            e_rows = sb1("e_rows", [EROWS, HALVES, HALF])
            tr, tz, hnb, rn, cand, diff, edge = (
                sb1(n, [P, HALF]) for n in ("tr", "tz", "hnb", "rn", "cand", "diff", "edge"))

            SETUP = [(x_sb[:, :, :], x_tiles), (xt_sb[:, :], x_t),
                     (wt_sb[:, :, :], w_t.rearrange("k c h -> c k h")),
                     (w_sb[:, :, :], w.rearrange("k h c -> h k c")), (at_sb[:, :], a_t),
                     (wg[:, 0, :], edge_wih), (wg[:, 1, :], edge_whh),
                     (bias[:, :, :], biases.rearrange("p (b g) -> p b g", b=4)),
                     (row_pick_sb[:, :], row_pick), (bc_pick_sb[:, :, :], bc_pick), (eye_sb[:, :], eye),
                     (keep_sb[:, :, :], keep)]
            USES = [5, 4, 4, 4]

            with nc.Block() as block:

                @block.sync
                def _(sp):
                    for dst, src in SETUP:
                        sp.dma_start(dst, src).then_inc(setup_loaded, 16)
                    with sp.Fori(0, GROUPS) as g:
                        with sp.Fori(0, TURNS) as t:
                            for j in range(STEP):
                                c = TILES * g + STEP * t + j
                                sp.wait_ge(chunk_done, c + 1)
                                sp.dma_start(chunks[:, j, :], adj_t[bass.ds(c, 1), :, :].rearrange("o p i -> p (o i)"))\
                                  .then_inc(chunk_loaded[j], 16)

                @block.gpsimd
                def _(pool):
                    pool.wait_ge(setup_loaded, 16 * len(SETUP))
                    pool.wait_ge(u_split, 1)
                    with pool.Fori(0, GROUPS) as g:
                        with pool.Fori(0, TURNS) as t:
                            for j in range(STEP):
                                wait_apart(pool, pool_waits, chunk_loaded[j], (g * TURNS + t + 1) * 16)
                                block_j = chunks[:, j, j * P:(j + 1) * P]
                                nc.gpsimd.tensor_tensor(
                                    block_j, block_j,
                                    keep_sb[:, bass.ds((t + (GROUPS - 1)) - g, 1), :].rearrange("p o i -> p (o i)"),
                                    ALU.mult)
                                nc.gpsimd.tensor_copy(u_ring[:, j, :], u_all[:, bass.ds(t * STEP + j, 1), :].rearrange("p o i -> p (o i)"))
                                nc.gpsimd.tensor_copy(x_ring[:, j, :], x_sb[:, bass.ds(t * STEP + j, 1), :].rearrange("p o i -> p (o i)"))\
                                  .then_inc(chunk_staged, 1)

                @block.scalar
                def _(act):
                    act.wait_ge(setup_loaded, 16 * len(SETUP))
                    act.wait_ge(setup_made, 4)
                    with act.Fori(0, GROUPS) as g:
                        act.wait_ge(sums_closed, (g + 1) * 4)
                        for h in range(HALVES):
                            nc.scalar.activation(st_sb[:, h, :], ps_s[h][:, :], ACT.Copy).then_inc(st_copied, 1)
                        for i in range(8):
                            b, rows = i % 4, EROWS if i < 2 else P
                            act.wait_ge(filled[b], g * USES[b] + i // 4 + 1)
                            if i >= 2:
                                act.wait_ge(emptied[(i - 2) % 4], g * USES[(i - 2) % 4] + (i - 2) // 4 + 1)
                            nc.scalar.activation(sloped[0:rows, i % 2, :], ps_g[b][0:rows, :], ACT.Copy, scale=SLOPE)\
                              .then_inc(slope_ready, 1)
                            if i == 3:
                                act.dma_start(eminus_dram[:, bass.ds(g * GROUP, GROUP)],
                                              e_rows[HEADS:EROWS, :, :].rearrange("k h i -> k (h i)"))\
                                   .then_inc(eminus_stored, 16)
                        for h in range(HALVES):
                            act.wait_ge(filled[0], g * USES[0] + 3 + h)
                            act.wait_ge(edge_ready, g * HALVES + h)
                            nc.scalar.activation(tr[:, :], ps_g[0][:, :], ACT.Tanh, bias=half_rz[:, 0, 0:1], scale=0.5)\
                              .then_inc(emptied[0], 1)
                            act.wait_ge(filled[1], g * USES[1] + 3 + h)
                            nc.scalar.activation(tz[:, :], ps_g[1][:, :], ACT.Tanh, bias=half_rz[:, 0, 1:2], scale=0.5)\
                              .then_inc(emptied[1], 1)
                            act.wait_ge(emptied[3], g * USES[3] + 3 + h)
                            nc.scalar.activation(cand[:, :], rn[:, :], ACT.Tanh).then_inc(n_ready, 1)
                            act.wait_ge(edge_ready, g * HALVES + h + 1)
                            act.dma_start(edge_dram[:, bass.ds(g * GROUP + h * HALF, HALF)], edge[:, :])\
                               .then_inc(edge_stored, 16)
                    act.wait_ge(edge_stored, 16 * GROUPS * HALVES)
                    act.wait_ge(eminus_stored, 16 * GROUPS)

                @block.tensor
                def _(pe):
                    pe.sem_inc(chunk_done, RING1)
                    pe.wait_ge(setup_loaded, 16 * len(SETUP))
                    for k in range(HEADS):
                        last = nc.tensor.matmul(ps_g[0][:, 2 * k:2 * k + 2], wt_sb[:, k, :], at_sb[:, 2 * k:2 * k + 2],
                                                start=True, stop=True)
                    last.then_inc(v_ready, 1)
                    pe.wait_ge(v_copied, 1)
                    for t in range(TILES):
                        last = nc.tensor.matmul(ps_g[1][:, EROWS * t:EROWS * (t + 1)], xt_sb[:, t * P:(t + 1) * P],
                                                v_sb[:, :], start=True, stop=True)
                    last.then_inc(u_ready, 1)
                    pe.wait_ge(setup_made, 4)
                    with pe.Fori(0, GROUPS) as g:
                        pe.wait_ge(st_copied, g * HALVES)
                        pe.wait_ge(pm_copied, g * HALVES)
                        for h in range(HALVES):
                            nc.tensor.matmul(ps_s[h][:, :], zeros_sb[:, 0:P], zeros_sb[:, :], start=True, stop=False)
                            nc.tensor.matmul(ps_pm[h][0:2 * UCOLS, :], zeros_sb[:, 0:2 * UCOLS], zeros_sb[:, :],
                                             start=True, stop=False)
                        with pe.Fori(0, TURNS) as t:
                            for j in range(STEP):
                                c = TILES * g + STEP * t + j
                                pe.wait_ge(chunk_staged, c + 1)
                                for h in range(HALVES):
                                    nc.tensor.matmul(ps_s[h][:, :], x_ring[:, j, :], chunks[:, j, h * HALF:(h + 1) * HALF],
                                                     start=False, stop=False)
                                pe.wait_ge(masks_ready, c + 1)
                                for h in range(HALVES):
                                    for m in range(2):
                                        last = nc.tensor.matmul(
                                            ps_pm[h][m * UCOLS:(m + 1) * UCOLS, :], u_ring[:, j, :],
                                            masks[:, j % MASKS, m, h * HALF:(h + 1) * HALF],
                                            start=False, stop=False, skip_group_check=True)
                                last.then_inc(chunk_done, 1)
                        for h in range(HALVES):
                            nc.tensor.matmul(ps_s[h][:, :], zeros_sb[:, 0:P], zeros_sb[:, :], start=False, stop=True)\
                              .then_inc(sums_closed, 1)
                            nc.tensor.matmul(ps_pm[h][0:2 * UCOLS, :], zeros_sb[:, 0:2 * UCOLS], zeros_sb[:, :],
                                             start=False, stop=True).then_inc(sums_closed, 1)
                        pe.wait_ge(pm_copied, (g + 1) * HALVES)
                        for i in range(8):
                            b, h = i % 4, i % 2
                            wait_apart(pe, pe_waits, emptied[b], g * USES[b] + i // 4)
                            if i < 2:
                                nc.tensor.matmul(ps_g[b][0:EROWS, :], row_pick_sb[:, :], pm_sb[:, h, :],
                                                 start=True, stop=True).then_inc(filled[b], 1)
                            else:
                                nc.tensor.matmul(ps_g[b][:, :], bc_pick_sb[:, i // 2 - 1, :], pm_sb[:, h, :],
                                                 start=True, stop=True).then_inc(filled[b], 1)
                        pe.wait_ge(st_copied, (g + 1) * HALVES)
                        for h in range(HALVES):
                            state = xt_sb[:, bass.ds(g * GROUP + h * HALF, HALF)]
                            for b in range(4):
                                pe.wait_ge(emptied[b], g * USES[b] + 2 + h)
                                gate = wg[:, :, b * H:(b + 1) * H] if b < 2 else wg[:, :, 2 * H:3 * H]
                                if b < 2:
                                    nc.tensor.matmul(ps_g[b][:, :], gate[:, 0, :], st_sb[:, h, :], start=True, stop=False)
                                    nc.tensor.matmul(ps_g[b][:, :], gate[:, 1, :], state, start=False, stop=True)\
                                      .then_inc(filled[b], 1)
                                elif b == 2:
                                    nc.tensor.matmul(ps_g[b][:, :], gate[:, 1, :], state, start=True, stop=True)\
                                      .then_inc(filled[b], 1)
                                else:
                                    nc.tensor.matmul(ps_g[b][:, :], gate[:, 0, :], st_sb[:, h, :], start=True, stop=True)\
                                      .then_inc(filled[b], 1)
                        pe.wait_ge(emptied[0], g * USES[0] + 4)
                        for i in range(GTILES):
                            r = i % (HALF // P)
                            last = nc.tensor.matmul(ps_g[0][:, EROWS * i:EROWS * (i + 1)],
                                                    e_rows[:, i * P // HALF, r * P:(r + 1) * P], eye_sb[0:EROWS, 0:EROWS],
                                                    start=True, stop=True)
                        last.then_inc(filled[0], 1)

                @block.vector
                def _(dve):
                    steps = [0]

                    def link(ins):
                        steps[0] += 1
                        ins.then_inc(dve_step, 1)
                        dve.wait_ge(dve_step, steps[0])

                    nc.vector.memset(ones_sb[:, :], 1.0).then_inc(setup_made, 1)
                    nc.vector.memset(zeros_sb[:, :], 0.0).then_inc(setup_made, 1)
                    link(nc.vector.memset(u_all[:, :, :], 0.0))
                    nc.vector.memset(u_all[:, :, 0:1], 1.0)
                    dve.wait_ge(setup_loaded, 16 * len(SETUP))
                    for b in range(2):
                        link(nc.vector.tensor_tensor(half_rz[:, b, :], bias[:, 2 * b, 0:2], bias[:, 2 * b + 1, 0:2], ALU.add))
                        nc.vector.tensor_scalar(half_rz[:, b, :], half_rz[:, b, :], 0.5, None, ALU.mult)\
                          .then_inc(setup_made, 1)
                    dve.wait_ge(v_ready, 1)
                    nc.vector.tensor_copy(v_sb[:, :], ps_g[0][:, 0:EROWS]).then_inc(v_copied, 1)
                    dve.wait_ge(u_ready, 1)
                    link(nc.vector.tensor_copy(u_rest[:, :, :], ps_g[1][:, 0:TILES * EROWS].rearrange("p (t c) -> p t c", c=EROWS)))
                    for s in range(SPLITS):
                        part = u_all[:, :, 1 + s * EROWS:1 + (s + 1) * EROWS]
                        ins = nc.vector.tensor_copy(part, u_rest[:, :, :])
                        if s < SPLITS - 1:
                            link(ins)
                            link(nc.vector.tensor_tensor(u_rest[:, :, :], u_rest[:, :, :], part, ALU.subtract))
                        else:
                            ins.then_inc(u_split, 1)
                    before = steps[0]
                    PER_GROUP = 1 + HALVES * 3
                    with dve.Fori(0, GROUPS) as g:
                        with dve.Fori(0, TURNS) as t:
                            for j in range(STEP):
                                c = TILES * g + STEP * t + j
                                dve.wait_ge(chunk_staged, c + 1)
                                dve.wait_ge(chunk_done, c + 1 + RING1 - MASKS)
                                nc.vector.tensor_scalar(masks[:, j % MASKS, 0, :], chunks[:, j, :], 0.0, None, ALU.is_gt)
                                nc.vector.tensor_scalar(masks[:, j % MASKS, 1, :], chunks[:, j, :], 0.0, None, ALU.is_lt)\
                                  .then_inc(masks_ready, 1)
                        local = [0]

                        def link_g(ins):
                            local[0] += 1
                            ins.then_inc(dve_step, 1)
                            dve.wait_ge(dve_step, g * PER_GROUP + (before + local[0]))

                        dve.wait_ge(sums_closed, (g + 1) * 4)
                        for h in range(HALVES):
                            ins = nc.vector.tensor_copy(pm_sb[:, h, :], ps_pm[h][0:2 * UCOLS, :])
                            ins.then_inc(pm_copied, 1)
                        dve.wait_ge(pm_copied, (g + 1) * HALVES)
                        link_g(nc.vector.tensor_reduce(negatives[UCOLS:UCOLS + 1, bass.ds(g, 1)],
                                                       pm_sb[UCOLS:UCOLS + 1, :, :], axis=AX.XY, op=ALU.max))
                        dve.wait_ge(eminus_stored, g * 16)
                        for i in range(8):
                            b, h = i % 4, i % 2
                            dve.wait_ge(slope_ready, g * 8 + i + 1)
                            if i < 2:
                                dst, rows = e_rows[:, h, :], EROWS
                            else:
                                dst, rows = e_bc[:, i // 2 - 1, bass.ds(g * GROUP + h * HALF, HALF)], P
                            nc.vector.tensor_tensor(dst, ps_g[b][0:rows, :], sloped[0:rows, i % 2, :], ALU.max)\
                              .then_inc(emptied[b], 1)
                        for h in range(HALVES):
                            state = xt_sb[:, bass.ds(g * GROUP + h * HALF, HALF)]
                            dve.wait_ge(filled[2], g * USES[2] + 3 + h)
                            nc.vector.tensor_scalar(hnb[:, :], ps_g[2][:, :], bias[:, 1, 2:3], 0.5, ALU.add, ALU.mult)\
                              .then_inc(emptied[2], 1)
                            dve.wait_ge(emptied[2], g * USES[2] + 3 + h)
                            dve.wait_ge(emptied[0], g * USES[0] + 3 + h)
                            link_g(nc.vector.scalar_tensor_tensor(rn[:, :], tr[:, :], 1.0, hnb[:, :], ALU.add, ALU.mult))
                            dve.wait_ge(filled[3], g * USES[3] + 3 + h)
                            nc.vector.scalar_tensor_tensor(rn[:, :], ps_g[3][:, :], bias[:, 0, 2:3], rn[:, :], ALU.add, ALU.add)\
                              .then_inc(emptied[3], 1)
                            dve.wait_ge(n_ready, g * HALVES + h + 1)
                            link_g(nc.vector.tensor_tensor(diff[:, :], state, cand[:, :], ALU.subtract))
                            dve.wait_ge(emptied[1], g * USES[1] + 3 + h)
                            link_g(nc.vector.scalar_tensor_tensor(diff[:, :], tz[:, :], 1.0, diff[:, :], ALU.add, ALU.mult))
                            dve.wait_ge(edge_stored, (g * HALVES + h) * 16)
                            nc.vector.scalar_tensor_tensor(edge[:, :], diff[:, :], 0.5, cand[:, :], ALU.mult, ALU.add)\
                              .then_inc(edge_ready, 1)
                        dve.wait_ge(filled[0], (g + 1) * USES[0])
                        nc.vector.tensor_copy(e_col[:, bass.ds(g * GTILES * EROWS, GTILES * EROWS)],
                                              ps_g[0][:, 0:GTILES * EROWS]).then_inc(emptied[0], 1)
                        assert local[0] == PER_GROUP
                    ins = nc.vector.tensor_reduce(negative_max[UCOLS:UCOLS + 1, :], negatives[UCOLS:UCOLS + 1, :],
                                                  axis=AX.X, op=ALU.max)
                    ins.then_inc(flag_made, 1)
                    dve.wait_ge(flag_made, 1)
                    nc.vector.tensor_copy(negative_int[UCOLS:UCOLS + 1, :], negative_max[UCOLS:UCOLS + 1, :])\
                      .then_inc(flag_made, 1)
                    dve.wait_ge(flag_made, 2)

        inputs2 = sem("inputs2")
        constants2 = sem("constants2")
        minus_half_made = sem("minus_half_made")
        row_loaded = sem("row_loaded")
        row_clean = sem("row_clean")
        row_used = sem("row_used")
        eminus_loaded, eminus_used = sem("eminus_loaded"), sem("eminus_used")
        logits_used = sem("logits_used")
        max_ready = sem("max_ready")
        max_diag = sem("max_diag")
        max_spread = sem("max_spread")
        slot_loaded = [sem(f"slot_loaded{i}") for i in range(RING2)]
        slot_staged = sem("slot_staged")
        clamped = sem("clamped")
        exponent_ready = sem("exponent_ready")
        weight_ready = sem("weight_ready")
        weight_used = sem("weight_used")
        product_ready = sem("product_ready")
        unit_done = sem("unit_done")
        heads_closed = sem("heads_closed")
        heads_copied = sem("heads_copied")
        misc_filled = [sem(f"misc_filled{b}") for b in range(2)]
        misc_read = [sem(f"misc_read{b}") for b in range(2)]
        scale_diag = sem("scale_diag")
        tail_loaded = sem("tail_loaded")
        node_n_ready = sem("node_n_ready")
        node_ready = sem("node_ready")
        var_ready, rstd_ready = sem("var_ready"), sem("rstd_ready")
        normed, stored = sem("normed"), sem("stored")
        dve_step2 = sem("dve_step2")

        with ExitStack() as two:
            def sb2(name, shape, dt=F32):
                return sb(name, shape, dt, two)

            ps_u = [[two.enter_context(nc.psum_tensor(f"ps_u{k}{h}", [P, HALF], F32)) for h in range(HALVES)]
                    for k in range(HEADS)]
            ps_m = [two.enter_context(nc.psum_tensor(f"ps_m{b}", [P, HALF], F32)) for b in range(2)]

            row = sb2("row", [P, N])
            holes = sb2("holes", [P, N], BF16)
            logits = sb2("logits", [P, LOGIT_SLOTS, ROWHALF])
            slots = sb2("slots", [P, RING2, GROUP])
            x_ring = sb2("x_ring2", [P, RING2, H])
            weights = sb2("weights", [P, WEIGHTS, GROUP])
            products = sb2("products", [P, WEIGHTS, GROUP])
            neg_max_bc = sb2("neg_max_bc", [P, 2, HEADS, GROUP])
            heads = sb2("heads", [P, HEADS, GROUP])
            scratch = sb2("scratch", [P, PART])
            eminus = sb2("eminus", [P, PART])
            half_max = sb2("half_max", [P, 2 * HEADS])
            neg_max = sb2("neg_max", [P, TILES * HEADS])
            expsum = sb2("expsum", [P, TILES * HEADS * 2])
            pair_sum = sb2("pair_sum", [P, PAIR * HEADS])
            inv_sum = sb2("inv_sum", [P, PAIR, HEADS])
            max_diag_sb = sb2("max_diag_sb", [P, HEADS, P])
            scale_diag_sb = sb2("scale_diag_sb", [P, HEADS, PAIR, P])
            third_eye = sb2("third_eye", [P, P])
            neg_e_col = sb2("neg_e_col", [P, TILES * EROWS])
            minus_half = sb2("minus_half", [P, PAIR])
            state, edge_sb, mix, tr, tz, hnb, cand, diff = (
                sb2(n, [P, PW]) for n in ("state", "edge_sb", "mix", "tr2", "tz2", "hnb2", "cand2", "diff2"))
            y = sb2("y", [P, PAIR, H])
            moments = sb2("moments", [P, PAIR, 6])
            mean_var = sb2("mean_var", [P, PAIR, 2])
            var_eps = sb2("var_eps", [P, PAIR])
            rstd = sb2("rstd", [P, PAIR])
            normal = sb2("normal", [P, PAIR, H])

            TAIL_USES = ["scale01", "scale2", "mix", "gates_rz", "gates_n"]
            ROW_ONLY = ["max0", "max1"]
            TAIL_ONLY = TAIL_USES + ["turned"]
            BOTH = TAIL_USES + ["max0", "turned", "max1"]
            SECTIONS = [("rows", 0, ROW_ONLY)]
            for g in range(GROUPS):
                SECTIONS.append(("group", g, ROW_ONLY if g == 0 else BOTH if g < GROUPS - 1 else TAIL_ONLY))
            SECTIONS.append(("tail", GROUPS, TAIL_ONLY))

            def use(section, t, what):
                before = TURNS * sum(len(uses) for _, _, uses in SECTIONS[:section])
                uses = SECTIONS[section][2]
                at = uses.index(what)
                return at % 2, t * (len(uses) // 2) + (before // 2 + at // 2)

            def has_rows(section):
                return "max0" in SECTIONS[section][2]

            def has_tail(section):
                return "mix" in SECTIONS[section][2]

            MAX_SPREAD = [4, 7]

            def first_tile(section):
                return 0 if section == 0 else (SECTIONS[section][1] + 1) * GTILES

            def first_pair(section):
                return (SECTIONS[section][1] - 1) * (GTILES // PAIR)

            with nc.Block() as block:

                def on_negatives(eng, program):
                    count = eng.value_load(negative_int[UCOLS:UCOLS + 1, 0:1], min_val=0, max_val=N)
                    with eng.If(count > 0):
                        program(True)
                    with eng.Else():
                        program(False)

                def turns(eng, count=TURNS):
                    return eng.Fori(0, count)


                @block.sync
                def _(sp):
                    sp.dma_start(wg[:, 0, :], node_wih).then_inc(inputs2, 16)
                    sp.dma_start(wg[:, 1, :], node_whh).then_inc(inputs2, 16)
                    with nc.allow_non_contiguous_dma(reason="4096 diagonal elements"):
                        sp.dma_start(d_sb[:, :], diagonal).then_inc(inputs2, 16)

                    def load_row(tile):
                        sp.wait_ge(row_used, tile + 1)
                        src = adj_rows[bass.ds(tile, 1), :, :] if not isinstance(tile, int) else adj_rows[tile:tile + 1, :, :]
                        sp.dma_start(row[:, :], src.rearrange("o p j -> p (o j)")).then_inc(row_loaded, 16)

                    def load_chunk(c, slot):
                        if not isinstance(c, int) or c >= RING2:
                            sp.wait_ge(product_ready, (c + 1 - RING2) * HEADS + WEIGHTS)
                        src = adj_t[bass.ds(c, 1), :, :] if not isinstance(c, int) else adj_t[c:c + 1, :, :]
                        sp.dma_start(slots[:, slot, :], src.rearrange("o p i -> p (o i)")).then_inc(slot_loaded[slot], 16)

                    def load_eminus(tile):
                        for i in range(HEADS * N // PART):
                            k, part = divmod(i, N // PART)
                            sp.wait_ge(eminus_used, tile * (HEADS * N // PART) + (i + 1))
                            sp.dma_start(eminus[:, :], eminus_dram[k, part * PART:(part + 1) * PART].partition_broadcast(P))\
                              .then_inc(eminus_loaded, 16)

                    def turn(section, t, negative, more_rows=True, more_chunks=True):
                        name, g, _ = SECTIONS[section]
                        pair = t + first_pair(section)
                        if has_tail(section):
                            sp.wait_ge(node_ready, pair)
                            cols = bass.ds(pair * PW, PW)
                            sp.dma_start(state[:, :], x_t[:, cols]).then_inc(tail_loaded, 16)
                            sp.dma_start(edge_sb[:, :], edge_dram[:, cols]).then_inc(tail_loaded, 16)
                        for j in range(STEP):
                            if has_rows(section) and j % (STEP // PAIR) == 0:
                                r = j // (STEP // PAIR)
                                tile = t * PAIR + (first_tile(section) + r)
                                if negative:
                                    load_eminus(tile)
                                if more_rows or r < PAIR - 1:
                                    load_row(tile + 1)
                            if name == "group" and (more_chunks or j < STEP - RING2):
                                load_chunk(t * STEP + (g * TILES + j + RING2), j % RING2)
                        if has_tail(section):
                            sp.wait_ge(normed, pair + 1)
                            sp.dma_start(out_tiles[:, bass.ds(pair * PAIR, PAIR), :], normal[:, :, :]).then_inc(stored, 16)

                    def program(negative):
                        load_row(0)
                        for c in range(RING2):
                            load_chunk(c, c)
                        for section in range(len(SECTIONS)):
                            last_rows = section == GROUPS - 1
                            last_chunks = section == GROUPS
                            whole_turns = TURNS - (last_rows or last_chunks)
                            with turns(sp, whole_turns) as t:
                                turn(section, t, negative)
                            if last_rows or last_chunks:
                                turn(section, TURNS - 1, negative, not last_rows, not last_chunks)

                    on_negatives(sp, program)
                    sp.wait_ge(stored, 16 * TILES // PAIR)


                @block.gpsimd
                def _(pool):
                    nc.gpsimd.memset(minus_half[:, :], -0.5).then_inc(minus_half_made, 1)
                    pool.wait_ge(minus_half_made, 1)

                    def turn(section, t):
                        name, g, _ = SECTIONS[section]
                        for j in range(STEP):
                            if has_rows(section) and j % (STEP // PAIR) == 0:
                                tile = t * PAIR + (first_tile(section) + j // (STEP // PAIR))
                                wait_apart(pool, pool_waits, row_loaded, (tile + 1) * 16)
                                own = row[:, bass.ds(tile * P, P)]
                                nc.gpsimd.tensor_tensor(own, own, keep_sb[:, GROUPS - 1, :], ALU.mult).then_inc(row_clean, 1)
                            if name == "group":
                                s = j % RING2
                                c = t * STEP + (g * TILES + j)
                                wait_apart(pool, pool_waits, slot_loaded[s],
                                           (t * (STEP // RING2) + (g * TILES // RING2 + j // RING2 + 1)) * 16)
                                own = slots[:, s, j * P:(j + 1) * P]
                                nc.gpsimd.tensor_tensor(
                                    own, own, keep_sb[:, bass.ds(t + (GROUPS - 1 - g), 1), :].rearrange("p o i -> p (o i)"),
                                    ALU.mult)
                                pool.wait_ge(unit_done, (c + 1) * HEADS)
                                nc.gpsimd.tensor_copy(x_ring[:, s, :], x_sb[:, bass.ds(t * STEP + j, 1), :].rearrange("p o i -> p (o i)"))\
                                  .then_inc(slot_staged, 1)
                            if has_tail(section) and j == STEP - 1:
                                pair = t + first_pair(section)
                                pool.wait_ge(var_ready, pair + 1)
                                nc.gpsimd.tensor_tensor(rstd[:, :], var_eps[:, :], minus_half[:, :], ALU.pow).then_inc(rstd_ready, 1)

                    for section in range(len(SECTIONS)):
                        with turns(pool) as t:
                            turn(section, t)


                @block.scalar
                def _(act):
                    def row_exps(tile, r, k):
                        act.wait_ge(max_ready, tile * HEADS + (k + 1))
                        for h in range(2):
                            slot = (HEADS * 2 * r + 2 * k + h) % LOGIT_SLOTS
                            nc.scalar.activation(logits[:, slot, :], logits[:, slot, :], ACT.Exp,
                                                 bias=neg_max[:, bass.ds(tile * HEADS + k, 1)],
                                                 accum_out=expsum[:, bass.ds(tile * (2 * HEADS) + (2 * k + h), 1)])\
                              .then_inc(logits_used, 1)

                    def spread_copy(section, t, r):
                        b, n = use(section, t, f"max{r}")
                        act.wait_ge(misc_filled[b], n + 1)
                        parity = 0 if section == 0 else (SECTIONS[section][1] + 1) % 2
                        nc.scalar.activation(neg_max_bc[:, parity, :, bass.ds(t * PW + r * P, P)],
                                             ps_m[b][:, 0:HEADS * P].rearrange("p (k i) -> p k i", k=HEADS), ACT.Copy)\
                          .then_inc(misc_read[b], 1)

                    def turn(section, t, negative):
                        name, g, _ = SECTIONS[section]
                        for j in range(STEP):
                            r, q = divmod(j, STEP // PAIR)
                            tile = t * PAIR + (first_tile(section) + r)
                            if name == "group":
                                for k in range(HEADS):
                                    for s in range(2 if negative else 1):
                                        unit = t * HEAD_UNITS + (g * TILES * HEADS + j * HEADS + k)
                                        i = 2 * (j * HEADS + k) + s if negative else k
                                        weight = weights[:, i % WEIGHTS, :]
                                        if not negative and k in DVE_CLAMPS:
                                            n = len(DVE_CLAMPS)
                                            act.wait_ge(clamped, t * (STEP * n) + ((g * TILES + j) * n + DVE_CLAMPS.index(k) + 1))
                                            nc.scalar.activation(weight, weight, ACT.Exp).then_inc(weight_ready, 1)
                                            continue
                                        n = 2 if negative else 1
                                        if negative:
                                            act.wait_ge(weight_used, unit * 2 + (s + 1))
                                        else:
                                            act.wait_ge(product_ready, unit + 1)
                                        col = t * (STEP * EROWS) + (j * EROWS + s * HEADS + k)
                                        nc.scalar.activation(weight, neg_max_bc[:, g % 2, k, :], ACT.Relu, scale=-1.0,
                                                             bias=neg_e_col[:, bass.ds(col, 1)]).then_inc(exponent_ready, 1)
                                        per = 2 * HEADS if negative else HEADS - len(DVE_CLAMPS)
                                        act.wait_ge(exponent_ready, t * (STEP * per) + (
                                            (g * TILES + j) * per + (2 * k + s if negative else k) + 1))
                                        nc.scalar.activation(weight, weight, ACT.Exp, scale=-1.0).then_inc(weight_ready, 1)
                            if has_rows(section) and q >= 1:
                                row_exps(tile, r, q - 1)
                            if has_tail(section):
                                pair = t + first_pair(section)
                                if j == 2:
                                    b, n = use(section, t, "mix")
                                    act.wait_ge(misc_filled[b], n + 1)
                                    nc.scalar.activation(mix[:, :], ps_m[b][:, 0:PW], ACT.Copy).then_inc(misc_read[b], 1)
                                if j == 4:
                                    b, n = use(section, t, "gates_rz")
                                    act.wait_ge(misc_filled[b], n + 1)
                                    act.wait_ge(node_ready, pair)
                                    nc.scalar.activation(tr[:, :], ps_m[b][:, 0:PW], ACT.Tanh, bias=half_rz[:, 1, 0:1], scale=0.5)
                                    nc.scalar.activation(tz[:, :], ps_m[b][:, PW:2 * PW], ACT.Tanh, bias=half_rz[:, 1, 1:2], scale=0.5)\
                                      .then_inc(misc_read[b], 1)
                                if j == 5:
                                    b, n = use(section, t, "gates_n")
                                    act.wait_ge(misc_read[b], n + 1)
                                    nc.scalar.activation(cand[:, :], hnb[:, :], ACT.Tanh).then_inc(node_n_ready, 1)
                            if has_rows(section) and j in MAX_SPREAD:
                                spread_copy(section, t, MAX_SPREAD.index(j))

                    def program(negative):
                        for section in range(len(SECTIONS)):
                            name, g, _ = SECTIONS[section]
                            if name == "group":
                                for r in range(PAIR):
                                    b, n = use(section - 1, TURNS - 1, f"max{r}")
                                    act.wait_ge(misc_read[b], n + 1)
                            with turns(act) as t:
                                turn(section, t, negative)
                            if name == "group":
                                act.wait_ge(heads_closed, (g + 1) * HEADS * HALVES)
                                for k in range(HEADS):
                                    nc.scalar.activation(heads[:, k, 0:HALF], ps_u[k][0][:, :], ACT.Copy).then_inc(heads_copied, 1)

                    act.sem_inc(logits_used, LOGIT_SLOTS)
                    act.wait_ge(constants2, 1)
                    on_negatives(act, program)
                    act.wait_ge(constants2, 1)


                @block.tensor
                def _(pe):
                    pe.sem_inc(unit_done, RING2 * HEADS)
                    pe.wait_ge(inputs2, 48)
                    pe.wait_ge(constants2, 1)

                    def spread(section, t, what, ready, count, ncols, source):
                        b, n = use(section, t, what)
                        pe.wait_ge(misc_read[b], n)
                        pe.wait_ge(ready, count)
                        nc.tensor.matmul(ps_m[b][:, 0:ncols], ones_sb[:, :], source, start=True, stop=True)\
                          .then_inc(misc_filled[b], 1)

                    def spread_max(section, t, tile, r):
                        spread(section, t, f"max{r}", max_diag, tile + 1, HEADS * P,
                               max_diag_sb[:, :, :].rearrange("p k i -> p (k i)"))

                    def turn(section, t):
                        name, g, _ = SECTIONS[section]
                        pair = t + first_pair(section)
                        cols = bass.ds(t * PW, PW)
                        for j in range(STEP):
                            if has_rows(section) and j in MAX_SPREAD:
                                r = MAX_SPREAD.index(j)
                                spread_max(section, t, t * PAIR + (first_tile(section) + r), r)
                            if name == "group":
                                c = t * STEP + (g * TILES + j)
                                pe.wait_ge(slot_staged, c + 1)
                                for k in range(HEADS):
                                    pe.wait_ge(product_ready, c * HEADS + (k + 1 + WEIGHTS))
                                    for h in range(HALVES):
                                        last = nc.tensor.matmul(ps_u[k][h][:, :], x_ring[:, j % RING2, :],
                                                                products[:, k, h * HALF:(h + 1) * HALF],
                                                                start=False, stop=False)
                                    last.then_inc(unit_done, 1)
                            if not has_tail(section):
                                continue
                            if j == 0:
                                spread(section, t, "scale01", scale_diag, pair + 1, 2 * PW,
                                       scale_diag_sb[:, 0:2, :, :].rearrange("p k r i -> p (k r i)"))
                                spread(section, t, "scale2", scale_diag, pair + 1, PW,
                                       scale_diag_sb[:, 2, :, :].rearrange("p r i -> p (r i)"))
                            if j == 1:
                                b, n = use(section, t, "mix")
                                for before in ("scale01", "scale2"):
                                    bb, nn = use(section, t, before)
                                    pe.wait_ge(misc_read[bb], nn + 1)
                                pe.wait_ge(misc_read[b], n)
                                for k in range(HEADS):
                                    last = nc.tensor.matmul(ps_m[b][:, 0:PW], w_sb[:, k, :], heads[:, k, cols],
                                                            start=(k == 0), stop=(k == HEADS - 1))
                                last.then_inc(misc_filled[b], 1)
                            if j == 2:
                                b, n = use(section, t, "gates_rz")
                                bb, nn = use(section, t, "mix")
                                pe.wait_ge(misc_read[bb], nn + 1)
                                pe.wait_ge(misc_read[b], n)
                                pe.wait_ge(tail_loaded, (pair + 1) * 32)
                                for i in range(2):
                                    dst = ps_m[b][:, i * PW:(i + 1) * PW]
                                    nc.tensor.matmul(dst, wg[:, 0, i * H:(i + 1) * H], mix[:, :], start=True, stop=False)
                                    last = nc.tensor.matmul(dst, wg[:, 1, i * H:(i + 1) * H], state[:, :], start=False, stop=True)
                                last.then_inc(misc_filled[b], 1)
                                b, n = use(section, t, "gates_n")
                                pe.wait_ge(misc_read[b], n)
                                nc.tensor.matmul(ps_m[b][:, 0:PW], wg[:, 0, 2 * H:3 * H], mix[:, :], start=True, stop=True)
                                nc.tensor.matmul(ps_m[b][:, PW:2 * PW], wg[:, 1, 2 * H:3 * H], state[:, :], start=True, stop=True)\
                                  .then_inc(misc_filled[b], 1)
                            if j == 6:
                                b, n = use(section, t, "turned")
                                pe.wait_ge(misc_read[b], n)
                                pe.wait_ge(node_ready, pair + 1)
                                for i in range(PAIR):
                                    last = nc.tensor.transpose(ps_m[b][:, i * P:(i + 1) * P], diff[:, i * P:(i + 1) * P], eye_sb[:, :])
                                last.then_inc(misc_filled[b], 1)

                    for section in range(len(SECTIONS)):
                        name, g, _ = SECTIONS[section]
                        if name == "group":
                            pe.wait_ge(heads_copied, g * HEADS * HALVES)
                            for k in range(HEADS):
                                for h in range(HALVES):
                                    nc.tensor.matmul(ps_u[k][h][:, :], zeros_sb[:, 0:P], zeros_sb[:, :], start=True, stop=False)
                        with turns(pe) as t:
                            turn(section, t)
                        if name == "group":
                            for k in range(HEADS):
                                for h in range(HALVES):
                                    nc.tensor.matmul(ps_u[k][h][:, :], zeros_sb[:, 0:P], zeros_sb[:, :], start=False, stop=True)\
                                      .then_inc(heads_closed, 1)


                @block.vector
                def _(dve):
                    def chain(expr_base):
                        local = [0]

                        def link(ins, apart=False):
                            local[0] += 1
                            ins.then_inc(dve_step2, 1)
                            if apart:
                                wait_apart(dve, dve_waits, dve_step2, expr_base + local[0])
                            else:
                                dve.wait_ge(dve_step2, expr_base + local[0])
                        link.local = local
                        return link

                    def row_holes(section, t, tile, link):
                        dve.wait_ge(row_clean, tile + 1)
                        return nc.vector.tensor_scalar(holes[:, :], row[:, :], 0.0, MASKED, ALU.is_le, ALU.mult)

                    def row_max(tile, r, k, link):
                        for h in range(2):
                            i = HEADS * 2 * r + 2 * k + h
                            slot = i % LOGIT_SLOTS
                            wait_apart(dve, dve_waits, logits_used, tile * (2 * HEADS) + (2 * k + h + 1))
                            cols = slice(h * ROWHALF, (h + 1) * ROWHALF)
                            ins = nc.vector.tensor_tensor_reduce(
                                out=logits[:, slot, :], in0=holes[:, cols], in1=e_bc[:, k, cols], scale=1.0,
                                scalar=LOWEST, op0=ALU.add, op1=ALU.max, accum_out=half_max[:, 2 * k + h:2 * k + h + 1])
                            if h == 1:
                                link(ins)
                        nc.vector.tensor_scalar(neg_max[:, bass.ds(tile * HEADS + k, 1)], half_max[:, 2 * k:2 * k + 1],
                                                half_max[:, 2 * k + 1:2 * k + 2],
                                                -1.0, ALU.max, ALU.mult).then_inc(max_ready, 1)

                    def row_max_negative(tile, r, k, link):
                        for h in range(2):
                            i = HEADS * 2 * r + 2 * k + h
                            slot = i % LOGIT_SLOTS
                            dve.wait_ge(logits_used, tile * (2 * HEADS) + (2 * k + h + 1))
                            for q in range(ROWHALF // PART):
                                part = h * (ROWHALF // PART) + q
                                cols = slice(part * PART, (part + 1) * PART)
                                dst = logits[:, slot, q * PART:(q + 1) * PART]
                                link(nc.vector.tensor_scalar(scratch[:, :], row[:, cols], 0.0, MASKED, ALU.is_ge, ALU.mult))
                                dve.wait_ge(eminus_loaded, (tile * (HEADS * N // PART) + (k * (N // PART) + part + 1)) * 16)
                                nc.vector.tensor_tensor(scratch[:, :], scratch[:, :], eminus[:, :], ALU.add)\
                                  .then_inc(eminus_used, 1)
                                link(nc.vector.tensor_tensor(dst, holes[:, cols], e_bc[:, k, cols], ALU.add))
                                dve.wait_ge(eminus_used, tile * (HEADS * N // PART) + (k * (N // PART) + part + 2))
                                link(nc.vector.tensor_tensor(dst, dst, scratch[:, :], ALU.max))
                            link(nc.vector.tensor_reduce(half_max[:, 2 * k + h:2 * k + h + 1], logits[:, slot, :], axis=AX.X, op=ALU.max))
                        nc.vector.tensor_scalar(neg_max[:, bass.ds(tile * HEADS + k, 1)], half_max[:, 2 * k:2 * k + 1],
                                                half_max[:, 2 * k + 1:2 * k + 2],
                                                -1.0, ALU.max, ALU.mult).then_inc(max_ready, 1)

                    def row_diag(tile):
                        dve.wait_ge(max_ready, (tile + 1) * HEADS)
                        nc.vector.tensor_tensor(
                            max_diag_sb[:, :, :], eye_sb[:, :].unsqueeze(1).broadcast_to([P, HEADS, P]),
                            neg_max[:, bass.ds(tile * HEADS, HEADS)].unsqueeze(2).broadcast_to([P, HEADS, P]), ALU.mult)\
                          .then_inc(max_diag, 1)

                    def clamp(section, t, j, k):
                        g = SECTIONS[section][1]
                        unit = t * HEAD_UNITS + (g * TILES * HEADS + j * HEADS + k)
                        dve.wait_ge(product_ready, unit + 1)
                        nc.vector.tensor_scalar(weights[:, k, :], neg_max_bc[:, g % 2, k, :],
                                                e_col[:, bass.ds(t * (STEP * EROWS) + (j * EROWS + k), 1)], 0.0,
                                                ALU.add, ALU.min).then_inc(clamped, 1)

                    def column_units(section, t, j, negative, link):
                        g = SECTIONS[section][1]
                        for k in range(HEADS):
                            unit = t * HEAD_UNITS + (g * TILES * HEADS + j * HEADS + k)
                            slot = slots[:, j % RING2, :]
                            if k == 0:
                                dve.wait_ge(slot_staged, t * STEP + (g * TILES + j + 1))
                            dve.wait_ge(unit_done, unit + (1 + RING2 * HEADS - WEIGHTS))
                            if not negative:
                                dve.wait_ge(weight_ready, unit + 1)
                                nc.vector.tensor_tensor(products[:, k, :], weights[:, k, :], slot, ALU.mult)\
                                  .then_inc(product_ready, 1)
                                if k in DVE_CLAMPS and j < STEP - 1:
                                    clamp(section, t, j + 1, k)
                                continue
                            i = 2 * (j * HEADS + k)
                            dve.wait_ge(weight_ready, unit * 2 + 2)
                            for q in range(GROUP // PART):
                                part = slice(q * PART, (q + 1) * PART)
                                link(nc.vector.tensor_scalar(scratch[:, :], slot[:, part], 0.0, None, ALU.max))
                                link(nc.vector.tensor_tensor(products[:, k, part], weights[:, i % WEIGHTS, part],
                                                             scratch[:, :], ALU.mult))
                                link(nc.vector.tensor_scalar(scratch[:, :], slot[:, part], 0.0, None, ALU.min))
                                link(nc.vector.tensor_tensor(scratch[:, :], weights[:, (i + 1) % WEIGHTS, part],
                                                             scratch[:, :], ALU.mult))
                                ins = nc.vector.tensor_tensor(products[:, k, part], products[:, k, part], scratch[:, :], ALU.add)
                            ins.then_inc(product_ready, 1)
                            dve.sem_inc(weight_used, 2)

                    def tail_scale_diag(section, t, pair, link):
                        sums = expsum[:, bass.ds(pair * (PAIR * HEADS * 2), PAIR * HEADS * 2)].rearrange("p (c h) -> p c h", h=2)
                        link(nc.vector.tensor_reduce(pair_sum[:, :], sums, axis=AX.X, op=ALU.add))
                        link(nc.vector.reciprocal(inv_sum[:, :, :].rearrange("p r k -> p (r k)"), pair_sum[:, :]))
                        nc.vector.tensor_tensor(
                            scale_diag_sb[:, :, :, :].rearrange("p k r i -> p k r i"),
                            third_eye[:, :].unsqueeze(1).unsqueeze(1).broadcast_to([P, HEADS, PAIR, P]),
                            inv_sum[:, :, :].rearrange("p r k -> p k r").unsqueeze(3).broadcast_to([P, HEADS, PAIR, P]), ALU.mult)\
                          .then_inc(scale_diag, 1)

                    def tail_scale(section, t):
                        cols = bass.ds(t * PW, PW)
                        for what, k0, k1 in (("scale01", 0, 2), ("scale2", 2, 3)):
                            b, n = use(section, t, what)
                            dve.wait_ge(misc_filled[b], n + 1)
                            part = heads[:, k0:k1, cols]
                            nc.vector.tensor_tensor(part, part, ps_m[b][:, 0:(k1 - k0) * PW].rearrange("p (k i) -> p k i", i=PW),
                                                    ALU.mult).then_inc(misc_read[b], 1)

                    def tail_candidate(section, t, link):
                        b, n = use(section, t, "gates_n")
                        dve.wait_ge(misc_filled[b], n + 1)
                        link(nc.vector.tensor_scalar(hnb[:, :], ps_m[b][:, PW:2 * PW], bias[:, 3, 2:3], 0.5, ALU.add, ALU.mult))
                        bb, nn = use(section, t, "gates_rz")
                        dve.wait_ge(misc_read[bb], nn + 1)
                        link(nc.vector.scalar_tensor_tensor(hnb[:, :], tr[:, :], 1.0, hnb[:, :], ALU.add, ALU.mult))
                        nc.vector.scalar_tensor_tensor(hnb[:, :], ps_m[b][:, 0:PW], bias[:, 2, 2:3], hnb[:, :], ALU.add, ALU.add)\
                          .then_inc(misc_read[b], 1)

                    def tail_state(pair, link):
                        dve.wait_ge(tail_loaded, (pair + 1) * 32)
                        dve.wait_ge(node_n_ready, pair + 1)
                        link(nc.vector.tensor_tensor(diff[:, :], state[:, :], cand[:, :], ALU.subtract))
                        link(nc.vector.scalar_tensor_tensor(diff[:, :], tz[:, :], 1.0, diff[:, :], ALU.add, ALU.mult))
                        link(nc.vector.scalar_tensor_tensor(diff[:, :], diff[:, :], 0.5, cand[:, :], ALU.mult, ALU.add))
                        nc.vector.tensor_tensor(diff[:, :], diff[:, :], edge_sb[:, :], ALU.add).then_inc(node_ready, 1)

                    def tail_residual(section, t, pair, link):
                        b, n = use(section, t, "turned")
                        dve.wait_ge(misc_filled[b], n + 1)
                        for i in range(PAIR):
                            tile = pair * PAIR + i
                            ins = nc.vector.scalar_tensor_tensor(
                                y[:, i, :], ps_m[b][:, i * P:(i + 1) * P], d_sb[:, bass.ds(tile, 1)],
                                x_sb[:, bass.ds(tile, 1), :].rearrange("p o h -> p (o h)"), ALU.mult, ALU.add)
                        ins.then_inc(misc_read[b], 1)
                        dve.wait_ge(misc_read[b], n + 1)
                        for i in range(PAIR):
                            ins = nc.vector.bn_stats(moments[:, i, :], y[:, i, :])
                        link(ins, apart=True)
                        for i in range(PAIR):
                            ins = nc.vector.bn_aggr(mean_var[:, i, :], moments[:, i, :])
                        link(ins)
                        nc.vector.tensor_scalar(var_eps[:, :], mean_var[:, :, 1], EPS, None, ALU.add).then_inc(var_ready, 1)

                    def tail_norm(pair):
                        dve.wait_ge(rstd_ready, pair + 1)
                        dve.wait_ge(stored, pair * 16)
                        for i in range(PAIR):
                            ins = nc.vector.tensor_scalar(normal[:, i, :], y[:, i, :], mean_var[:, i, 0:1], rstd[:, i:i + 1],
                                                          ALU.subtract, ALU.mult)
                        ins.then_inc(normed, 1)

                    def turn(section, t, negative, link):
                        name, g, _ = SECTIONS[section]
                        pair = t + first_pair(section)
                        if name == "group":
                            for r in range(PAIR):
                                b, n = use(section - 1, TURNS - 1, f"max{r}")
                                dve.wait_ge(misc_read[b], n + 1)
                            if not negative:
                                for k in DVE_CLAMPS:
                                    clamp(section, t, 0, k)
                        for j in range(STEP):
                            r, q = divmod(j, STEP // PAIR)
                            tile = t * PAIR + (first_tile(section) + r)
                            if has_tail(section) and j == 0:
                                tail_scale_diag(section, t, pair, link)
                            if has_rows(section):
                                if q == 0:
                                    ins = row_holes(section, t, tile, link)
                                    link(ins)
                                    if not negative:
                                        dve.sem_inc(row_used, 1)
                                if q < HEADS:
                                    (row_max_negative if negative else row_max)(tile, r, q, link)
                                else:
                                    if negative:
                                        dve.sem_inc(row_used, 1)
                                    row_diag(tile)
                            if name == "group":
                                column_units(section, t, j, negative, link)
                            if has_tail(section):
                                if j == 1:
                                    tail_scale(section, t)
                                if j == 4:
                                    tail_candidate(section, t, link)
                                if j == 5:
                                    tail_state(pair, link)
                                if j == 7:
                                    tail_residual(section, t, pair, link)
                                    tail_norm(pair)

                    ROW_LINKS = {False: PAIR * (1 + HEADS), True: PAIR * (1 + HEADS * 2 * (1 + 3 * ROWHALF // PART))}
                    COLUMN_LINKS = {False: 0, True: HEAD_UNITS * 4 * (GROUP // PART)}
                    TAIL_LINKS = 2 + 2 + 3 + 2

                    def program(negative):
                        done = 1
                        for section in range(len(SECTIONS)):
                            name, g, _ = SECTIONS[section]
                            per_turn = (has_rows(section) * ROW_LINKS[negative] + (name == "group") * COLUMN_LINKS[negative]
                                        + has_tail(section) * TAIL_LINKS)
                            with turns(dve) as t:
                                link = chain(t * per_turn + done)
                                turn(section, t, negative, link)
                                assert link.local[0] == per_turn, (link.local, per_turn)
                            done += TURNS * per_turn
                            if name == "group":
                                dve.wait_ge(heads_closed, (g + 1) * HEADS * HALVES)
                                for k in range(HEADS):
                                    nc.vector.tensor_copy(heads[:, k, HALF:2 * HALF], ps_u[k][1][:, :]).then_inc(heads_copied, 1)
                                dve.wait_ge(heads_copied, (g + 1) * HEADS * HALVES)

                    nc.vector.tensor_scalar(neg_e_col[:, :], e_col[:, :], -1.0, None, ALU.mult)
                    nc.vector.tensor_scalar(third_eye[:, :], eye_sb[:, :], 1.0 / HEADS, None, ALU.mult).then_inc(constants2, 1)
                    dve.sem_inc(row_used, 1)
                    dve.sem_inc(eminus_used, 1)
                    dve.sem_inc(weight_used, WEIGHTS)
                    dve.sem_inc(product_ready, WEIGHTS)
                    dve.sem_inc(dve_step2, 1)
                    dve.wait_ge(inputs2, 48)
                    dve.wait_ge(constants2, 1)
                    on_negatives(dve, program)
                    dve.wait_ge(constants2, 1)


_OUTS = [((N, H), "float32")]


def kernel(**inputs):
    import numpy as _np
    import concourse.bacc as _bacc
    from concourse import mybir as _mybir
    from concourse.bass_utils import run_bass_kernel_spmd as _run

    c = _np.ascontiguousarray
    pre = "L0_gnn_"
    adj, x = _np.asarray(inputs["adj"]), _np.asarray(inputs["x"])
    gate_biases = [_np.asarray(inputs[pre + n]).reshape(3, H).T for n in ("edge_bih", "edge_bhh", "node_bih", "node_bhh")]
    row_pick = _np.zeros((2 * UCOLS, EROWS), _np.float32)
    for k in range(HEADS):
        for s in range(SPLITS):
            first = 1 + s * EROWS + 2 * k
            row_pick[[first, UCOLS + first + 1], k] = 1.0
            row_pick[[first + 1, UCOLS + first], HEADS + k] = 1.0
    keep = _np.ones((P, KEEP, P), _np.float32)
    keep[:, GROUPS - 1, :] -= _np.eye(P, dtype=_np.float32)
    w = _np.asarray(inputs[pre + "gat_W"])
    arrays = {
        "x": c(x), "x_t": c(x.T), "adj": c(adj),
        "adj_t": c(adj.T.reshape(N, GROUPS, GROUP).transpose(1, 0, 2)).reshape(GROUPS * TILES, P, GROUP),
        "w": c(w), "w_t": c(w.transpose(0, 2, 1)),
        "a_t": c(_np.asarray(inputs[pre + "gat_a"]).reshape(EROWS, H).T),
        "edge_wih": c(_np.asarray(inputs[pre + "edge_Wih"]).T), "edge_whh": c(_np.asarray(inputs[pre + "edge_Whh"]).T),
        "node_wih": c(_np.asarray(inputs[pre + "node_Wih"]).T), "node_whh": c(_np.asarray(inputs[pre + "node_Whh"]).T),
        "biases": c(_np.concatenate(gate_biases, axis=1)),
        "row_pick": row_pick, "bc_pick": c(_np.repeat(row_pick[:, :HEADS, None], P, axis=2)),
        "eye": _np.eye(P, dtype=_np.float32), "keep": keep,
    }
    nc = _bacc.Bacc("TRN2", target_bir_lowering=False, num_devices=1, dynamic_dma_scratch_size=1024)
    args = [nc.dram_tensor(f"in_{n}", a.shape, _mybir.dt.from_np(a.dtype), kind="ExternalInput").ap() for n, a in arrays.items()]
    for i, (shape, dtype) in enumerate(_OUTS):
        args.append(nc.dram_tensor(f"out_{i}", shape, _mybir.dt.from_np(_np.dtype(dtype)), kind="ExternalOutput").ap())
    gnn_kernel(nc, *args)
    r = _run(nc, [{f"in_{n}": a for n, a in arrays.items()}], core_ids=[0])
    return r.results[0]["out_0"]
```

```python
import numpy as np
import concourse.bass as bass
from concourse import mybir
from contextlib import ExitStack

ALU = mybir.AluOpType
ACT = mybir.ActivationFunctionType
AX = mybir.AxisListType
F32 = mybir.dt.float32
BF16 = mybir.dt.bfloat16
I32 = mybir.dt.int32

N, H, HEADS = 4096, 128, 3
P = 128
TILES = N // P
GROUP = 1024
GROUPS = N // GROUP
GTILES = GROUP // P
HALF = 512
HALVES = GROUP // HALF
STEP = 8
TURNS = TILES // STEP
PAIR = 2
PW = PAIR * P
HEAD_UNITS = STEP * HEADS
RING1, MASKS = 8, 4
RING2, WEIGHTS = 4, 3
LOGIT_SLOTS = 3
ROWHALF = N // 2
PART = 512
KEEP = 2 * GROUPS - 1
MASKED = -1.0e30
LOWEST = -3.0e38
DVE_CLAMPS = [2]
ROW_PLAN = [["holes", (0, 0)], [(0, 1), (1, 0)], [(1, 1), (2, 0)], [(2, 1), "diagonal"]]
SLOPE = 0.2
EPS = 1e-5
EROWS = 2 * HEADS
SPLITS = 3
UCOLS = 32


def wait_apart(eng, passed, semaphore, value):
    eng.wait_ge(semaphore, value)
    eng.sem_inc(passed, 1)


def gnn_kernel(nc, x, x_t, adj, adj_t, w, w_t, a_t, edge_wih, edge_whh, node_wih, node_whh,
               biases, row_pick, bc_pick, eye, keep, out):
    x_tiles = x.rearrange("(t p) h -> p t h", p=P)
    adj_rows = adj.rearrange("(t p) j -> t p j", p=P)
    out_tiles = out.rearrange("(t p) h -> p t h", p=P)
    diagonal = bass.AP(tensor=adj.tensor, offset=0, ap=[[N + 1, P], [P * (N + 1), TILES]])

    edge_dram = nc.dram_tensor("edge_out", (P, N), F32, kind="Internal").ap()
    eminus_dram = nc.dram_tensor("e_minus", (HEADS, N), F32, kind="Internal").ap()

    whole = ExitStack()
    with whole:
        def sb(name, shape, dt=F32, ctx=whole):
            return ctx.enter_context(nc.sbuf_tensor(name, shape, dt))

        def sem(name):
            return whole.enter_context(nc.semaphore(name))

        x_sb = sb("x_sb", [P, TILES, H])
        e_bc = sb("e_bc", [P, HEADS, N])
        e_col = sb("e_col", [P, TILES * EROWS])
        w_sb = sb("w_sb", [P, HEADS, H])
        wg = sb("wg", [P, 2, 3 * H])
        bias = sb("bias", [P, 4, 3])
        half_rz = sb("half_rz", [P, 2, 2])
        eye_sb = sb("eye_sb", [P, P])
        ones_sb = sb("ones_sb", [P, P])
        zeros_sb = sb("zeros_sb", [P, HALF], BF16)
        keep_sb = sb("keep_sb", [P, KEEP, P])
        d_sb = sb("d_sb", [P, TILES])
        negatives = sb("negatives", [P, GROUPS])
        negative_max = sb("negative_max", [P, 1])
        negative_int = sb("negative_int", [P, 1], I32)

        dve_waits, pe_waits, pool_waits = sem("dve_waits"), sem("pe_waits"), sem("pool_waits")

        for_u_loaded, d_loaded = sem("for_u_loaded"), sem("d_loaded")
        setup_loaded = sem("setup_loaded")
        setup_made = sem("setup_made")
        v_ready, v_copied, u_ready, u_split = (sem(n) for n in ("v_ready", "v_copied", "u_ready", "u_split"))
        chunk_loaded = [sem(f"chunk_loaded{i}") for i in range(RING1)]
        chunk_staged = sem("chunk_staged")
        masks_ready = sem("masks_ready")
        chunk_done = sem("chunk_done")
        sums_closed = sem("sums_closed")
        st_copied, pm_copied = sem("st_copied"), sem("pm_copied")
        filled = [sem(f"filled{b}") for b in range(4)]
        emptied = [sem(f"emptied{b}") for b in range(4)]
        slope_ready = sem("slope_ready")
        eminus_stored = sem("eminus_stored")
        n_ready = sem("n_ready")
        edge_ready, edge_stored = sem("edge_ready"), sem("edge_stored")
        dve_step = sem("dve_step")
        flag_made = sem("flag_made")

        with ExitStack() as one:
            def sb1(name, shape, dt=F32):
                return sb(name, shape, dt, one)

            ps_s = [one.enter_context(nc.psum_tensor(f"ps_s{i}", [P, HALF], F32)) for i in range(HALVES)]
            ps_pm = [one.enter_context(nc.psum_tensor(f"ps_pm{i}", [P, HALF], F32)) for i in range(HALVES)]
            ps_g = [one.enter_context(nc.psum_tensor(f"ps_g{i}", [P, HALF], F32)) for i in range(4)]

            xt_sb = sb1("xt_sb", [P, N])
            chunks = sb1("chunks1", [P, RING1, GROUP])
            masks = sb1("masks", [P, MASKS, 2, GROUP], BF16)
            x_ring = sb1("x_ring1", [P, RING1, H])
            u_ring = sb1("u_ring", [P, RING1, UCOLS], BF16)
            u_all = sb1("u_all", [P, TILES, UCOLS], BF16)
            u_rest = sb1("u_rest", [P, TILES, EROWS])
            wt_sb = sb1("wt_sb", [P, HEADS, H])
            at_sb = sb1("at_sb", [P, EROWS])
            v_sb = sb1("v_sb", [P, EROWS])
            row_pick_sb = sb1("row_pick_sb", [2 * UCOLS, EROWS])
            bc_pick_sb = sb1("bc_pick_sb", [2 * UCOLS, HEADS, P])
            pm_sb = sb1("pm_sb", [2 * UCOLS, HALVES, HALF])
            st_sb = sb1("st_sb", [P, HALVES, HALF])
            sloped = sb1("sloped", [P, 2, HALF])
            e_rows = sb1("e_rows", [EROWS, HALVES, HALF])
            tr, tz, hnb, rn, cand, diff, edge = (
                sb1(n, [P, HALF]) for n in ("tr", "tz", "hnb", "rn", "cand", "diff", "edge"))

            FOR_U = [(wt_sb[:, :, :], w_t.rearrange("k c h -> c k h")), (at_sb[:, :], a_t), (xt_sb[:, :], x_t)]
            SETUP = [(x_sb[:, :, :], x_tiles), (w_sb[:, :, :], w.rearrange("k h c -> h k c")),
                     (wg[:, 0, :], edge_wih), (wg[:, 1, :], edge_whh),
                     (bias[:, :, :], biases.rearrange("p (b g) -> p b g", b=4)),
                     (row_pick_sb[:, :], row_pick), (bc_pick_sb[:, :, :], bc_pick), (eye_sb[:, :], eye),
                     (keep_sb[:, :, :], keep)]
            USES = [5, 4, 4, 4]
            FINISH_TURNS = 2

            with nc.Block() as block:

                @block.sync
                def _(sp):
                    for dst, src in FOR_U:
                        sp.dma_start(dst, src).then_inc(for_u_loaded, 16)
                    for dst, src in SETUP:
                        sp.dma_start(dst, src).then_inc(setup_loaded, 16)
                    with sp.Fori(0, GROUPS) as g:
                        with sp.Fori(0, TURNS) as t:
                            for j in range(STEP):
                                c = TILES * g + STEP * t + j
                                sp.wait_ge(chunk_done, c + 1)
                                sp.dma_start(chunks[:, j, :], adj_t[bass.ds(c, 1), :, :].rearrange("o p i -> p (o i)"))\
                                  .then_inc(chunk_loaded[j], 16)
                    with nc.allow_non_contiguous_dma(reason="4096 diagonal elements"):
                        sp.dma_start(d_sb[:, :], diagonal).then_inc(d_loaded, 16)

                @block.gpsimd
                def _(pool):
                    pool.wait_ge(setup_loaded, 16 * len(SETUP))
                    pool.wait_ge(u_split, 1)
                    with pool.Fori(0, GROUPS) as g:
                        with pool.Fori(0, TURNS) as t:
                            for j in range(STEP):
                                wait_apart(pool, pool_waits, chunk_loaded[j], (g * TURNS + t + 1) * 16)
                                block_j = chunks[:, j, j * P:(j + 1) * P]
                                nc.gpsimd.tensor_tensor(
                                    block_j, block_j,
                                    keep_sb[:, bass.ds((t + (GROUPS - 1)) - g, 1), :].rearrange("p o i -> p (o i)"),
                                    ALU.mult)
                                nc.gpsimd.tensor_copy(u_ring[:, j, :], u_all[:, bass.ds(t * STEP + j, 1), :].rearrange("p o i -> p (o i)"))
                                nc.gpsimd.tensor_copy(x_ring[:, j, :], x_sb[:, bass.ds(t * STEP + j, 1), :].rearrange("p o i -> p (o i)"))\
                                  .then_inc(chunk_staged, 1)

                @block.scalar
                def _(act):
                    for start in (st_copied, eminus_stored, edge_stored):
                        act.sem_inc(start, 1)
                    act.wait_ge(setup_loaded, 16 * len(SETUP))
                    act.wait_ge(setup_made, 4)
                    with act.Fori(0, GROUPS) as g:
                        act.wait_ge(sums_closed, (g + 1) * 4)
                        for h in range(HALVES):
                            nc.scalar.activation(st_sb[:, h, :], ps_s[h][:, :], ACT.Copy).then_inc(st_copied, 1)
                        for i in range(8):
                            b, rows = i % 4, EROWS if i < 2 else P
                            act.wait_ge(filled[b], g * USES[b] + i // 4 + 1)
                            if i >= 2:
                                act.wait_ge(emptied[(i - 2) % 4], g * USES[(i - 2) % 4] + (i - 2) // 4 + 2)
                            nc.scalar.activation(sloped[0:rows, i % 2, :], ps_g[b][0:rows, :], ACT.Copy, scale=SLOPE)\
                              .then_inc(slope_ready, 1)
                            if i == 3:
                                act.dma_start(eminus_dram[:, bass.ds(g * GROUP, GROUP)],
                                              e_rows[HEADS:EROWS, :, :].rearrange("k h i -> k (h i)"))\
                                   .then_inc(eminus_stored, 16)
                        for h in range(HALVES):
                            act.wait_ge(filled[0], g * USES[0] + 3 + h)
                            act.wait_ge(edge_ready, g * HALVES + h + 1)
                            nc.scalar.activation(tr[:, :], ps_g[0][:, :], ACT.Tanh, bias=half_rz[:, 0, 0:1], scale=0.5)\
                              .then_inc(emptied[0], 1)
                            act.wait_ge(filled[1], g * USES[1] + 3 + h)
                            nc.scalar.activation(tz[:, :], ps_g[1][:, :], ACT.Tanh, bias=half_rz[:, 0, 1:2], scale=0.5)\
                              .then_inc(emptied[1], 1)
                            act.wait_ge(emptied[3], g * USES[3] + 3 + h + 1)
                            nc.scalar.activation(cand[:, :], rn[:, :], ACT.Tanh).then_inc(n_ready, 1)
                            act.wait_ge(edge_ready, g * HALVES + h + 2)
                            act.dma_start(edge_dram[:, bass.ds(g * GROUP + h * HALF, HALF)], edge[:, :])\
                               .then_inc(edge_stored, 16)
                    act.wait_ge(edge_stored, 16 * GROUPS * HALVES + 1)
                    act.wait_ge(eminus_stored, 16 * GROUPS + 1)

                @block.tensor
                def _(pe):
                    pe.sem_inc(chunk_done, RING1)
                    pe.wait_ge(for_u_loaded, 16 * len(FOR_U))
                    for k in range(HEADS):
                        last = nc.tensor.matmul(ps_g[0][:, 2 * k:2 * k + 2], wt_sb[:, k, :], at_sb[:, 2 * k:2 * k + 2],
                                                start=True, stop=True)
                    last.then_inc(v_ready, 1)
                    pe.wait_ge(v_copied, 1)
                    for t in range(TILES):
                        last = nc.tensor.matmul(ps_g[1][:, EROWS * t:EROWS * (t + 1)], xt_sb[:, t * P:(t + 1) * P],
                                                v_sb[:, :], start=True, stop=True)
                    last.then_inc(u_ready, 1)
                    pe.wait_ge(setup_loaded, 16 * len(SETUP))
                    pe.wait_ge(setup_made, 4)

                    def open_sums(g):
                        pe.wait_ge(st_copied, g * HALVES + 1)
                        pe.wait_ge(pm_copied, g * HALVES + 1)
                        for h in range(HALVES):
                            nc.tensor.matmul(ps_s[h][:, :], zeros_sb[:, 0:P], zeros_sb[:, :], start=True, stop=False)
                            nc.tensor.matmul(ps_pm[h][0:2 * UCOLS, :], zeros_sb[:, 0:2 * UCOLS], zeros_sb[:, :],
                                             start=True, stop=False)

                    def chunk(g, t, j):
                        c = TILES * g + STEP * t + j
                        pe.wait_ge(chunk_staged, c + 1)
                        for h in range(HALVES):
                            nc.tensor.matmul(ps_s[h][:, :], x_ring[:, j, :], chunks[:, j, h * HALF:(h + 1) * HALF],
                                             start=False, stop=False)
                        pe.wait_ge(masks_ready, c + 1)
                        for h in range(HALVES):
                            for m in range(2):
                                last = nc.tensor.matmul(
                                    ps_pm[h][m * UCOLS:(m + 1) * UCOLS, :], u_ring[:, j, :],
                                    masks[:, j % MASKS, m, h * HALF:(h + 1) * HALF],
                                    start=False, stop=False, skip_group_check=True)
                        last.then_inc(chunk_done, 1)

                    def close_sums():
                        for h in range(HALVES):
                            nc.tensor.matmul(ps_s[h][:, :], zeros_sb[:, 0:P], zeros_sb[:, :], start=False, stop=True)\
                              .then_inc(sums_closed, 1)
                            nc.tensor.matmul(ps_pm[h][0:2 * UCOLS, :], zeros_sb[:, 0:2 * UCOLS], zeros_sb[:, :],
                                             start=False, stop=True).then_inc(sums_closed, 1)

                    def scores(g, first, last):
                        for i in range(first, last):
                            b, h = i % 4, i % 2
                            wait_apart(pe, pe_waits, emptied[b], g * USES[b] + i // 4 + 1)
                            if i < 2:
                                nc.tensor.matmul(ps_g[b][0:EROWS, :], row_pick_sb[:, :], pm_sb[:, h, :],
                                                 start=True, stop=True).then_inc(filled[b], 1)
                            else:
                                nc.tensor.matmul(ps_g[b][:, :], bc_pick_sb[:, i // 2 - 1, :], pm_sb[:, h, :],
                                                 start=True, stop=True).then_inc(filled[b], 1)

                    def gates(g, h):
                        state = xt_sb[:, bass.ds(g * GROUP + h * HALF, HALF)]
                        for b in range(4):
                            pe.wait_ge(emptied[b], g * USES[b] + 2 + h + 1)
                            gate = wg[:, :, b * H:(b + 1) * H] if b < 2 else wg[:, :, 2 * H:3 * H]
                            if b < 2:
                                nc.tensor.matmul(ps_g[b][:, :], gate[:, 0, :], st_sb[:, h, :], start=True, stop=False)
                                nc.tensor.matmul(ps_g[b][:, :], gate[:, 1, :], state, start=False, stop=True)\
                                  .then_inc(filled[b], 1)
                            elif b == 2:
                                nc.tensor.matmul(ps_g[b][:, :], gate[:, 1, :], state, start=True, stop=True)\
                                  .then_inc(filled[b], 1)
                            else:
                                nc.tensor.matmul(ps_g[b][:, :], gate[:, 0, :], st_sb[:, h, :], start=True, stop=True)\
                                  .then_inc(filled[b], 1)

                    def score_columns(g):
                        pe.wait_ge(emptied[0], g * USES[0] + 4 + 1)
                        for i in range(GTILES):
                            r = i % (HALF // P)
                            last = nc.tensor.matmul(ps_g[0][:, EROWS * i:EROWS * (i + 1)],
                                                    e_rows[:, i * P // HALF, r * P:(r + 1) * P], eye_sb[0:EROWS, 0:EROWS],
                                                    start=True, stop=True)
                        last.then_inc(filled[0], 1)

                    def finish(g, at):
                        if at == 0:
                            pe.wait_ge(pm_copied, (g + 1) * HALVES + 1)
                            scores(g, 0, 4)
                        if at == 3:
                            scores(g, 4, 8)
                        if at == 6:
                            pe.wait_ge(st_copied, (g + 1) * HALVES + 1)
                            gates(g, 0)
                        if at == 9:
                            gates(g, 1)
                        if at == 12:
                            score_columns(g)

                    open_sums(0)
                    with pe.Fori(0, TURNS) as t:
                        for j in range(STEP):
                            chunk(0, t, j)
                    close_sums()
                    with pe.Fori(1, GROUPS) as g:
                        open_sums(g)
                        for at in range(FINISH_TURNS * STEP):
                            chunk(g, at // STEP, at % STEP)
                            finish(g - 1, at)
                        with pe.Fori(FINISH_TURNS, TURNS) as t:
                            for j in range(STEP):
                                chunk(g, t, j)
                        close_sums()
                    for at in range(FINISH_TURNS * STEP):
                        finish(GROUPS - 1, at)

                @block.vector
                def _(dve):
                    steps = [0]

                    def link(ins):
                        steps[0] += 1
                        ins.then_inc(dve_step, 1)
                        dve.wait_ge(dve_step, steps[0])

                    for start in (pm_copied, edge_ready, *emptied):
                        dve.sem_inc(start, 1)
                    nc.vector.memset(ones_sb[:, :], 1.0).then_inc(setup_made, 1)
                    nc.vector.memset(zeros_sb[:, :], 0.0).then_inc(setup_made, 1)
                    link(nc.vector.memset(u_all[:, :, :], 0.0))
                    nc.vector.memset(u_all[:, :, 0:1], 1.0)
                    dve.wait_ge(v_ready, 1)
                    nc.vector.tensor_copy(v_sb[:, :], ps_g[0][:, 0:EROWS]).then_inc(v_copied, 1)
                    dve.wait_ge(setup_loaded, 16 * len(SETUP))
                    for b in range(2):
                        link(nc.vector.tensor_tensor(half_rz[:, b, :], bias[:, 2 * b, 0:2], bias[:, 2 * b + 1, 0:2], ALU.add))
                        nc.vector.tensor_scalar(half_rz[:, b, :], half_rz[:, b, :], 0.5, None, ALU.mult)\
                          .then_inc(setup_made, 1)
                    dve.wait_ge(u_ready, 1)
                    link(nc.vector.tensor_copy(u_rest[:, :, :], ps_g[1][:, 0:TILES * EROWS].rearrange("p (t c) -> p t c", c=EROWS)))
                    for s in range(SPLITS):
                        part = u_all[:, :, 1 + s * EROWS:1 + (s + 1) * EROWS]
                        ins = nc.vector.tensor_copy(part, u_rest[:, :, :])
                        if s < SPLITS - 1:
                            link(ins)
                            link(nc.vector.tensor_tensor(u_rest[:, :, :], u_rest[:, :, :], part, ALU.subtract))
                        else:
                            ins.then_inc(u_split, 1)
                    before = steps[0]
                    PER_GROUP = 1 + HALVES * 3

                    def chain(g, done):
                        local = [done]

                        def link_g(ins):
                            local[0] += 1
                            ins.then_inc(dve_step, 1)
                            dve.wait_ge(dve_step, g * PER_GROUP + (before + local[0]))
                        return link_g

                    def chunk(g, t, j):
                        c = TILES * g + STEP * t + j
                        dve.wait_ge(chunk_staged, c + 1)
                        dve.wait_ge(chunk_done, c + 1 + RING1 - MASKS)
                        nc.vector.tensor_scalar(masks[:, j % MASKS, 0, :], chunks[:, j, :], 0.0, None, ALU.is_gt)
                        nc.vector.tensor_scalar(masks[:, j % MASKS, 1, :], chunks[:, j, :], 0.0, None, ALU.is_lt)\
                          .then_inc(masks_ready, 1)

                    def copy_sums(g):
                        dve.wait_ge(sums_closed, (g + 1) * 4)
                        for h in range(HALVES):
                            nc.vector.tensor_copy(pm_sb[:, h, :], ps_pm[h][0:2 * UCOLS, :]).then_inc(pm_copied, 1)

                    def count_negatives(g):
                        dve.wait_ge(pm_copied, (g + 1) * HALVES + 1)
                        chain(g, 0)(nc.vector.tensor_reduce(negatives[UCOLS:UCOLS + 1, bass.ds(g, 1)],
                                                            pm_sb[UCOLS:UCOLS + 1, :, :], axis=AX.XY, op=ALU.max))

                    def scores(g, first, last):
                        for i in range(first, last):
                            b, h = i % 4, i % 2
                            dve.wait_ge(slope_ready, g * 8 + i + 1)
                            if i < 2:
                                dst, rows = e_rows[:, h, :], EROWS
                            else:
                                dst, rows = e_bc[:, i // 2 - 1, bass.ds(g * GROUP + h * HALF, HALF)], P
                            nc.vector.tensor_tensor(dst, ps_g[b][0:rows, :], sloped[0:rows, i % 2, :], ALU.max)\
                              .then_inc(emptied[b], 1)

                    def candidate(g, h):
                        dve.wait_ge(filled[2], g * USES[2] + 3 + h)
                        nc.vector.tensor_scalar(hnb[:, :], ps_g[2][:, :], bias[:, 1, 2:3], 0.5, ALU.add, ALU.mult)\
                          .then_inc(emptied[2], 1)
                        dve.wait_ge(emptied[2], g * USES[2] + 3 + h + 1)
                        dve.wait_ge(emptied[0], g * USES[0] + 3 + h + 1)
                        chain(g, 1 + 3 * h)(nc.vector.scalar_tensor_tensor(rn[:, :], tr[:, :], 1.0, hnb[:, :], ALU.add, ALU.mult))
                        dve.wait_ge(filled[3], g * USES[3] + 3 + h)
                        nc.vector.scalar_tensor_tensor(rn[:, :], ps_g[3][:, :], bias[:, 0, 2:3], rn[:, :], ALU.add, ALU.add)\
                          .then_inc(emptied[3], 1)

                    def edge_output(g, h):
                        link_g = chain(g, 2 + 3 * h)
                        state = xt_sb[:, bass.ds(g * GROUP + h * HALF, HALF)]
                        dve.wait_ge(n_ready, g * HALVES + h + 1)
                        link_g(nc.vector.tensor_tensor(diff[:, :], state, cand[:, :], ALU.subtract))
                        dve.wait_ge(emptied[1], g * USES[1] + 3 + h + 1)
                        link_g(nc.vector.scalar_tensor_tensor(diff[:, :], tz[:, :], 1.0, diff[:, :], ALU.add, ALU.mult))
                        dve.wait_ge(edge_stored, (g * HALVES + h) * 16 + 1)
                        nc.vector.scalar_tensor_tensor(edge[:, :], diff[:, :], 0.5, cand[:, :], ALU.mult, ALU.add)\
                          .then_inc(edge_ready, 1)

                    def finish(g, at):
                        if at == 0:
                            count_negatives(g)
                        if at == 2:
                            dve.wait_ge(eminus_stored, g * 16 + 1)
                            scores(g, 0, 4)
                        if at == 5:
                            scores(g, 4, 8)
                        if at == 8:
                            candidate(g, 0)
                        if at == 10:
                            edge_output(g, 0)
                        if at == 11:
                            candidate(g, 1)
                        if at == 13:
                            edge_output(g, 1)
                        if at == 14:
                            dve.wait_ge(filled[0], (g + 1) * USES[0])
                            nc.vector.tensor_copy(e_col[:, bass.ds(g * (GTILES * EROWS), GTILES * EROWS)],
                                                  ps_g[0][:, 0:GTILES * EROWS]).then_inc(emptied[0], 1)

                    with dve.Fori(0, TURNS) as t:
                        for j in range(STEP):
                            chunk(0, t, j)
                    copy_sums(0)
                    with dve.Fori(1, GROUPS) as g:
                        for at in range(FINISH_TURNS * STEP):
                            chunk(g, at // STEP, at % STEP)
                            finish(g - 1, at)
                        with dve.Fori(FINISH_TURNS, TURNS) as t:
                            for j in range(STEP):
                                chunk(g, t, j)
                        copy_sums(g)
                    for at in range(FINISH_TURNS * STEP):
                        finish(GROUPS - 1, at)
                    ins = nc.vector.tensor_reduce(negative_max[UCOLS:UCOLS + 1, :], negatives[UCOLS:UCOLS + 1, :],
                                                  axis=AX.X, op=ALU.max)
                    ins.then_inc(flag_made, 1)
                    dve.wait_ge(flag_made, 1)
                    nc.vector.tensor_copy(negative_int[UCOLS:UCOLS + 1, :], negative_max[UCOLS:UCOLS + 1, :])\
                      .then_inc(flag_made, 1)
                    dve.wait_ge(flag_made, 2)

        inputs2 = sem("inputs2")
        constants2 = sem("constants2")
        minus_half_made = sem("minus_half_made")
        row_loaded = sem("row_loaded")
        row_clean = sem("row_clean")
        row_used = sem("row_used")
        eminus_loaded, eminus_used = sem("eminus_loaded"), sem("eminus_used")
        logits_used = sem("logits_used")
        max_ready = sem("max_ready")
        max_diag = sem("max_diag")
        max_spread = sem("max_spread")
        slot_loaded = [sem(f"slot_loaded{i}") for i in range(RING2)]
        slot_staged = sem("slot_staged")
        clamped = sem("clamped")
        exponent_ready = sem("exponent_ready")
        weight_ready = sem("weight_ready")
        weight_used = sem("weight_used")
        product_ready = sem("product_ready")
        unit_done = sem("unit_done")
        heads_closed = sem("heads_closed")
        heads_copied = sem("heads_copied")
        misc_filled = [sem(f"misc_filled{b}") for b in range(2)]
        misc_read = [sem(f"misc_read{b}") for b in range(2)]
        scale_diag = sem("scale_diag")
        tail_loaded = sem("tail_loaded")
        node_n_ready = sem("node_n_ready")
        node_ready = sem("node_ready")
        var_ready, rstd_ready = sem("var_ready"), sem("rstd_ready")
        normed, stored = sem("normed"), sem("stored")
        dve_step2 = sem("dve_step2")

        with ExitStack() as two:
            def sb2(name, shape, dt=F32):
                return sb(name, shape, dt, two)

            ps_u = [[two.enter_context(nc.psum_tensor(f"ps_u{k}{h}", [P, HALF], F32)) for h in range(HALVES)]
                    for k in range(HEADS)]
            ps_m = [two.enter_context(nc.psum_tensor(f"ps_m{b}", [P, HALF], F32)) for b in range(2)]

            row = sb2("row", [P, N])
            holes = sb2("holes", [P, N], BF16)
            logits = sb2("logits", [P, LOGIT_SLOTS, ROWHALF])
            slots = sb2("slots", [P, RING2, GROUP])
            x_ring = sb2("x_ring2", [P, RING2, H])
            weights = sb2("weights", [P, WEIGHTS, GROUP])
            products = sb2("products", [P, WEIGHTS, GROUP])
            neg_max_bc = sb2("neg_max_bc", [P, 2, HEADS, GROUP])
            heads = sb2("heads", [P, HEADS, GROUP])
            scratch = sb2("scratch", [P, PART])
            eminus = sb2("eminus", [P, PART])
            half_max = sb2("half_max", [P, 2 * HEADS])
            neg_max = sb2("neg_max", [P, TILES * HEADS])
            expsum = sb2("expsum", [P, TILES * HEADS * 2])
            pair_sum = sb2("pair_sum", [P, PAIR * HEADS])
            inv_sum = sb2("inv_sum", [P, PAIR, HEADS])
            max_diag_sb = sb2("max_diag_sb", [P, HEADS, P])
            scale_diag_sb = sb2("scale_diag_sb", [P, HEADS, PAIR, P])
            third_eye = sb2("third_eye", [P, P])
            neg_e_col = sb2("neg_e_col", [P, TILES * EROWS])
            minus_half = sb2("minus_half", [P, PAIR])
            state, edge_sb, mix, tr, tz, hnb, cand, diff = (
                sb2(n, [P, PW]) for n in ("state", "edge_sb", "mix", "tr2", "tz2", "hnb2", "cand2", "diff2"))
            y = sb2("y", [P, PAIR, H])
            moments = sb2("moments", [P, PAIR, 6])
            mean_var = sb2("mean_var", [P, PAIR, 2])
            var_eps = sb2("var_eps", [P, PAIR])
            rstd = sb2("rstd", [P, PAIR])
            normal = sb2("normal", [P, PAIR, H])

            TAIL_USES = ["scale01", "scale2", "mix", "gates_rz", "gates_n"]
            ROW_ONLY = ["max0", "max1"]
            TAIL_ONLY = TAIL_USES + ["turned"]
            BOTH = TAIL_USES + ["max0", "turned", "max1"]
            SECTIONS = [("rows", 0, ROW_ONLY)]
            for g in range(GROUPS):
                SECTIONS.append(("group", g, ROW_ONLY if g == 0 else BOTH if g < GROUPS - 1 else TAIL_ONLY))
            SECTIONS.append(("tail", GROUPS, TAIL_ONLY))

            def use(section, t, what):
                before = TURNS * sum(len(uses) for _, _, uses in SECTIONS[:section])
                uses = SECTIONS[section][2]
                at = uses.index(what)
                return at % 2, t * (len(uses) // 2) + (before // 2 + at // 2)

            def has_rows(section):
                return "max0" in SECTIONS[section][2]

            def has_tail(section):
                return "mix" in SECTIONS[section][2]

            MAX_SPREAD = [4, 7]

            def first_tile(section):
                return 0 if section == 0 else (SECTIONS[section][1] + 1) * GTILES

            def first_pair(section):
                return (SECTIONS[section][1] - 1) * (GTILES // PAIR)

            with nc.Block() as block:

                def on_negatives(eng, program):
                    count = eng.value_load(negative_int[UCOLS:UCOLS + 1, 0:1], min_val=0, max_val=N)
                    with eng.If(count > 0):
                        program(True)
                    with eng.Else():
                        program(False)

                def turns(eng, count=TURNS):
                    return eng.Fori(0, count)


                @block.sync
                def _(sp):
                    def load_row(tile):
                        sp.wait_ge(row_used, tile + 1)
                        src = adj_rows[bass.ds(tile, 1), :, :] if not isinstance(tile, int) else adj_rows[tile:tile + 1, :, :]
                        sp.dma_start(row[:, :], src.rearrange("o p j -> p (o j)")).then_inc(row_loaded, 16)

                    def load_chunk(c, slot):
                        if not isinstance(c, int) or c >= RING2:
                            sp.wait_ge(product_ready, (c + 1 - RING2) * HEADS + WEIGHTS)
                        src = adj_t[bass.ds(c, 1), :, :] if not isinstance(c, int) else adj_t[c:c + 1, :, :]
                        sp.dma_start(slots[:, slot, :], src.rearrange("o p i -> p (o i)")).then_inc(slot_loaded[slot], 16)

                    def load_eminus(tile):
                        for i in range(HEADS * N // PART):
                            k, part = divmod(i, N // PART)
                            sp.wait_ge(eminus_used, tile * (HEADS * N // PART) + (i + 1))
                            sp.dma_start(eminus[:, :], eminus_dram[k, part * PART:(part + 1) * PART].partition_broadcast(P))\
                              .then_inc(eminus_loaded, 16)

                    def turn(section, t, negative, more_rows=True, more_chunks=True):
                        name, g, _ = SECTIONS[section]
                        pair = t + first_pair(section)
                        if has_tail(section):
                            sp.wait_ge(node_ready, pair + 1)
                            cols = bass.ds(pair * PW, PW)
                            sp.dma_start(state[:, :], x_t[:, cols]).then_inc(tail_loaded, 16)
                            sp.dma_start(edge_sb[:, :], edge_dram[:, cols]).then_inc(tail_loaded, 16)
                        for j in range(STEP):
                            if has_rows(section) and j % (STEP // PAIR) == 0:
                                r = j // (STEP // PAIR)
                                tile = t * PAIR + (first_tile(section) + r)
                                if negative:
                                    load_eminus(tile)
                                if more_rows or r < PAIR - 1:
                                    load_row(tile + 1)
                            if name == "group" and (more_chunks or j < STEP - RING2):
                                load_chunk(t * STEP + (g * TILES + j + RING2), j % RING2)
                        if has_tail(section):
                            sp.wait_ge(normed, pair + 1)
                            sp.dma_start(out_tiles[:, bass.ds(pair * PAIR, PAIR), :], normal[:, :, :]).then_inc(stored, 16)

                    def program(negative):
                        for section in range(len(SECTIONS)):
                            last_rows = section == GROUPS - 1
                            last_chunks = section == GROUPS
                            whole_turns = TURNS - (last_rows or last_chunks)
                            with turns(sp, whole_turns) as t:
                                turn(section, t, negative)
                            if last_rows or last_chunks:
                                turn(section, TURNS - 1, negative, not last_rows, not last_chunks)

                    sp.sem_inc(stored, 1)
                    load_row(0)
                    sp.dma_start(wg[:, 0, :], node_wih).then_inc(inputs2, 16)
                    sp.dma_start(wg[:, 1, :], node_whh).then_inc(inputs2, 16)
                    for c in range(RING2):
                        load_chunk(c, c)
                    on_negatives(sp, program)
                    sp.wait_ge(stored, 16 * TILES // PAIR + 1)


                @block.gpsimd
                def _(pool):
                    nc.gpsimd.memset(minus_half[:, :], -0.5).then_inc(minus_half_made, 1)
                    pool.wait_ge(minus_half_made, 1)

                    def turn(section, t):
                        name, g, _ = SECTIONS[section]
                        for j in range(STEP):
                            if has_rows(section) and j % (STEP // PAIR) == 0:
                                tile = t * PAIR + (first_tile(section) + j // (STEP // PAIR))
                                wait_apart(pool, pool_waits, row_loaded, (tile + 1) * 16)
                                own = row[:, bass.ds(tile * P, P)]
                                nc.gpsimd.tensor_tensor(own, own, keep_sb[:, GROUPS - 1, :], ALU.mult).then_inc(row_clean, 1)
                            if name == "group":
                                s = j % RING2
                                c = t * STEP + (g * TILES + j)
                                wait_apart(pool, pool_waits, slot_loaded[s],
                                           (t * (STEP // RING2) + (g * TILES // RING2 + j // RING2 + 1)) * 16)
                                own = slots[:, s, j * P:(j + 1) * P]
                                nc.gpsimd.tensor_tensor(
                                    own, own, keep_sb[:, bass.ds(t + (GROUPS - 1 - g), 1), :].rearrange("p o i -> p (o i)"),
                                    ALU.mult)
                                pool.wait_ge(unit_done, (c + 1) * HEADS)
                                nc.gpsimd.tensor_copy(x_ring[:, s, :], x_sb[:, bass.ds(t * STEP + j, 1), :].rearrange("p o i -> p (o i)"))\
                                  .then_inc(slot_staged, 1)
                            if has_tail(section) and j == STEP - 1:
                                pair = t + first_pair(section)
                                pool.wait_ge(var_ready, pair + 1)
                                nc.gpsimd.tensor_tensor(rstd[:, :], var_eps[:, :], minus_half[:, :], ALU.pow).then_inc(rstd_ready, 1)

                    for section in range(len(SECTIONS)):
                        with turns(pool) as t:
                            turn(section, t)


                @block.scalar
                def _(act):
                    def row_exps(tile, r, k):
                        act.wait_ge(max_ready, tile * HEADS + (k + 1))
                        for h in range(2):
                            slot = (HEADS * 2 * r + 2 * k + h) % LOGIT_SLOTS
                            nc.scalar.activation(logits[:, slot, :], logits[:, slot, :], ACT.Exp,
                                                 bias=neg_max[:, bass.ds(tile * HEADS + k, 1)],
                                                 accum_out=expsum[:, bass.ds(tile * (2 * HEADS) + (2 * k + h), 1)])\
                              .then_inc(logits_used, 1)

                    def spread_copy(section, t, r):
                        b, n = use(section, t, f"max{r}")
                        act.wait_ge(misc_filled[b], n + 1)
                        parity = 0 if section == 0 else (SECTIONS[section][1] + 1) % 2
                        nc.scalar.activation(neg_max_bc[:, parity, :, bass.ds(t * PW + r * P, P)],
                                             ps_m[b][:, 0:HEADS * P].rearrange("p (k i) -> p k i", k=HEADS), ACT.Copy)\
                          .then_inc(misc_read[b], 1)

                    def turn(section, t, negative):
                        name, g, _ = SECTIONS[section]
                        for j in range(STEP):
                            r, q = divmod(j, STEP // PAIR)
                            tile = t * PAIR + (first_tile(section) + r)
                            exps_first = negative
                            if has_rows(section) and q >= 1 and exps_first:
                                row_exps(tile, r, q - 1)
                            if name == "group":
                                for k in range(HEADS):
                                    for s in range(2 if negative else 1):
                                        unit = t * HEAD_UNITS + (g * TILES * HEADS + j * HEADS + k)
                                        i = 2 * (j * HEADS + k) + s if negative else k
                                        weight = weights[:, i % WEIGHTS, :]
                                        if not negative and k in DVE_CLAMPS:
                                            n = len(DVE_CLAMPS)
                                            act.wait_ge(clamped, t * (STEP * n) + ((g * TILES + j) * n + DVE_CLAMPS.index(k) + 1))
                                            nc.scalar.activation(weight, weight, ACT.Exp).then_inc(weight_ready, 1)
                                            continue
                                        n = 2 if negative else 1
                                        if negative:
                                            act.wait_ge(weight_used, unit * 2 + (s + 1))
                                        else:
                                            act.wait_ge(product_ready, unit + 1)
                                        col = t * (STEP * EROWS) + (j * EROWS + s * HEADS + k)
                                        nc.scalar.activation(weight, neg_max_bc[:, g % 2, k, :], ACT.Relu, scale=-1.0,
                                                             bias=neg_e_col[:, bass.ds(col, 1)]).then_inc(exponent_ready, 1)
                                        per = 2 * HEADS if negative else HEADS - len(DVE_CLAMPS)
                                        act.wait_ge(exponent_ready, t * (STEP * per) + (
                                            (g * TILES + j) * per + (2 * k + s if negative else k) + 1))
                                        nc.scalar.activation(weight, weight, ACT.Exp, scale=-1.0).then_inc(weight_ready, 1)
                            if has_rows(section) and q >= 1 and not exps_first:
                                row_exps(tile, r, q - 1)
                            if has_tail(section):
                                pair = t + first_pair(section)
                                if j == 2:
                                    b, n = use(section, t, "mix")
                                    act.wait_ge(misc_filled[b], n + 1)
                                    nc.scalar.activation(mix[:, :], ps_m[b][:, 0:PW], ACT.Copy).then_inc(misc_read[b], 1)
                                if j == 4:
                                    b, n = use(section, t, "gates_rz")
                                    act.wait_ge(misc_filled[b], n + 1)
                                    act.wait_ge(node_ready, pair + 1)
                                    nc.scalar.activation(tr[:, :], ps_m[b][:, 0:PW], ACT.Tanh, bias=half_rz[:, 1, 0:1], scale=0.5)
                                    nc.scalar.activation(tz[:, :], ps_m[b][:, PW:2 * PW], ACT.Tanh, bias=half_rz[:, 1, 1:2], scale=0.5)\
                                      .then_inc(misc_read[b], 1)
                                if j == 5:
                                    b, n = use(section, t, "gates_n")
                                    act.wait_ge(misc_read[b], n + 2)
                                    nc.scalar.activation(cand[:, :], hnb[:, :], ACT.Tanh).then_inc(node_n_ready, 1)
                            if has_rows(section) and j in MAX_SPREAD:
                                spread_copy(section, t, MAX_SPREAD.index(j))

                    def program(negative):
                        for section in range(len(SECTIONS)):
                            name, g, _ = SECTIONS[section]
                            if name == "group":
                                for r in range(PAIR):
                                    b, n = use(section - 1, TURNS - 1, f"max{r}")
                                    act.wait_ge(misc_read[b], n + 2)
                            with turns(act) as t:
                                turn(section, t, negative)
                            if name == "group":
                                act.wait_ge(heads_closed, (g + 1) * HEADS * HALVES)
                                for k in range(HEADS):
                                    nc.scalar.activation(heads[:, k, 0:HALF], ps_u[k][0][:, :], ACT.Copy).then_inc(heads_copied, 1)

                    act.sem_inc(logits_used, LOGIT_SLOTS)
                    act.wait_ge(constants2, 1)
                    on_negatives(act, program)
                    act.wait_ge(constants2, 1)


                @block.tensor
                def _(pe):
                    pe.sem_inc(unit_done, RING2 * HEADS)
                    pe.wait_ge(inputs2, 32)
                    pe.wait_ge(constants2, 1)

                    def spread(section, t, what, ready, count, ncols, source):
                        b, n = use(section, t, what)
                        pe.wait_ge(misc_read[b], n + 1)
                        pe.wait_ge(ready, count)
                        nc.tensor.matmul(ps_m[b][:, 0:ncols], ones_sb[:, :], source, start=True, stop=True)\
                          .then_inc(misc_filled[b], 1)

                    def spread_max(section, t, tile, r):
                        spread(section, t, f"max{r}", max_diag, tile + 1, HEADS * P,
                               max_diag_sb[:, :, :].rearrange("p k i -> p (k i)"))

                    def turn(section, t):
                        name, g, _ = SECTIONS[section]
                        pair = t + first_pair(section)
                        cols = bass.ds(t * PW, PW)
                        for j in range(STEP):
                            if has_rows(section) and j in MAX_SPREAD:
                                r = MAX_SPREAD.index(j)
                                spread_max(section, t, t * PAIR + (first_tile(section) + r), r)
                            if name == "group":
                                c = t * STEP + (g * TILES + j)
                                pe.wait_ge(slot_staged, c + 1)
                                for k in range(HEADS):
                                    pe.wait_ge(product_ready, c * HEADS + (k + 1 + WEIGHTS))
                                    for h in range(HALVES):
                                        last = nc.tensor.matmul(ps_u[k][h][:, :], x_ring[:, j % RING2, :],
                                                                products[:, k, h * HALF:(h + 1) * HALF],
                                                                start=False, stop=False)
                                    last.then_inc(unit_done, 1)
                            if not has_tail(section):
                                continue
                            if j == 0:
                                spread(section, t, "scale01", scale_diag, pair + 1, 2 * PW,
                                       scale_diag_sb[:, 0:2, :, :].rearrange("p k r i -> p (k r i)"))
                                spread(section, t, "scale2", scale_diag, pair + 1, PW,
                                       scale_diag_sb[:, 2, :, :].rearrange("p r i -> p (r i)"))
                            if j == 1:
                                b, n = use(section, t, "mix")
                                for before in ("scale01", "scale2"):
                                    bb, nn = use(section, t, before)
                                    pe.wait_ge(misc_read[bb], nn + 2)
                                pe.wait_ge(misc_read[b], n + 1)
                                for k in range(HEADS):
                                    last = nc.tensor.matmul(ps_m[b][:, 0:PW], w_sb[:, k, :], heads[:, k, cols],
                                                            start=(k == 0), stop=(k == HEADS - 1))
                                last.then_inc(misc_filled[b], 1)
                            if j == 2:
                                b, n = use(section, t, "gates_rz")
                                bb, nn = use(section, t, "mix")
                                pe.wait_ge(misc_read[bb], nn + 2)
                                pe.wait_ge(misc_read[b], n + 1)
                                pe.wait_ge(tail_loaded, (pair + 1) * 32)
                                for i in range(2):
                                    dst = ps_m[b][:, i * PW:(i + 1) * PW]
                                    nc.tensor.matmul(dst, wg[:, 0, i * H:(i + 1) * H], mix[:, :], start=True, stop=False)
                                    last = nc.tensor.matmul(dst, wg[:, 1, i * H:(i + 1) * H], state[:, :], start=False, stop=True)
                                last.then_inc(misc_filled[b], 1)
                                b, n = use(section, t, "gates_n")
                                pe.wait_ge(misc_read[b], n + 1)
                                nc.tensor.matmul(ps_m[b][:, 0:PW], wg[:, 0, 2 * H:3 * H], mix[:, :], start=True, stop=True)
                                nc.tensor.matmul(ps_m[b][:, PW:2 * PW], wg[:, 1, 2 * H:3 * H], state[:, :], start=True, stop=True)\
                                  .then_inc(misc_filled[b], 1)
                            if j == 6:
                                b, n = use(section, t, "turned")
                                pe.wait_ge(misc_read[b], n + 1)
                                pe.wait_ge(node_ready, pair + 2)
                                for i in range(PAIR):
                                    last = nc.tensor.transpose(ps_m[b][:, i * P:(i + 1) * P], diff[:, i * P:(i + 1) * P], eye_sb[:, :])
                                last.then_inc(misc_filled[b], 1)

                    for section in range(len(SECTIONS)):
                        name, g, _ = SECTIONS[section]
                        if name == "group":
                            pe.wait_ge(heads_copied, g * HEADS * HALVES)
                            for k in range(HEADS):
                                for h in range(HALVES):
                                    nc.tensor.matmul(ps_u[k][h][:, :], zeros_sb[:, 0:P], zeros_sb[:, :], start=True, stop=False)
                        with turns(pe) as t:
                            turn(section, t)
                        if name == "group":
                            for k in range(HEADS):
                                for h in range(HALVES):
                                    nc.tensor.matmul(ps_u[k][h][:, :], zeros_sb[:, 0:P], zeros_sb[:, :], start=False, stop=True)\
                                      .then_inc(heads_closed, 1)


                @block.vector
                def _(dve):
                    def chain(expr_base):
                        local = [0]

                        def link(ins, apart=False):
                            local[0] += 1
                            ins.then_inc(dve_step2, 1)
                            if apart:
                                wait_apart(dve, dve_waits, dve_step2, expr_base + local[0])
                            else:
                                dve.wait_ge(dve_step2, expr_base + local[0])
                        link.local = local
                        return link

                    def row_holes(section, t, tile, link):
                        dve.wait_ge(row_clean, tile + 1)
                        return nc.vector.tensor_scalar(holes[:, :], row[:, :], 0.0, MASKED, ALU.is_le, ALU.mult)

                    def row_logits(tile, r, k, h, link):
                        slot = (HEADS * 2 * r + 2 * k + h) % LOGIT_SLOTS
                        wait_apart(dve, dve_waits, logits_used, tile * (2 * HEADS) + (2 * k + h + 1))
                        cols = slice(h * ROWHALF, (h + 1) * ROWHALF)
                        ins = nc.vector.tensor_tensor_reduce(
                            out=logits[:, slot, :], in0=holes[:, cols], in1=e_bc[:, k, cols], scale=1.0,
                            scalar=LOWEST, op0=ALU.add, op1=ALU.max, accum_out=half_max[:, 2 * k + h:2 * k + h + 1])
                        if h == 1:
                            link(ins)
                            nc.vector.tensor_scalar(neg_max[:, bass.ds(tile * HEADS + k, 1)], half_max[:, 2 * k:2 * k + 1],
                                                    half_max[:, 2 * k + 1:2 * k + 2], -1.0, ALU.max, ALU.mult)\
                              .then_inc(max_ready, 1)

                    def row_max_negative(tile, r, k, link):
                        for h in range(2):
                            i = HEADS * 2 * r + 2 * k + h
                            slot = i % LOGIT_SLOTS
                            dve.wait_ge(logits_used, tile * (2 * HEADS) + (2 * k + h + 1))
                            for q in range(ROWHALF // PART):
                                part = h * (ROWHALF // PART) + q
                                cols = slice(part * PART, (part + 1) * PART)
                                dst = logits[:, slot, q * PART:(q + 1) * PART]
                                link(nc.vector.tensor_scalar(scratch[:, :], row[:, cols], 0.0, MASKED, ALU.is_ge, ALU.mult))
                                dve.wait_ge(eminus_loaded, (tile * (HEADS * N // PART) + (k * (N // PART) + part + 1)) * 16)
                                nc.vector.tensor_tensor(scratch[:, :], scratch[:, :], eminus[:, :], ALU.add)\
                                  .then_inc(eminus_used, 1)
                                link(nc.vector.tensor_tensor(dst, holes[:, cols], e_bc[:, k, cols], ALU.add))
                                dve.wait_ge(eminus_used, tile * (HEADS * N // PART) + (k * (N // PART) + part + 2))
                                link(nc.vector.tensor_tensor(dst, dst, scratch[:, :], ALU.max))
                            link(nc.vector.tensor_reduce(half_max[:, 2 * k + h:2 * k + h + 1], logits[:, slot, :], axis=AX.X, op=ALU.max))
                        nc.vector.tensor_scalar(neg_max[:, bass.ds(tile * HEADS + k, 1)], half_max[:, 2 * k:2 * k + 1],
                                                half_max[:, 2 * k + 1:2 * k + 2],
                                                -1.0, ALU.max, ALU.mult).then_inc(max_ready, 1)

                    def row_diag(tile):
                        dve.wait_ge(max_ready, (tile + 1) * HEADS)
                        nc.vector.tensor_tensor(
                            max_diag_sb[:, :, :], eye_sb[:, :].unsqueeze(1).broadcast_to([P, HEADS, P]),
                            neg_max[:, bass.ds(tile * HEADS, HEADS)].unsqueeze(2).broadcast_to([P, HEADS, P]), ALU.mult)\
                          .then_inc(max_diag, 1)

                    def clamp(section, t, j, k):
                        g = SECTIONS[section][1]
                        unit = t * HEAD_UNITS + (g * TILES * HEADS + j * HEADS + k)
                        dve.wait_ge(product_ready, unit + 1)
                        nc.vector.tensor_scalar(weights[:, k, :], neg_max_bc[:, g % 2, k, :],
                                                e_col[:, bass.ds(t * (STEP * EROWS) + (j * EROWS + k), 1)], 0.0,
                                                ALU.add, ALU.min).then_inc(clamped, 1)

                    def column_units(section, t, j, negative, link):
                        g = SECTIONS[section][1]
                        for k in range(HEADS):
                            unit = t * HEAD_UNITS + (g * TILES * HEADS + j * HEADS + k)
                            slot = slots[:, j % RING2, :]
                            if k == 0:
                                dve.wait_ge(slot_staged, t * STEP + (g * TILES + j + 1))
                            dve.wait_ge(unit_done, unit + (1 + RING2 * HEADS - WEIGHTS))
                            if not negative:
                                dve.wait_ge(weight_ready, unit + 1)
                                nc.vector.tensor_tensor(products[:, k, :], weights[:, k, :], slot, ALU.mult)\
                                  .then_inc(product_ready, 1)
                                if k in DVE_CLAMPS and j < STEP - 1:
                                    clamp(section, t, j + 1, k)
                                continue
                            i = 2 * (j * HEADS + k)
                            dve.wait_ge(weight_ready, unit * 2 + 2)
                            for q in range(GROUP // PART):
                                part = slice(q * PART, (q + 1) * PART)
                                link(nc.vector.tensor_scalar(scratch[:, :], slot[:, part], 0.0, None, ALU.max))
                                link(nc.vector.tensor_tensor(products[:, k, part], weights[:, i % WEIGHTS, part],
                                                             scratch[:, :], ALU.mult))
                                link(nc.vector.tensor_scalar(scratch[:, :], slot[:, part], 0.0, None, ALU.min))
                                link(nc.vector.tensor_tensor(scratch[:, :], weights[:, (i + 1) % WEIGHTS, part],
                                                             scratch[:, :], ALU.mult))
                                link(nc.vector.tensor_tensor(products[:, k, part], products[:, k, part], scratch[:, :], ALU.add))
                            dve.sem_inc(product_ready, 1)
                            dve.sem_inc(weight_used, 2)

                    def tail_scale_diag(section, t, pair, link):
                        sums = expsum[:, bass.ds(pair * (PAIR * HEADS * 2), PAIR * HEADS * 2)].rearrange("p (c h) -> p c h", h=2)
                        link(nc.vector.tensor_reduce(pair_sum[:, :], sums, axis=AX.X, op=ALU.add))
                        link(nc.vector.reciprocal(inv_sum[:, :, :].rearrange("p r k -> p (r k)"), pair_sum[:, :]))
                        nc.vector.tensor_tensor(
                            scale_diag_sb[:, :, :, :].rearrange("p k r i -> p k r i"),
                            third_eye[:, :].unsqueeze(1).unsqueeze(1).broadcast_to([P, HEADS, PAIR, P]),
                            inv_sum[:, :, :].rearrange("p r k -> p k r").unsqueeze(3).broadcast_to([P, HEADS, PAIR, P]), ALU.mult)\
                          .then_inc(scale_diag, 1)

                    def tail_scale(section, t):
                        cols = bass.ds(t * PW, PW)
                        for what, k0, k1 in (("scale01", 0, 2), ("scale2", 2, 3)):
                            b, n = use(section, t, what)
                            dve.wait_ge(misc_filled[b], n + 1)
                            part = heads[:, k0:k1, cols]
                            nc.vector.tensor_tensor(part, part, ps_m[b][:, 0:(k1 - k0) * PW].rearrange("p (k i) -> p k i", i=PW),
                                                    ALU.mult).then_inc(misc_read[b], 1)

                    def tail_candidate(section, t, link):
                        b, n = use(section, t, "gates_n")
                        dve.wait_ge(misc_filled[b], n + 1)
                        link(nc.vector.tensor_scalar(hnb[:, :], ps_m[b][:, PW:2 * PW], bias[:, 3, 2:3], 0.5, ALU.add, ALU.mult))
                        bb, nn = use(section, t, "gates_rz")
                        dve.wait_ge(misc_read[bb], nn + 2)
                        link(nc.vector.scalar_tensor_tensor(hnb[:, :], tr[:, :], 1.0, hnb[:, :], ALU.add, ALU.mult))
                        nc.vector.scalar_tensor_tensor(hnb[:, :], ps_m[b][:, 0:PW], bias[:, 2, 2:3], hnb[:, :], ALU.add, ALU.add)\
                          .then_inc(misc_read[b], 1)

                    def tail_state(pair, link):
                        dve.wait_ge(tail_loaded, (pair + 1) * 32)
                        dve.wait_ge(node_n_ready, pair + 1)
                        link(nc.vector.tensor_tensor(diff[:, :], state[:, :], cand[:, :], ALU.subtract))
                        link(nc.vector.scalar_tensor_tensor(diff[:, :], tz[:, :], 1.0, diff[:, :], ALU.add, ALU.mult))
                        link(nc.vector.scalar_tensor_tensor(diff[:, :], diff[:, :], 0.5, cand[:, :], ALU.mult, ALU.add))
                        nc.vector.tensor_tensor(diff[:, :], diff[:, :], edge_sb[:, :], ALU.add).then_inc(node_ready, 1)

                    def tail_residual(section, t, pair, link):
                        b, n = use(section, t, "turned")
                        dve.wait_ge(misc_filled[b], n + 1)
                        for i in range(PAIR):
                            tile = pair * PAIR + i
                            ins = nc.vector.scalar_tensor_tensor(
                                y[:, i, :], ps_m[b][:, i * P:(i + 1) * P], d_sb[:, bass.ds(tile, 1)],
                                x_sb[:, bass.ds(tile, 1), :].rearrange("p o h -> p (o h)"), ALU.mult, ALU.add)
                        ins.then_inc(misc_read[b], 1)
                        dve.wait_ge(misc_read[b], n + 2)
                        for i in range(PAIR):
                            ins = nc.vector.bn_stats(moments[:, i, :], y[:, i, :])
                        link(ins, apart=True)
                        for i in range(PAIR):
                            ins = nc.vector.bn_aggr(mean_var[:, i, :], moments[:, i, :])
                        link(ins)
                        nc.vector.tensor_scalar(var_eps[:, :], mean_var[:, :, 1], EPS, None, ALU.add).then_inc(var_ready, 1)

                    def tail_norm(pair):
                        dve.wait_ge(rstd_ready, pair + 1)
                        dve.wait_ge(stored, pair * 16 + 1)
                        for i in range(PAIR):
                            ins = nc.vector.tensor_scalar(normal[:, i, :], y[:, i, :], mean_var[:, i, 0:1], rstd[:, i:i + 1],
                                                          ALU.subtract, ALU.mult)
                        ins.then_inc(normed, 1)

                    def turn(section, t, negative, link):
                        name, g, _ = SECTIONS[section]
                        pair = t + first_pair(section)
                        if name == "group":
                            for r in range(PAIR):
                                b, n = use(section - 1, TURNS - 1, f"max{r}")
                                dve.wait_ge(misc_read[b], n + 2)
                            if not negative:
                                for k in DVE_CLAMPS:
                                    clamp(section, t, 0, k)
                        for j in range(STEP):
                            r, q = divmod(j, STEP // PAIR)
                            tile = t * PAIR + (first_tile(section) + r)
                            if has_tail(section) and j == 0:
                                tail_scale_diag(section, t, pair, link)
                            if has_rows(section):
                                for part in ROW_PLAN[q] if not negative else []:
                                    if part == "holes":
                                        link(row_holes(section, t, tile, link))
                                        dve.sem_inc(row_used, 1)
                                    elif part == "diagonal":
                                        row_diag(tile)
                                    else:
                                        row_logits(tile, r, *part, link)
                                if negative and q == 0:
                                    link(row_holes(section, t, tile, link))
                                if negative and q < HEADS:
                                    row_max_negative(tile, r, q, link)
                                if negative and q == HEADS:
                                    dve.sem_inc(row_used, 1)
                                    row_diag(tile)
                            if name == "group":
                                column_units(section, t, j, negative, link)
                            if has_tail(section):
                                if j == 1:
                                    tail_scale(section, t)
                                if j == 4:
                                    tail_candidate(section, t, link)
                                if j == 5:
                                    tail_state(pair, link)
                                if j == 7:
                                    tail_residual(section, t, pair, link)
                                    tail_norm(pair)

                    ROW_LINKS = {False: PAIR * (1 + HEADS), True: PAIR * (1 + HEADS * 2 * (1 + 3 * ROWHALF // PART))}
                    COLUMN_LINKS = {False: 0, True: HEAD_UNITS * 5 * (GROUP // PART)}
                    TAIL_LINKS = 2 + 2 + 3 + 2

                    def program(negative):
                        done = 1
                        for section in range(len(SECTIONS)):
                            name, g, _ = SECTIONS[section]
                            per_turn = (has_rows(section) * ROW_LINKS[negative] + (name == "group") * COLUMN_LINKS[negative]
                                        + has_tail(section) * TAIL_LINKS)
                            with turns(dve) as t:
                                link = chain(t * per_turn + done)
                                turn(section, t, negative, link)
                                assert link.local[0] == per_turn, (link.local, per_turn)
                            done += TURNS * per_turn
                            if name == "group":
                                dve.wait_ge(heads_closed, (g + 1) * HEADS * HALVES)
                                for k in range(HEADS):
                                    nc.vector.tensor_copy(heads[:, k, HALF:2 * HALF], ps_u[k][1][:, :]).then_inc(heads_copied, 1)
                                dve.wait_ge(heads_copied, (g + 1) * HEADS * HALVES)

                    nc.vector.tensor_scalar(neg_e_col[:, :], e_col[:, :], -1.0, None, ALU.mult)
                    nc.vector.tensor_scalar(third_eye[:, :], eye_sb[:, :], 1.0 / HEADS, None, ALU.mult).then_inc(constants2, 1)
                    dve.sem_inc(row_used, 1)
                    dve.sem_inc(eminus_used, 1)
                    dve.sem_inc(weight_used, WEIGHTS)
                    dve.sem_inc(product_ready, WEIGHTS)
                    dve.sem_inc(dve_step2, 1)
                    dve.sem_inc(node_ready, 1)
                    for b in range(2):
                        dve.sem_inc(misc_read[b], 1)
                    dve.wait_ge(constants2, 1)
                    dve.wait_ge(d_loaded, 16)
                    on_negatives(dve, program)
                    dve.wait_ge(constants2, 1)


_OUTS = [((N, H), "float32")]


def kernel(**inputs):
    import numpy as _np
    import concourse.bacc as _bacc
    from concourse import mybir as _mybir
    from concourse.bass_utils import run_bass_kernel_spmd as _run

    c = _np.ascontiguousarray
    pre = "L0_gnn_"
    adj, x = _np.asarray(inputs["adj"]), _np.asarray(inputs["x"])
    gate_biases = [_np.asarray(inputs[pre + n]).reshape(3, H).T for n in ("edge_bih", "edge_bhh", "node_bih", "node_bhh")]
    row_pick = _np.zeros((2 * UCOLS, EROWS), _np.float32)
    for k in range(HEADS):
        for s in range(SPLITS):
            first = 1 + s * EROWS + 2 * k
            row_pick[[first, UCOLS + first + 1], k] = 1.0
            row_pick[[first + 1, UCOLS + first], HEADS + k] = 1.0
    keep = _np.ones((P, KEEP, P), _np.float32)
    keep[:, GROUPS - 1, :] -= _np.eye(P, dtype=_np.float32)
    w = _np.asarray(inputs[pre + "gat_W"])
    arrays = {
        "x": c(x), "x_t": c(x.T), "adj": c(adj),
        "adj_t": c(adj.T.reshape(N, GROUPS, GROUP).transpose(1, 0, 2)).reshape(GROUPS * TILES, P, GROUP),
        "w": c(w), "w_t": c(w.transpose(0, 2, 1)),
        "a_t": c(_np.asarray(inputs[pre + "gat_a"]).reshape(EROWS, H).T),
        "edge_wih": c(_np.asarray(inputs[pre + "edge_Wih"]).T), "edge_whh": c(_np.asarray(inputs[pre + "edge_Whh"]).T),
        "node_wih": c(_np.asarray(inputs[pre + "node_Wih"]).T), "node_whh": c(_np.asarray(inputs[pre + "node_Whh"]).T),
        "biases": c(_np.concatenate(gate_biases, axis=1)),
        "row_pick": row_pick, "bc_pick": c(_np.repeat(row_pick[:, :HEADS, None], P, axis=2)),
        "eye": _np.eye(P, dtype=_np.float32), "keep": keep,
    }
    nc = _bacc.Bacc("TRN2", target_bir_lowering=False, num_devices=1, dynamic_dma_scratch_size=1024)
    args = [nc.dram_tensor(f"in_{n}", a.shape, _mybir.dt.from_np(a.dtype), kind="ExternalInput").ap() for n, a in arrays.items()]
    for i, (shape, dtype) in enumerate(_OUTS):
        args.append(nc.dram_tensor(f"out_{i}", shape, _mybir.dt.from_np(_np.dtype(dtype)), kind="ExternalOutput").ap())
    gnn_kernel(nc, *args)
    r = _run(nc, [{f"in_{n}": a for n, a in arrays.items()}], core_ids=[0])
    return r.results[0]["out_0"]
```

```python
import numpy as np
import concourse.bass as bass
from concourse import mybir
from contextlib import ExitStack

ALU = mybir.AluOpType
ACT = mybir.ActivationFunctionType
AX = mybir.AxisListType
F32 = mybir.dt.float32
BF16 = mybir.dt.bfloat16
I32 = mybir.dt.int32

N, H, HEADS = 4096, 128, 3
P = 128
TILES = N // P
GROUP = 1024
GROUPS = N // GROUP
GTILES = GROUP // P
HALF = 512
HALVES = GROUP // HALF
STEP = 8
TURNS = TILES // STEP
PAIR = 2
PW = PAIR * P
HEAD_UNITS = STEP * HEADS
RING1, MASKS = 8, 4
RING2, WEIGHTS = 4, 3
LOGIT_SLOTS = 3
ROWHALF = N // 2
PART = 512
KEEP = 2 * GROUPS - 1
MASKED = 1.0e30
HIGHEST = 3.0e38
DVE_CLAMPS = [1]
ACT_BOUNDS = [k for k in range(HEADS) if k not in DVE_CLAMPS]
ROW_PLAN = [["holes", "bounds", (0, 0)], [(0, 1), (1, 0)], [(1, 1), (2, 0)], [(2, 1), "diagonal"]]
SLOPE = 0.2
EPS = 1e-5
EROWS = 2 * HEADS
SPLITS = 3
UCOLS = 32


def wait_apart(eng, passed, semaphore, value):
    eng.wait_ge(semaphore, value)
    eng.sem_inc(passed, 1)


def gnn_kernel(nc, x, x_t, adj, adj_t, w, w_t, a_t, edge_wih, edge_whh, node_wih, node_whh,
               biases, row_pick, bc_pick, eye, keep, out):
    x_tiles = x.rearrange("(t p) h -> p t h", p=P)
    adj_rows = adj.rearrange("(t p) j -> t p j", p=P)
    out_tiles = out.rearrange("(t p) h -> p t h", p=P)
    diagonal = bass.AP(tensor=adj.tensor, offset=0, ap=[[N + 1, P], [P * (N + 1), TILES]])

    edge_dram = nc.dram_tensor("edge_out", (P, N), F32, kind="Internal").ap()
    eminus_dram = nc.dram_tensor("e_minus", (HEADS, N), F32, kind="Internal").ap()

    whole = ExitStack()
    with whole:
        def sb(name, shape, dt=F32, ctx=whole):
            return ctx.enter_context(nc.sbuf_tensor(name, shape, dt))

        def sem(name):
            return whole.enter_context(nc.semaphore(name))

        x_sb = sb("x_sb", [P, TILES, H])
        neg_e_bc = sb("neg_e_bc", [P, HEADS, N])
        neg_e_col = sb("neg_e_col", [P, TILES * EROWS])
        w_sb = sb("w_sb", [P, HEADS, H])
        wg = sb("wg", [P, 2, 3 * H])
        bias = sb("bias", [P, 4, 3])
        half_rz = sb("half_rz", [P, 2, 2])
        eye_sb = sb("eye_sb", [P, P])
        ones_sb = sb("ones_sb", [P, P])
        zeros_sb = sb("zeros_sb", [P, HALF], BF16)
        keep_sb = sb("keep_sb", [P, KEEP, P])
        d_sb = sb("d_sb", [P, TILES])
        row = sb("row", [P, N])
        negatives = sb("negatives", [P, GROUPS])
        negative_max = sb("negative_max", [P, 1])
        negative_int = sb("negative_int", [P, 1], I32)

        dve_waits, pe_waits, pool_waits = sem("dve_waits"), sem("pe_waits"), sem("pool_waits")

        row_loaded = sem("row_loaded")
        for_u_loaded, d_loaded = sem("for_u_loaded"), sem("d_loaded")
        setup_loaded = sem("setup_loaded")
        setup_made = sem("setup_made")
        v_ready, v_copied, u_ready, u_split = (sem(n) for n in ("v_ready", "v_copied", "u_ready", "u_split"))
        chunk_loaded = [sem(f"chunk_loaded{i}") for i in range(RING1)]
        chunk_staged = sem("chunk_staged")
        masks_ready = sem("masks_ready")
        chunk_done = sem("chunk_done")
        sums_closed = sem("sums_closed")
        st_copied, pm_copied = sem("st_copied"), sem("pm_copied")
        filled = [sem(f"filled{b}") for b in range(4)]
        emptied = [sem(f"emptied{b}") for b in range(4)]
        slope_ready = sem("slope_ready")
        eminus_stored = sem("eminus_stored")
        n_ready = sem("n_ready")
        edge_ready, edge_stored = sem("edge_ready"), sem("edge_stored")
        dve_step = sem("dve_step")
        flag_made = sem("flag_made")

        with ExitStack() as one:
            def sb1(name, shape, dt=F32):
                return sb(name, shape, dt, one)

            ps_s = [one.enter_context(nc.psum_tensor(f"ps_s{i}", [P, HALF], F32)) for i in range(HALVES)]
            ps_pm = [one.enter_context(nc.psum_tensor(f"ps_pm{i}", [P, HALF], F32)) for i in range(HALVES)]
            ps_g = [one.enter_context(nc.psum_tensor(f"ps_g{i}", [P, HALF], F32)) for i in range(4)]

            xt_sb = sb1("xt_sb", [P, N])
            chunks = sb1("chunks1", [P, RING1, GROUP])
            masks = sb1("masks", [P, MASKS, 2, GROUP], BF16)
            x_ring = sb1("x_ring1", [P, RING1, H])
            u_ring = sb1("u_ring", [P, RING1, UCOLS], BF16)
            u_all = sb1("u_all", [P, TILES, UCOLS], BF16)
            u_rest = sb1("u_rest", [P, TILES, EROWS])
            wt_sb = sb1("wt_sb", [P, HEADS, H])
            at_sb = sb1("at_sb", [P, EROWS])
            v_sb = sb1("v_sb", [P, EROWS])
            row_pick_sb = sb1("row_pick_sb", [2 * UCOLS, EROWS])
            bc_pick_sb = sb1("bc_pick_sb", [2 * UCOLS, HEADS, P])
            pm_sb = sb1("pm_sb", [2 * UCOLS, HALVES, HALF])
            st_sb = sb1("st_sb", [P, HALVES, HALF])
            sloped = sb1("sloped", [P, 2, HALF])
            e_rows = sb1("e_rows", [EROWS, HALVES, HALF])
            reset_tanh, update_tanh, state_part, n_argument, cand, diff, edge = (
                sb1(n, [P, HALF]) for n in ("reset_tanh", "update_tanh", "state_part", "n_argument", "cand", "diff", "edge"))

            FOR_U = [(wt_sb[:, :, :], w_t.rearrange("k c h -> c k h")), (at_sb[:, :], a_t), (xt_sb[:, :], x_t)]
            SETUP = [(x_sb[:, :, :], x_tiles), (w_sb[:, :, :], w.rearrange("k h c -> h k c")),
                     (wg[:, 0, :], edge_wih), (wg[:, 1, :], edge_whh),
                     (bias[:, :, :], biases.rearrange("p (b g) -> p b g", b=4)),
                     (row_pick_sb[:, :], row_pick), (bc_pick_sb[:, :, :], bc_pick), (eye_sb[:, :], eye),
                     (keep_sb[:, :, :], keep)]
            USES = [5, 4, 4, 4]
            FINISH_TURNS = 2

            with nc.Block() as block:

                @block.sync
                def _(sp):
                    for dst, src in FOR_U:
                        sp.dma_start(dst, src).then_inc(for_u_loaded, 16)
                    for dst, src in SETUP:
                        sp.dma_start(dst, src).then_inc(setup_loaded, 16)
                    with sp.Fori(0, GROUPS) as g:
                        with sp.Fori(0, TURNS) as t:
                            for j in range(STEP):
                                c = TILES * g + STEP * t + j
                                sp.wait_ge(chunk_done, c + 1)
                                sp.dma_start(chunks[:, j, :], adj_t[bass.ds(c, 1), :, :].rearrange("o p i -> p (o i)"))\
                                  .then_inc(chunk_loaded[j], 16)
                    sp.dma_start(row[:, :], adj_rows[0:1, :, :].rearrange("o p j -> p (o j)")).then_inc(row_loaded, 16)
                    with nc.allow_non_contiguous_dma(reason="4096 diagonal elements"):
                        sp.dma_start(d_sb[:, :], diagonal).then_inc(d_loaded, 16)

                @block.gpsimd
                def _(pool):
                    pool.wait_ge(setup_loaded, 16 * len(SETUP))
                    pool.wait_ge(u_split, 1)
                    with pool.Fori(0, GROUPS) as g:
                        with pool.Fori(0, TURNS) as t:
                            for j in range(STEP):
                                wait_apart(pool, pool_waits, chunk_loaded[j], (g * TURNS + t + 1) * 16)
                                block_j = chunks[:, j, j * P:(j + 1) * P]
                                nc.gpsimd.tensor_tensor(
                                    block_j, block_j,
                                    keep_sb[:, bass.ds((t + (GROUPS - 1)) - g, 1), :].rearrange("p o i -> p (o i)"),
                                    ALU.mult)
                                nc.gpsimd.tensor_copy(u_ring[:, j, :], u_all[:, bass.ds(t * STEP + j, 1), :].rearrange("p o i -> p (o i)"))
                                nc.gpsimd.tensor_copy(x_ring[:, j, :], x_sb[:, bass.ds(t * STEP + j, 1), :].rearrange("p o i -> p (o i)"))\
                                  .then_inc(chunk_staged, 1)

                @block.scalar
                def _(act):
                    for start in (st_copied, eminus_stored, edge_stored):
                        act.sem_inc(start, 1)
                    act.wait_ge(setup_loaded, 16 * len(SETUP))
                    act.wait_ge(setup_made, 4)
                    with act.Fori(0, GROUPS) as g:
                        act.wait_ge(sums_closed, (g + 1) * 4)
                        for h in range(HALVES):
                            nc.scalar.activation(st_sb[:, h, :], ps_s[h][:, :], ACT.Copy).then_inc(st_copied, 1)
                        for i in range(8):
                            b, rows = i % 4, EROWS if i < 2 else P
                            act.wait_ge(filled[b], g * USES[b] + i // 4 + 1)
                            if i >= 2:
                                act.wait_ge(emptied[(i - 2) % 4], g * USES[(i - 2) % 4] + (i - 2) // 4 + 2)
                            nc.scalar.activation(sloped[0:rows, i % 2, :], ps_g[b][0:rows, :], ACT.Copy, scale=SLOPE)\
                              .then_inc(slope_ready, 1)
                            if i == 3:
                                act.dma_start(eminus_dram[:, bass.ds(g * GROUP, GROUP)],
                                              e_rows[HEADS:EROWS, :, :].rearrange("k h i -> k (h i)"))\
                                   .then_inc(eminus_stored, 16)
                        for h in range(HALVES):
                            act.wait_ge(filled[0], g * USES[0] + 3 + h)
                            act.wait_ge(edge_ready, g * HALVES + h + 1)
                            nc.scalar.activation(reset_tanh[:, :], ps_g[0][:, :], ACT.Tanh, bias=half_rz[:, 0, 0:1], scale=0.5)\
                              .then_inc(emptied[0], 1)
                            act.wait_ge(filled[1], g * USES[1] + 3 + h)
                            nc.scalar.activation(update_tanh[:, :], ps_g[1][:, :], ACT.Tanh, bias=half_rz[:, 0, 1:2], scale=0.5)\
                              .then_inc(emptied[1], 1)
                            act.wait_ge(emptied[3], g * USES[3] + 3 + h + 1)
                            nc.scalar.activation(cand[:, :], n_argument[:, :], ACT.Tanh).then_inc(n_ready, 1)
                            act.wait_ge(edge_ready, g * HALVES + h + 2)
                            act.dma_start(edge_dram[:, bass.ds(g * GROUP + h * HALF, HALF)], edge[:, :])\
                               .then_inc(edge_stored, 16)
                    act.wait_ge(edge_stored, 16 * GROUPS * HALVES + 1)
                    act.wait_ge(eminus_stored, 16 * GROUPS + 1)

                @block.tensor
                def _(pe):
                    pe.sem_inc(chunk_done, RING1)
                    pe.wait_ge(for_u_loaded, 16 * len(FOR_U))
                    for k in range(HEADS):
                        last = nc.tensor.matmul(ps_g[0][:, 2 * k:2 * k + 2], wt_sb[:, k, :], at_sb[:, 2 * k:2 * k + 2],
                                                start=True, stop=True)
                    last.then_inc(v_ready, 1)
                    pe.wait_ge(v_copied, 1)
                    for t in range(TILES):
                        last = nc.tensor.matmul(ps_g[1][:, EROWS * t:EROWS * (t + 1)], xt_sb[:, t * P:(t + 1) * P],
                                                v_sb[:, :], start=True, stop=True)
                    last.then_inc(u_ready, 1)
                    pe.wait_ge(setup_loaded, 16 * len(SETUP))
                    pe.wait_ge(setup_made, 4)

                    def open_sums(g):
                        pe.wait_ge(st_copied, g * HALVES + 1)
                        pe.wait_ge(pm_copied, g * HALVES + 1)
                        for h in range(HALVES):
                            nc.tensor.matmul(ps_s[h][:, :], zeros_sb[:, 0:P], zeros_sb[:, :], start=True, stop=False)
                            nc.tensor.matmul(ps_pm[h][0:2 * UCOLS, :], zeros_sb[:, 0:2 * UCOLS], zeros_sb[:, :],
                                             start=True, stop=False)

                    def chunk(g, t, j):
                        c = TILES * g + STEP * t + j
                        pe.wait_ge(chunk_staged, c + 1)
                        for h in range(HALVES):
                            nc.tensor.matmul(ps_s[h][:, :], x_ring[:, j, :], chunks[:, j, h * HALF:(h + 1) * HALF],
                                             start=False, stop=False)
                        pe.wait_ge(masks_ready, c + 1)
                        for h in range(HALVES):
                            for m in range(2):
                                last = nc.tensor.matmul(
                                    ps_pm[h][m * UCOLS:(m + 1) * UCOLS, :], u_ring[:, j, :],
                                    masks[:, j % MASKS, m, h * HALF:(h + 1) * HALF],
                                    start=False, stop=False, skip_group_check=True)
                        last.then_inc(chunk_done, 1)

                    def close_sums():
                        for h in range(HALVES):
                            nc.tensor.matmul(ps_s[h][:, :], zeros_sb[:, 0:P], zeros_sb[:, :], start=False, stop=True)\
                              .then_inc(sums_closed, 1)
                            nc.tensor.matmul(ps_pm[h][0:2 * UCOLS, :], zeros_sb[:, 0:2 * UCOLS], zeros_sb[:, :],
                                             start=False, stop=True).then_inc(sums_closed, 1)

                    def scores(g, first, last):
                        for i in range(first, last):
                            b, h = i % 4, i % 2
                            wait_apart(pe, pe_waits, emptied[b], g * USES[b] + i // 4 + 1)
                            if i < 2:
                                nc.tensor.matmul(ps_g[b][0:EROWS, :], row_pick_sb[:, :], pm_sb[:, h, :],
                                                 start=True, stop=True).then_inc(filled[b], 1)
                            else:
                                nc.tensor.matmul(ps_g[b][:, :], bc_pick_sb[:, i // 2 - 1, :], pm_sb[:, h, :],
                                                 start=True, stop=True).then_inc(filled[b], 1)

                    def gates(g, h):
                        state = xt_sb[:, bass.ds(g * GROUP + h * HALF, HALF)]
                        for b in range(4):
                            pe.wait_ge(emptied[b], g * USES[b] + 2 + h + 1)
                            gate = wg[:, :, b * H:(b + 1) * H] if b < 2 else wg[:, :, 2 * H:3 * H]
                            if b < 2:
                                nc.tensor.matmul(ps_g[b][:, :], gate[:, 0, :], st_sb[:, h, :], start=True, stop=False)
                                nc.tensor.matmul(ps_g[b][:, :], gate[:, 1, :], state, start=False, stop=True)\
                                  .then_inc(filled[b], 1)
                            elif b == 2:
                                nc.tensor.matmul(ps_g[b][:, :], gate[:, 1, :], state, start=True, stop=True)\
                                  .then_inc(filled[b], 1)
                            else:
                                nc.tensor.matmul(ps_g[b][:, :], gate[:, 0, :], st_sb[:, h, :], start=True, stop=True)\
                                  .then_inc(filled[b], 1)

                    def score_columns(g):
                        pe.wait_ge(emptied[0], g * USES[0] + 4 + 1)
                        for i in range(GTILES):
                            r = i % (HALF // P)
                            last = nc.tensor.matmul(ps_g[0][:, EROWS * i:EROWS * (i + 1)],
                                                    e_rows[:, i * P // HALF, r * P:(r + 1) * P], eye_sb[0:EROWS, 0:EROWS],
                                                    start=True, stop=True)
                        last.then_inc(filled[0], 1)

                    def finish(g, at):
                        if at == 0:
                            pe.wait_ge(pm_copied, (g + 1) * HALVES + 1)
                            scores(g, 0, 4)
                        if at == 3:
                            scores(g, 4, 8)
                        if at == 6:
                            pe.wait_ge(st_copied, (g + 1) * HALVES + 1)
                            gates(g, 0)
                        if at == 9:
                            gates(g, 1)
                        if at == 12:
                            score_columns(g)

                    open_sums(0)
                    with pe.Fori(0, TURNS) as t:
                        for j in range(STEP):
                            chunk(0, t, j)
                    close_sums()
                    with pe.Fori(1, GROUPS) as g:
                        open_sums(g)
                        for at in range(FINISH_TURNS * STEP):
                            chunk(g, at // STEP, at % STEP)
                            finish(g - 1, at)
                        with pe.Fori(FINISH_TURNS, TURNS) as t:
                            for j in range(STEP):
                                chunk(g, t, j)
                        close_sums()
                    for at in range(FINISH_TURNS * STEP):
                        finish(GROUPS - 1, at)

                @block.vector
                def _(dve):
                    steps = [0]

                    def link(ins):
                        steps[0] += 1
                        ins.then_inc(dve_step, 1)
                        dve.wait_ge(dve_step, steps[0])

                    for start in (pm_copied, edge_ready, *emptied):
                        dve.sem_inc(start, 1)
                    nc.vector.memset(ones_sb[:, :], 1.0).then_inc(setup_made, 1)
                    nc.vector.memset(zeros_sb[:, :], 0.0).then_inc(setup_made, 1)
                    link(nc.vector.memset(u_all[:, :, :], 0.0))
                    nc.vector.memset(u_all[:, :, 0:1], 1.0)
                    dve.wait_ge(v_ready, 1)
                    nc.vector.tensor_copy(v_sb[:, :], ps_g[0][:, 0:EROWS]).then_inc(v_copied, 1)
                    dve.wait_ge(setup_loaded, 16 * len(SETUP))
                    for b in range(2):
                        link(nc.vector.tensor_tensor(half_rz[:, b, :], bias[:, 2 * b, 0:2], bias[:, 2 * b + 1, 0:2], ALU.add))
                        nc.vector.tensor_scalar(half_rz[:, b, :], half_rz[:, b, :], 0.5, None, ALU.mult)\
                          .then_inc(setup_made, 1)
                    dve.wait_ge(u_ready, 1)
                    link(nc.vector.tensor_copy(u_rest[:, :, :], ps_g[1][:, 0:TILES * EROWS].rearrange("p (t c) -> p t c", c=EROWS)))
                    for s in range(SPLITS):
                        part = u_all[:, :, 1 + s * EROWS:1 + (s + 1) * EROWS]
                        ins = nc.vector.tensor_copy(part, u_rest[:, :, :])
                        if s < SPLITS - 1:
                            link(ins)
                            link(nc.vector.tensor_tensor(u_rest[:, :, :], u_rest[:, :, :], part, ALU.subtract))
                        else:
                            ins.then_inc(u_split, 1)
                    before = steps[0]
                    PER_GROUP = 1 + HALVES * 3

                    def chain(g, done):
                        local = [done]

                        def link_g(ins):
                            local[0] += 1
                            ins.then_inc(dve_step, 1)
                            dve.wait_ge(dve_step, g * PER_GROUP + (before + local[0]))
                        return link_g

                    def chunk(g, t, j):
                        c = TILES * g + STEP * t + j
                        dve.wait_ge(chunk_staged, c + 1)
                        dve.wait_ge(chunk_done, c + 1 + RING1 - MASKS)
                        nc.vector.tensor_scalar(masks[:, j % MASKS, 0, :], chunks[:, j, :], 0.0, None, ALU.is_gt)
                        nc.vector.tensor_scalar(masks[:, j % MASKS, 1, :], chunks[:, j, :], 0.0, None, ALU.is_lt)\
                          .then_inc(masks_ready, 1)

                    def copy_sums(g):
                        dve.wait_ge(sums_closed, (g + 1) * 4)
                        for h in range(HALVES):
                            nc.vector.tensor_copy(pm_sb[:, h, :], ps_pm[h][0:2 * UCOLS, :]).then_inc(pm_copied, 1)

                    def count_negatives(g):
                        dve.wait_ge(pm_copied, (g + 1) * HALVES + 1)
                        chain(g, 0)(nc.vector.tensor_reduce(negatives[UCOLS:UCOLS + 1, bass.ds(g, 1)],
                                                            pm_sb[UCOLS:UCOLS + 1, :, :], axis=AX.XY, op=ALU.max))

                    def scores(g, first, last):
                        for i in range(first, last):
                            b, h = i % 4, i % 2
                            dve.wait_ge(slope_ready, g * 8 + i + 1)
                            if i < 2:
                                dst, rows = e_rows[:, h, :], EROWS
                            else:
                                dst, rows = neg_e_bc[:, i // 2 - 1, bass.ds(g * GROUP + h * HALF, HALF)], P
                            nc.vector.tensor_tensor(dst, ps_g[b][0:rows, :], sloped[0:rows, i % 2, :], ALU.min)\
                              .then_inc(emptied[b], 1)

                    def candidate(g, h):
                        dve.wait_ge(filled[2], g * USES[2] + 3 + h)
                        nc.vector.tensor_scalar(state_part[:, :], ps_g[2][:, :], bias[:, 1, 2:3], 0.5, ALU.add, ALU.mult)\
                          .then_inc(emptied[2], 1)
                        dve.wait_ge(emptied[2], g * USES[2] + 3 + h + 1)
                        dve.wait_ge(emptied[0], g * USES[0] + 3 + h + 1)
                        chain(g, 1 + 3 * h)(nc.vector.scalar_tensor_tensor(n_argument[:, :], reset_tanh[:, :], 1.0, state_part[:, :], ALU.add, ALU.mult))
                        dve.wait_ge(filled[3], g * USES[3] + 3 + h)
                        nc.vector.scalar_tensor_tensor(n_argument[:, :], ps_g[3][:, :], bias[:, 0, 2:3], n_argument[:, :], ALU.add, ALU.add)\
                          .then_inc(emptied[3], 1)

                    def edge_output(g, h):
                        link_g = chain(g, 2 + 3 * h)
                        state = xt_sb[:, bass.ds(g * GROUP + h * HALF, HALF)]
                        dve.wait_ge(n_ready, g * HALVES + h + 1)
                        link_g(nc.vector.tensor_tensor(diff[:, :], state, cand[:, :], ALU.subtract))
                        dve.wait_ge(emptied[1], g * USES[1] + 3 + h + 1)
                        link_g(nc.vector.scalar_tensor_tensor(diff[:, :], update_tanh[:, :], 1.0, diff[:, :], ALU.add, ALU.mult))
                        dve.wait_ge(edge_stored, (g * HALVES + h) * 16 + 1)
                        nc.vector.scalar_tensor_tensor(edge[:, :], diff[:, :], 0.5, cand[:, :], ALU.mult, ALU.add)\
                          .then_inc(edge_ready, 1)

                    def finish(g, at):
                        if at == 0:
                            count_negatives(g)
                        if at == 2:
                            dve.wait_ge(eminus_stored, g * 16 + 1)
                            scores(g, 0, 4)
                        if at == 5:
                            scores(g, 4, 8)
                        if at == 8:
                            candidate(g, 0)
                        if at == 10:
                            edge_output(g, 0)
                        if at == 11:
                            candidate(g, 1)
                        if at == 13:
                            edge_output(g, 1)
                        if at == 14:
                            dve.wait_ge(filled[0], (g + 1) * USES[0])
                            nc.vector.tensor_copy(neg_e_col[:, bass.ds(g * (GTILES * EROWS), GTILES * EROWS)],
                                                  ps_g[0][:, 0:GTILES * EROWS]).then_inc(emptied[0], 1)

                    with dve.Fori(0, TURNS) as t:
                        for j in range(STEP):
                            chunk(0, t, j)
                    copy_sums(0)
                    with dve.Fori(1, GROUPS) as g:
                        for at in range(FINISH_TURNS * STEP):
                            chunk(g, at // STEP, at % STEP)
                            finish(g - 1, at)
                        with dve.Fori(FINISH_TURNS, TURNS) as t:
                            for j in range(STEP):
                                chunk(g, t, j)
                        copy_sums(g)
                    for at in range(FINISH_TURNS * STEP):
                        finish(GROUPS - 1, at)
                    ins = nc.vector.tensor_reduce(negative_max[UCOLS:UCOLS + 1, :], negatives[UCOLS:UCOLS + 1, :],
                                                  axis=AX.X, op=ALU.max)
                    ins.then_inc(flag_made, 1)
                    dve.wait_ge(flag_made, 1)
                    nc.vector.tensor_copy(negative_int[UCOLS:UCOLS + 1, :], negative_max[UCOLS:UCOLS + 1, :])\
                      .then_inc(flag_made, 1)
                    dve.wait_ge(flag_made, 2)

        inputs2 = sem("inputs2")
        constants2 = sem("constants2")
        minus_half_made = sem("minus_half_made")
        row_clean = sem("row_clean")
        row_used = sem("row_used")
        eminus_loaded, eminus_used = sem("eminus_loaded"), sem("eminus_used")
        logits_used = sem("logits_used")
        half_ready = sem("half_ready")
        max_ready = sem("max_ready")
        max_diag = sem("max_diag")
        max_spread = sem("max_spread")
        slot_loaded = [sem(f"slot_loaded{i}") for i in range(RING2)]
        slot_staged = sem("slot_staged")
        clamped = sem("clamped")
        exponent_ready = sem("exponent_ready")
        weight_ready = sem("weight_ready")
        weight_used = sem("weight_used")
        product_ready = sem("product_ready")
        unit_done = sem("unit_done")
        heads_closed = sem("heads_closed")
        heads_copied = sem("heads_copied")
        misc_filled = [sem(f"misc_filled{b}") for b in range(2)]
        misc_read = [sem(f"misc_read{b}") for b in range(2)]
        scale_diag = sem("scale_diag")
        tail_loaded = sem("tail_loaded")
        node_n_ready = sem("node_n_ready")
        node_ready = sem("node_ready")
        var_ready, rstd_ready = sem("var_ready"), sem("rstd_ready")
        normed, stored = sem("normed"), sem("stored")
        dve_step2, dve_step3 = sem("dve_step2"), sem("dve_step3")
        last_loaded, last_scaled, last_mixed, last_mix_copied, last_gates, last_rz = (
            sem(n) for n in ("last_loaded", "last_scaled", "last_mixed", "last_mix_copied", "last_gates", "last_rz"))
        last_arg_ready, last_n_ready, last_node_ready, last_turned, last_var, last_rstd_ready, last_normed = (
            sem(n) for n in ("last_arg_ready", "last_n_ready", "last_node_ready", "last_turned", "last_var",
                             "last_rstd_ready", "last_normed"))

        with ExitStack() as two:
            def sb2(name, shape, dt=F32):
                return sb(name, shape, dt, two)

            ps_u = [[two.enter_context(nc.psum_tensor(f"ps_u{k}{h}", [P, HALF], F32)) for h in range(HALVES)]
                    for k in range(HEADS)]
            ps_m = [two.enter_context(nc.psum_tensor(f"ps_m{b}", [P, HALF], F32)) for b in range(2)]

            holes = sb2("holes", [P, N], BF16)
            logits = sb2("logits", [P, LOGIT_SLOTS, ROWHALF])
            slots = sb2("slots", [P, RING2, GROUP])
            x_ring = sb2("x_ring2", [P, RING2, H])
            weights = sb2("weights", [P, WEIGHTS, GROUP])
            products = sb2("products", [P, WEIGHTS, GROUP])
            neg_max_bc = sb2("neg_max_bc", [P, 2, HEADS, GROUP])
            heads = sb2("heads", [P, HEADS, GROUP])
            scratch = sb2("scratch", [P, PART])
            eminus = sb2("eminus", [P, PART])
            neg_half_max = sb2("neg_half_max", [P, 2 * HEADS])
            neg_max = sb2("neg_max", [P, PAIR * HEADS])
            expsum = sb2("expsum", [P, TILES * HEADS * 2])
            pair_sum = sb2("pair_sum", [P, PAIR * HEADS])
            inv_sum = sb2("inv_sum", [P, PAIR, HEADS])
            max_diag_sb = sb2("max_diag_sb", [P, HEADS, P])
            scale_diag_sb = sb2("scale_diag_sb", [P, HEADS, PAIR, P])
            third_eye = sb2("third_eye", [P, P])
            e_col = sb2("e_col", [P, TILES * EROWS])
            minus_half = sb2("minus_half", [P, PAIR])
            state, edge_sb, mix, reset_tanh, update_tanh, state_part, cand, diff = (
                sb2(n, [P, PW]) for n in ("state", "edge_sb", "mix", "reset_tanh2", "update_tanh2", "state_part2", "cand2", "diff2"))
            y = sb2("y", [P, PAIR, H])
            moments = sb2("moments", [P, PAIR, 6])
            mean_var = sb2("mean_var", [P, PAIR, 2])
            var_eps = sb2("var_eps", [P, PAIR])
            rstd = sb2("rstd", [P, PAIR])
            normal = sb2("normal", [P, PAIR, H])
            last_moments = sb2("last_moments", [P, GTILES, 6])
            last_mean_var = sb2("last_mean_var", [P, GTILES, 2])
            last_var_eps = sb2("last_var_eps", [P, GTILES])
            last_rstd = sb2("last_rstd", [P, GTILES])

            TAIL_USES = ["scale01", "scale2", "mix", "gates_rz", "gates_n"]
            ROW_ONLY = ["max0", "max1"]
            BOTH = TAIL_USES + ["max0", "turned", "max1"]
            WITH_OWN = ["scale01", "scale2", "own01", "own2", "mix", "gates_rz", "gates_n", "turned"]
            SECTIONS = [("rows", 0, ROW_ONLY)]
            for g in range(GROUPS):
                SECTIONS.append(("group", g, ROW_ONLY if g == 0 else BOTH if g < GROUPS - 1 else WITH_OWN))

            def use(section, t, what):
                before = TURNS * sum(len(uses) for _, _, uses in SECTIONS[:section])
                uses = SECTIONS[section][2]
                at = uses.index(what)
                return at % 2, t * (len(uses) // 2) + (before // 2 + at // 2)

            def has_rows(section):
                return "max0" in SECTIONS[section][2]

            def has_tail(section):
                return "mix" in SECTIONS[section][2]

            def has_own(section):
                return "own01" in SECTIONS[section][2]

            own_scale = neg_max_bc[:, GROUPS % 2, :, :]
            last_state, last_edge = row[:, 0:GROUP], row[:, GROUP:2 * GROUP]
            last_y = row[:, 2 * GROUP:3 * GROUP].rearrange("p (i h) -> p i h", h=H)
            last_normal = row[:, 3 * GROUP:4 * GROUP].rearrange("p (i h) -> p i h", h=H)
            last_mix, last_r = logits[:, 0, 0:GROUP], logits[:, 0, GROUP:2 * GROUP]
            last_z, last_arg = logits[:, 1, 0:GROUP], logits[:, 1, GROUP:2 * GROUP]
            last_n, last_node = logits[:, 2, 0:GROUP], logits[:, 2, GROUP:2 * GROUP]
            HTILES = HALF // P
            LAST_TILE = TILES - GTILES

            def half(buffer, h):
                return buffer[:, h * HALF:(h + 1) * HALF]

            def tiles_of(buffer, h):
                return buffer[:, h * HTILES:(h + 1) * HTILES]

            LAST_READ = [1 + TURNS * sum(len(uses) // 2 for _, _, uses in SECTIONS)] * 2

            MAX_SPREAD = [4, 7]

            def first_tile(section):
                return 0 if section == 0 else (SECTIONS[section][1] + 1) * GTILES

            def first_pair(section):
                return (SECTIONS[section][1] - 1) * (GTILES // PAIR)

            with nc.Block() as block:

                def on_negatives(eng, program):
                    count = eng.value_load(negative_int[UCOLS:UCOLS + 1, 0:1], min_val=0, max_val=N)
                    with eng.If(count > 0):
                        program(True)
                    with eng.Else():
                        program(False)

                def turns(eng, count=TURNS):
                    return eng.Fori(0, count)


                @block.sync
                def _(sp):
                    def load_row(tile):
                        sp.wait_ge(row_used, tile + 1)
                        sp.dma_start(row[:, :], adj_rows[bass.ds(tile, 1), :, :].rearrange("o p j -> p (o j)"))\
                          .then_inc(row_loaded, 16)

                    def load_chunk(c, slot):
                        if not isinstance(c, int) or c >= RING2:
                            sp.wait_ge(product_ready, (c + 1 - RING2) * HEADS + WEIGHTS)
                        sp.dma_start(slots[:, slot, :], adj_t[bass.ds(c, 1), :, :].rearrange("o p i -> p (o i)"))\
                          .then_inc(slot_loaded[slot], 16)

                    def load_eminus(tile):
                        for i in range(HEADS * N // PART):
                            k, part = divmod(i, N // PART)
                            sp.wait_ge(eminus_used, tile * (HEADS * N // PART) + (i + 1))
                            sp.dma_start(eminus[:, :], eminus_dram[k, part * PART:(part + 1) * PART].partition_broadcast(P))\
                              .then_inc(eminus_loaded, 16)

                    def turn(section, t, negative, more_rows=True, more_chunks=True):
                        name, g, _ = SECTIONS[section]
                        pair = t + first_pair(section)
                        if has_tail(section):
                            sp.wait_ge(node_ready, pair + 1)
                            cols = bass.ds(pair * PW, PW)
                            sp.dma_start(state[:, :], x_t[:, cols]).then_inc(tail_loaded, 16)
                            sp.dma_start(edge_sb[:, :], edge_dram[:, cols]).then_inc(tail_loaded, 16)
                        for j in range(STEP):
                            if has_rows(section) and j % (STEP // PAIR) == 0:
                                r = j // (STEP // PAIR)
                                tile = t * PAIR + (first_tile(section) + r)
                                if negative:
                                    load_eminus(tile)
                                if more_rows or r < PAIR - 1:
                                    load_row(tile + 1)
                            if name == "group" and (more_chunks or j < STEP - RING2):
                                load_chunk(t * STEP + (g * TILES + j + RING2), j % RING2)
                        if has_tail(section):
                            sp.wait_ge(normed, pair + 1)
                            sp.dma_start(out_tiles[:, bass.ds(pair * PAIR, PAIR), :], normal[:, :, :]).then_inc(stored, 16)

                    def program(negative):
                        for section in range(len(SECTIONS)):
                            if section == GROUPS:
                                sp.wait_ge(row_used, TILES + 1)
                                for dst, src in ((last_state, x_t), (last_edge, edge_dram)):
                                    sp.dma_start(dst, src[:, N - GROUP:N]).then_inc(last_loaded, 16)
                            last_rows = section == GROUPS - 1
                            last_chunks = section == GROUPS
                            whole_turns = TURNS - (last_rows or last_chunks)
                            with turns(sp, whole_turns) as t:
                                turn(section, t, negative)
                            if last_rows or last_chunks:
                                turn(section, TURNS - 1, negative, not last_rows, not last_chunks)

                    sp.sem_inc(stored, 1)
                    sp.dma_start(wg[:, 0, :], node_wih).then_inc(inputs2, 16)
                    sp.dma_start(wg[:, 1, :], node_whh).then_inc(inputs2, 16)
                    for c in range(RING2):
                        load_chunk(c, c)
                    on_negatives(sp, program)
                    for h in range(HALVES):
                        sp.wait_ge(last_normed, h + 1)
                        first = LAST_TILE + h * HTILES
                        sp.dma_start(out_tiles[:, first:first + HTILES, :], tiles_of(last_normal, h)).then_inc(stored, 16)
                    sp.wait_ge(stored, 16 * (LAST_TILE // PAIR + HALVES) + 1)


                @block.gpsimd
                def _(pool):
                    nc.gpsimd.memset(minus_half[:, :], -0.5).then_inc(minus_half_made, 1)
                    pool.wait_ge(minus_half_made, 1)

                    def turn(section, t):
                        name, g, _ = SECTIONS[section]
                        for j in range(STEP):
                            if has_rows(section) and j % (STEP // PAIR) == 0:
                                tile = t * PAIR + (first_tile(section) + j // (STEP // PAIR))
                                wait_apart(pool, pool_waits, row_loaded, (tile + 1) * 16)
                                own = row[:, bass.ds(tile * P, P)]
                                nc.gpsimd.tensor_tensor(own, own, keep_sb[:, GROUPS - 1, :], ALU.mult).then_inc(row_clean, 1)
                            if name == "group":
                                s = j % RING2
                                c = t * STEP + (g * TILES + j)
                                wait_apart(pool, pool_waits, slot_loaded[s],
                                           (t * (STEP // RING2) + (g * TILES // RING2 + j // RING2 + 1)) * 16)
                                own = slots[:, s, j * P:(j + 1) * P]
                                nc.gpsimd.tensor_tensor(
                                    own, own, keep_sb[:, bass.ds(t + (GROUPS - 1 - g), 1), :].rearrange("p o i -> p (o i)"),
                                    ALU.mult)
                                pool.wait_ge(unit_done, (c + 1) * HEADS)
                                nc.gpsimd.tensor_copy(x_ring[:, s, :], x_sb[:, bass.ds(t * STEP + j, 1), :].rearrange("p o i -> p (o i)"))\
                                  .then_inc(slot_staged, 1)
                            if has_tail(section) and j == STEP - 1:
                                pair = t + first_pair(section)
                                pool.wait_ge(var_ready, pair + 1)
                                nc.gpsimd.tensor_tensor(rstd[:, :], var_eps[:, :], minus_half[:, :], ALU.pow).then_inc(rstd_ready, 1)

                    for section in range(len(SECTIONS)):
                        with turns(pool) as t:
                            turn(section, t)
                    for h in range(HALVES):
                        pool.wait_ge(last_var, h + 1)
                        nc.gpsimd.tensor_tensor(tiles_of(last_rstd, h), tiles_of(last_var_eps, h),
                                                minus_half[:, 0:1].broadcast_to([P, HTILES]), ALU.pow).then_inc(last_rstd_ready, 1)


                @block.scalar
                def _(act):
                    def row_exps(tile, r, k):
                        act.wait_ge(max_ready, tile * HEADS + (k + 1))
                        for h in range(2):
                            slot = (HEADS * 2 * r + 2 * k + h) % LOGIT_SLOTS
                            nc.scalar.activation(logits[:, slot, :], logits[:, slot, :], ACT.Exp,
                                                 bias=neg_max[:, r * HEADS + k:r * HEADS + k + 1], scale=-1.0,
                                                 accum_out=expsum[:, bass.ds(tile * (2 * HEADS) + (2 * k + h), 1)])\
                              .then_inc(logits_used, 1)

                    def spread_copy(section, t, r):
                        b, n = use(section, t, f"max{r}")
                        act.wait_ge(misc_filled[b], n + 1)
                        parity = 0 if section == 0 else (SECTIONS[section][1] + 1) % 2
                        nc.scalar.activation(neg_max_bc[:, parity, :, bass.ds(t * PW + r * P, P)],
                                             ps_m[b][:, 0:HEADS * P].rearrange("p (k i) -> p k i", k=HEADS), ACT.Copy)\
                          .then_inc(misc_read[b], 1)

                    def bound(section, t, j, k, weight, column):
                        g = SECTIONS[section][1]
                        nc.scalar.activation(weight, neg_max_bc[:, g % 2, k, :], ACT.Relu, scale=-1.0,
                                             bias=neg_e_col[:, bass.ds(t * (STEP * EROWS) + (j * EROWS + column), 1)])\
                          .then_inc(exponent_ready, 1)

                    def weights_positive(section, t, j):
                        g = SECTIONS[section][1]
                        per, n = len(ACT_BOUNDS), len(DVE_CLAMPS)
                        steps = [("bound", k) for k in ACT_BOUNDS] + [("exp", k) for k in range(HEADS)]
                        if not has_rows(section):
                            steps = [(step, k) for k in range(HEADS) for step in ("bound", "exp")
                                     if step == "exp" or k in ACT_BOUNDS]
                        for step, k in steps:
                            weight = weights[:, k, :]
                            if step == "bound":
                                act.wait_ge(product_ready, t * HEAD_UNITS + (g * TILES * HEADS + j * HEADS + k + 1))
                                bound(section, t, j, k, weight, k)
                            elif k in DVE_CLAMPS:
                                act.wait_ge(clamped, t * (STEP * n) + ((g * TILES + j) * n + DVE_CLAMPS.index(k) + 1))
                                nc.scalar.activation(weight, weight, ACT.Exp).then_inc(weight_ready, 1)
                            else:
                                act.wait_ge(exponent_ready, t * (STEP * per) + ((g * TILES + j) * per + ACT_BOUNDS.index(k) + 1))
                                nc.scalar.activation(weight, weight, ACT.Exp, scale=-1.0).then_inc(weight_ready, 1)

                    def weights_negative(section, t, j):
                        g = SECTIONS[section][1]
                        per = 2 * HEADS
                        for k in range(HEADS):
                            for s in range(2):
                                i = 2 * (j * HEADS + k) + s
                                count = t * (STEP * per) + (g * TILES * per + i + 1)
                                weight = weights[:, i % WEIGHTS, :]
                                act.wait_ge(weight_used, count)
                                bound(section, t, j, k, weight, s * HEADS + k)
                                act.wait_ge(exponent_ready, count)
                                nc.scalar.activation(weight, weight, ACT.Exp, scale=-1.0).then_inc(weight_ready, 1)

                    def turn(section, t, negative):
                        name, g, _ = SECTIONS[section]
                        for j in range(STEP):
                            r, q = divmod(j, STEP // PAIR)
                            tile = t * PAIR + (first_tile(section) + r)
                            if has_rows(section) and q >= 1 and negative:
                                row_exps(tile, r, q - 1)
                            if name == "group":
                                (weights_negative if negative else weights_positive)(section, t, j)
                            if has_rows(section) and q >= 1 and not negative:
                                row_exps(tile, r, q - 1)
                            if has_tail(section):
                                pair = t + first_pair(section)
                                if has_own(section) and j == 2:
                                    for what, k0, k1 in (("own01", 0, 2), ("own2", 2, 3)):
                                        b, n = use(section, t, what)
                                        act.wait_ge(misc_filled[b], n + 1)
                                        nc.scalar.activation(own_scale[:, k0:k1, bass.ds(t * PW, PW)],
                                                             ps_m[b][:, 0:(k1 - k0) * PW].rearrange("p (k i) -> p k i", i=PW),
                                                             ACT.Copy).then_inc(misc_read[b], 1)
                                if j == 2 + has_own(section):
                                    b, n = use(section, t, "mix")
                                    act.wait_ge(misc_filled[b], n + 1)
                                    nc.scalar.activation(mix[:, :], ps_m[b][:, 0:PW], ACT.Copy).then_inc(misc_read[b], 1)
                                if j == 4:
                                    b, n = use(section, t, "gates_rz")
                                    act.wait_ge(misc_filled[b], n + 1)
                                    act.wait_ge(node_ready, pair + 1)
                                    nc.scalar.activation(reset_tanh[:, :], ps_m[b][:, 0:PW], ACT.Tanh, bias=half_rz[:, 1, 0:1], scale=0.5)
                                    nc.scalar.activation(update_tanh[:, :], ps_m[b][:, PW:2 * PW], ACT.Tanh, bias=half_rz[:, 1, 1:2], scale=0.5)\
                                      .then_inc(misc_read[b], 1)
                                if j == 5:
                                    b, n = use(section, t, "gates_n")
                                    act.wait_ge(misc_read[b], n + 2)
                                    nc.scalar.activation(cand[:, :], state_part[:, :], ACT.Tanh).then_inc(node_n_ready, 1)
                            if has_rows(section) and j in MAX_SPREAD:
                                spread_copy(section, t, MAX_SPREAD.index(j))

                    def program(negative):
                        for section in range(len(SECTIONS)):
                            name, g, _ = SECTIONS[section]
                            if name == "group":
                                for r in range(PAIR):
                                    b, n = use(section - 1, TURNS - 1, f"max{r}")
                                    act.wait_ge(misc_read[b], n + 2)
                            with turns(act) as t:
                                turn(section, t, negative)
                            if name == "group" and g < GROUPS - 1:
                                act.wait_ge(heads_closed, (g + 1) * HEADS * HALVES)
                                for k in range(HEADS):
                                    for h in range(HALVES):
                                        nc.scalar.activation(half(heads[:, k, :], h), ps_u[k][h][:, :], ACT.Copy)\
                                          .then_inc(heads_copied, 1)

                    act.sem_inc(logits_used, LOGIT_SLOTS)
                    act.wait_ge(constants2, 1)
                    on_negatives(act, program)

                    act.wait_ge(logits_used, TILES * HEADS * 2 + LOGIT_SLOTS)
                    for h in range(HALVES):
                        act.wait_ge(last_mixed, h + 1)
                        nc.scalar.activation(half(last_mix, h), ps_m[h][:, :], ACT.Copy).then_inc(last_mix_copied, 1)
                        act.wait_ge(last_gates, 4 * h + 1)
                        nc.scalar.activation(half(last_r, h), ps_u[0][h][:, :], ACT.Tanh, bias=half_rz[:, 1, 0:1], scale=0.5)\
                          .then_inc(last_rz, 1)
                        act.wait_ge(last_gates, 4 * h + 2)
                        nc.scalar.activation(half(last_z, h), ps_u[1][h][:, :], ACT.Tanh, bias=half_rz[:, 1, 1:2], scale=0.5)\
                          .then_inc(last_rz, 1)
                        act.wait_ge(last_arg_ready, h + 1)
                        nc.scalar.activation(half(last_n, h), half(last_arg, h), ACT.Tanh).then_inc(last_n_ready, 1)


                @block.tensor
                def _(pe):
                    pe.sem_inc(unit_done, RING2 * HEADS)
                    pe.wait_ge(inputs2, 32)
                    pe.wait_ge(constants2, 1)

                    def spread(section, t, what, ready, count, ncols, source):
                        b, n = use(section, t, what)
                        pe.wait_ge(misc_read[b], n + 1)
                        pe.wait_ge(ready, count)
                        nc.tensor.matmul(ps_m[b][:, 0:ncols], ones_sb[:, :], source, start=True, stop=True)\
                          .then_inc(misc_filled[b], 1)

                    def spread_max(section, t, tile, r):
                        spread(section, t, f"max{r}", max_diag, tile + 1, HEADS * P,
                               max_diag_sb[:, :, :].rearrange("p k i -> p (k i)"))

                    def turn(section, t):
                        name, g, _ = SECTIONS[section]
                        pair = t + first_pair(section)
                        cols = bass.ds(t * PW, PW)
                        for j in range(STEP):
                            if has_rows(section) and j in MAX_SPREAD:
                                r = MAX_SPREAD.index(j)
                                spread_max(section, t, t * PAIR + (first_tile(section) + r), r)
                            if has_tail(section) and j == 6:
                                b, n = use(section, t, "turned")
                                pe.wait_ge(misc_read[b], n + 1)
                                pe.wait_ge(node_ready, pair + 2)
                                for i in range(PAIR):
                                    last = nc.tensor.transpose(ps_m[b][:, i * P:(i + 1) * P], diff[:, i * P:(i + 1) * P], eye_sb[:, :])
                                last.then_inc(misc_filled[b], 1)
                            if name == "group":
                                c = t * STEP + (g * TILES + j)
                                pe.wait_ge(slot_staged, c + 1)
                                for k in range(HEADS):
                                    pe.wait_ge(product_ready, c * HEADS + (k + 1 + WEIGHTS))
                                    for h in range(HALVES):
                                        last = nc.tensor.matmul(ps_u[k][h][:, :], x_ring[:, j % RING2, :],
                                                                products[:, k, h * HALF:(h + 1) * HALF],
                                                                start=False, stop=False)
                                    last.then_inc(unit_done, 1)
                            if not has_tail(section):
                                continue
                            own = has_own(section)
                            for at, what, count in ((0, "scale", pair + t + 1 if own else pair + 1),
                                                    (1, "own", pair + t + 2)):
                                if j == at and (what == "scale" or own):
                                    spread(section, t, what + "01", scale_diag, count, 2 * PW,
                                           scale_diag_sb[:, 0:2, :, :].rearrange("p k r i -> p (k r i)"))
                                    spread(section, t, what + "2", scale_diag, count, PW,
                                           scale_diag_sb[:, 2, :, :].rearrange("p r i -> p (r i)"))
                            if j == 1 + own:
                                b, n = use(section, t, "mix")
                                for before in ("scale01", "scale2"):
                                    bb, nn = use(section, t, before)
                                    pe.wait_ge(misc_read[bb], nn + 2)
                                pe.wait_ge(misc_read[b], n + 1)
                                for k in range(HEADS):
                                    last = nc.tensor.matmul(ps_m[b][:, 0:PW], w_sb[:, k, :], heads[:, k, cols],
                                                            start=(k == 0), stop=(k == HEADS - 1))
                                last.then_inc(misc_filled[b], 1)
                            if j == 2 + own:
                                b, n = use(section, t, "gates_rz")
                                bb, nn = use(section, t, "mix")
                                pe.wait_ge(misc_read[bb], nn + 2)
                                pe.wait_ge(misc_read[b], n + 1)
                                pe.wait_ge(tail_loaded, (pair + 1) * 32)
                                for i in range(2):
                                    dst = ps_m[b][:, i * PW:(i + 1) * PW]
                                    nc.tensor.matmul(dst, wg[:, 0, i * H:(i + 1) * H], mix[:, :], start=True, stop=False)
                                    last = nc.tensor.matmul(dst, wg[:, 1, i * H:(i + 1) * H], state[:, :], start=False, stop=True)
                                last.then_inc(misc_filled[b], 1)
                                b, n = use(section, t, "gates_n")
                                pe.wait_ge(misc_read[b], n + 1)
                                nc.tensor.matmul(ps_m[b][:, 0:PW], wg[:, 0, 2 * H:3 * H], mix[:, :], start=True, stop=True)
                                nc.tensor.matmul(ps_m[b][:, PW:2 * PW], wg[:, 1, 2 * H:3 * H], state[:, :], start=True, stop=True)\
                                  .then_inc(misc_filled[b], 1)

                    for section in range(len(SECTIONS)):
                        name, g, _ = SECTIONS[section]
                        if name == "group":
                            pe.wait_ge(heads_copied, g * HEADS * HALVES)
                            for k in range(HEADS):
                                for h in range(HALVES):
                                    nc.tensor.matmul(ps_u[k][h][:, :], zeros_sb[:, 0:P], zeros_sb[:, :], start=True, stop=False)
                        with turns(pe) as t:
                            turn(section, t)
                        if name == "group":
                            for k in range(HEADS):
                                for h in range(HALVES):
                                    nc.tensor.matmul(ps_u[k][h][:, :], zeros_sb[:, 0:P], zeros_sb[:, :], start=False, stop=True)\
                                      .then_inc(heads_closed, 1)

                    for h in range(HALVES):
                        pe.wait_ge(misc_read[h], LAST_READ[h])
                    pe.wait_ge(last_loaded, 32)
                    for h in range(HALVES):
                        r_ps, z_ps, in_ps, state_ps = ps_u[0][h], ps_u[1][h], ps_u[2][h], ps_m[h]
                        own_state, mixed = half(last_state, h), half(last_mix, h)
                        pe.wait_ge(last_scaled, h + 1)
                        for k in range(HEADS):
                            last = nc.tensor.matmul(ps_m[h][:, :], w_sb[:, k, :], half(heads[:, k, :], h),
                                                    start=(k == 0), stop=(k == HEADS - 1))
                        last.then_inc(last_mixed, 1)
                        for i, gate_ps in ((0, r_ps), (1, z_ps)):
                            nc.tensor.matmul(gate_ps[:, :], wg[:, 1, i * H:(i + 1) * H], own_state, start=True, stop=False)
                        pe.wait_ge(last_mix_copied, h + 1)
                        for i, gate_ps in ((0, r_ps), (1, z_ps)):
                            nc.tensor.matmul(gate_ps[:, :], wg[:, 0, i * H:(i + 1) * H], mixed, start=False, stop=True)\
                              .then_inc(last_gates, 1)
                        nc.tensor.matmul(state_ps[:, :], wg[:, 1, 2 * H:3 * H], own_state, start=True, stop=True).then_inc(last_gates, 1)
                        nc.tensor.matmul(in_ps[:, :], wg[:, 0, 2 * H:3 * H], mixed, start=True, stop=True).then_inc(last_gates, 1)
                    for h in range(HALVES):
                        pe.wait_ge(last_node_ready, h + 1)
                        for i in range(HTILES):
                            tile = slice(h * HALF + i * P, h * HALF + (i + 1) * P)
                            last = nc.tensor.transpose(ps_u[0][h][:, i * P:(i + 1) * P], last_node[:, tile], eye_sb[:, :])
                        last.then_inc(last_turned, 1)


                @block.vector
                def _(dve):
                    def chain(expr_base):
                        local = [0]

                        def link(ins, apart=False):
                            local[0] += 1
                            ins.then_inc(dve_step2, 1)
                            if apart:
                                wait_apart(dve, dve_waits, dve_step2, expr_base + local[0])
                            else:
                                dve.wait_ge(dve_step2, expr_base + local[0])
                        link.local = local
                        return link

                    def row_holes(tile):
                        dve.wait_ge(row_clean, tile + 1)
                        return nc.vector.tensor_scalar(holes[:, :], row[:, :], 0.0, MASKED, ALU.is_le, ALU.mult)

                    def row_logits(tile, r, k, h):
                        slot = (HEADS * 2 * r + 2 * k + h) % LOGIT_SLOTS
                        wait_apart(dve, dve_waits, logits_used, tile * (2 * HEADS) + (2 * k + h + 1))
                        if (k, h) == (0, 0):
                            wait_apart(dve, dve_waits, row_used, tile + 2)
                        if h == 1:
                            wait_apart(dve, dve_waits, half_ready, tile * HEADS + (k + 1))
                        cols = slice(h * ROWHALF, (h + 1) * ROWHALF)
                        neg_half = neg_half_max[:, k:k + 1]
                        nc.vector.tensor_tensor_reduce(
                            out=logits[:, slot, :], in0=holes[:, cols], in1=neg_e_bc[:, k, cols], scale=1.0,
                            scalar=neg_half if h == 1 else HIGHEST, op0=ALU.add, op1=ALU.min,
                            accum_out=neg_max[:, r * HEADS + k:r * HEADS + k + 1] if h == 1 else neg_half)\
                          .then_inc(max_ready if h == 1 else half_ready, 1)

                    def row_max_negative(tile, r, k, link):
                        for h in range(2):
                            i = HEADS * 2 * r + 2 * k + h
                            slot = i % LOGIT_SLOTS
                            dve.wait_ge(logits_used, tile * (2 * HEADS) + (2 * k + h + 1))
                            for q in range(ROWHALF // PART):
                                part = h * (ROWHALF // PART) + q
                                cols = slice(part * PART, (part + 1) * PART)
                                dst = logits[:, slot, q * PART:(q + 1) * PART]
                                link(nc.vector.tensor_scalar(scratch[:, :], row[:, cols], 0.0, MASKED, ALU.is_ge, ALU.mult))
                                dve.wait_ge(eminus_loaded, (tile * (HEADS * N // PART) + (k * (N // PART) + part + 1)) * 16)
                                nc.vector.tensor_tensor(scratch[:, :], scratch[:, :], eminus[:, :], ALU.add)\
                                  .then_inc(eminus_used, 1)
                                link(nc.vector.tensor_tensor(dst, holes[:, cols], neg_e_bc[:, k, cols], ALU.add))
                                dve.wait_ge(eminus_used, tile * (HEADS * N // PART) + (k * (N // PART) + part + 2))
                                link(nc.vector.tensor_tensor(dst, dst, scratch[:, :], ALU.min))
                            link(nc.vector.tensor_reduce(neg_half_max[:, 2 * k + h:2 * k + h + 1], logits[:, slot, :], axis=AX.X, op=ALU.min))
                        nc.vector.tensor_scalar(neg_max[:, r * HEADS + k:r * HEADS + k + 1], neg_half_max[:, 2 * k:2 * k + 1],
                                                neg_half_max[:, 2 * k + 1:2 * k + 2], None, ALU.min).then_inc(max_ready, 1)

                    def row_diag(tile, r):
                        dve.wait_ge(max_ready, (tile + 1) * HEADS)
                        nc.vector.tensor_tensor(
                            max_diag_sb[:, :, :], eye_sb[:, :].unsqueeze(1).broadcast_to([P, HEADS, P]),
                            neg_max[:, r * HEADS:(r + 1) * HEADS].unsqueeze(2).broadcast_to([P, HEADS, P]), ALU.mult)\
                          .then_inc(max_diag, 1)

                    def clamp(section, t, j, k):
                        g = SECTIONS[section][1]
                        unit = t * HEAD_UNITS + (g * TILES * HEADS + j * HEADS + k)
                        dve.wait_ge(product_ready, unit + 1)
                        nc.vector.tensor_scalar(weights[:, k, :], neg_max_bc[:, g % 2, k, :],
                                                e_col[:, bass.ds(t * (STEP * EROWS) + (j * EROWS + k), 1)], 0.0,
                                                ALU.add, ALU.min).then_inc(clamped, 1)

                    def clamps(section, t, j):
                        if j == 0:
                            for r in range(PAIR):
                                b, n = use(section - 1, TURNS - 1, f"max{r}")
                                dve.wait_ge(misc_read[b], n + 2)
                        for k in DVE_CLAMPS:
                            clamp(section, t, j, k)

                    def column_units(section, t, j, negative, link):
                        g = SECTIONS[section][1]
                        for k in range(HEADS):
                            unit = t * HEAD_UNITS + (g * TILES * HEADS + j * HEADS + k)
                            slot = slots[:, j % RING2, :]
                            if k == 0:
                                dve.wait_ge(slot_staged, t * STEP + (g * TILES + j + 1))
                            dve.wait_ge(unit_done, unit + (1 + RING2 * HEADS - WEIGHTS))
                            if not negative:
                                dve.wait_ge(weight_ready, unit + 1)
                                nc.vector.tensor_tensor(products[:, k, :], weights[:, k, :], slot, ALU.mult)\
                                  .then_inc(product_ready, 1)
                                continue
                            i = 2 * (j * HEADS + k)
                            dve.wait_ge(weight_ready, unit * 2 + 2)
                            for q in range(GROUP // PART):
                                part = slice(q * PART, (q + 1) * PART)
                                link(nc.vector.tensor_scalar(scratch[:, :], slot[:, part], 0.0, None, ALU.max))
                                link(nc.vector.tensor_tensor(products[:, k, part], weights[:, i % WEIGHTS, part],
                                                             scratch[:, :], ALU.mult))
                                link(nc.vector.tensor_scalar(scratch[:, :], slot[:, part], 0.0, None, ALU.min))
                                link(nc.vector.tensor_tensor(scratch[:, :], weights[:, (i + 1) % WEIGHTS, part],
                                                             scratch[:, :], ALU.mult))
                                link(nc.vector.tensor_tensor(products[:, k, part], products[:, k, part], scratch[:, :], ALU.add))
                            dve.sem_inc(product_ready, 1)
                            dve.sem_inc(weight_used, 2)

                    def tail_scale_diag(section, t, pair, link):
                        sums = expsum[:, bass.ds(pair * (PAIR * HEADS * 2), PAIR * HEADS * 2)].rearrange("p (c h) -> p c h", h=2)
                        link(nc.vector.tensor_reduce(pair_sum[:, :], sums, axis=AX.X, op=ALU.add))
                        link(nc.vector.reciprocal(inv_sum[:, :, :].rearrange("p r k -> p (r k)"), pair_sum[:, :]))
                        nc.vector.tensor_tensor(
                            scale_diag_sb[:, :, :, :].rearrange("p k r i -> p k r i"),
                            third_eye[:, :].unsqueeze(1).unsqueeze(1).broadcast_to([P, HEADS, PAIR, P]),
                            inv_sum[:, :, :].rearrange("p r k -> p k r").unsqueeze(3).broadcast_to([P, HEADS, PAIR, P]), ALU.mult)\
                          .then_inc(scale_diag, 1)

                    def tail_scale(section, t):
                        cols = bass.ds(t * PW, PW)
                        dve.wait_ge(heads_copied, SECTIONS[section][1] * HEADS * HALVES)
                        for what, k0, k1 in (("scale01", 0, 2), ("scale2", 2, 3)):
                            b, n = use(section, t, what)
                            dve.wait_ge(misc_filled[b], n + 1)
                            part = heads[:, k0:k1, cols]
                            nc.vector.tensor_tensor(part, part, ps_m[b][:, 0:(k1 - k0) * PW].rearrange("p (k i) -> p k i", i=PW),
                                                    ALU.mult).then_inc(misc_read[b], 1)

                    def tail_candidate(section, t, link):
                        b, n = use(section, t, "gates_n")
                        dve.wait_ge(misc_filled[b], n + 1)
                        link(nc.vector.tensor_scalar(state_part[:, :], ps_m[b][:, PW:2 * PW], bias[:, 3, 2:3], 0.5, ALU.add, ALU.mult))
                        bb, nn = use(section, t, "gates_rz")
                        dve.wait_ge(misc_read[bb], nn + 2)
                        link(nc.vector.scalar_tensor_tensor(state_part[:, :], reset_tanh[:, :], 1.0, state_part[:, :], ALU.add, ALU.mult))
                        nc.vector.scalar_tensor_tensor(state_part[:, :], ps_m[b][:, 0:PW], bias[:, 2, 2:3], state_part[:, :], ALU.add, ALU.add)\
                          .then_inc(misc_read[b], 1)

                    def tail_state(pair, link):
                        dve.wait_ge(tail_loaded, (pair + 1) * 32)
                        dve.wait_ge(node_n_ready, pair + 1)
                        link(nc.vector.tensor_tensor(diff[:, :], state[:, :], cand[:, :], ALU.subtract))
                        link(nc.vector.scalar_tensor_tensor(diff[:, :], update_tanh[:, :], 1.0, diff[:, :], ALU.add, ALU.mult))
                        link(nc.vector.scalar_tensor_tensor(diff[:, :], diff[:, :], 0.5, cand[:, :], ALU.mult, ALU.add))
                        nc.vector.tensor_tensor(diff[:, :], diff[:, :], edge_sb[:, :], ALU.add).then_inc(node_ready, 1)

                    def tail_residual(section, t, pair, link):
                        b, n = use(section, t, "turned")
                        dve.wait_ge(misc_filled[b], n + 1)
                        for i in range(PAIR):
                            tile = pair * PAIR + i
                            ins = nc.vector.scalar_tensor_tensor(
                                y[:, i, :], ps_m[b][:, i * P:(i + 1) * P], d_sb[:, bass.ds(tile, 1)],
                                x_sb[:, bass.ds(tile, 1), :].rearrange("p o h -> p (o h)"), ALU.mult, ALU.add)
                        ins.then_inc(misc_read[b], 1)
                        dve.wait_ge(misc_read[b], n + 2)
                        for i in range(PAIR):
                            ins = nc.vector.bn_stats(moments[:, i, :], y[:, i, :])
                        link(ins, apart=True)
                        for i in range(PAIR):
                            ins = nc.vector.bn_aggr(mean_var[:, i, :], moments[:, i, :])
                        link(ins)
                        nc.vector.tensor_scalar(var_eps[:, :], mean_var[:, :, 1], EPS, None, ALU.add).then_inc(var_ready, 1)

                    def tail_norm(pair):
                        dve.wait_ge(rstd_ready, pair + 1)
                        dve.wait_ge(stored, pair * 16 + 1)
                        for i in range(PAIR):
                            ins = nc.vector.tensor_scalar(normal[:, i, :], y[:, i, :], mean_var[:, i, 0:1], rstd[:, i:i + 1],
                                                          ALU.subtract, ALU.mult)
                        ins.then_inc(normed, 1)

                    def turn(section, t, negative, link):
                        name, g, _ = SECTIONS[section]
                        pair = t + first_pair(section)
                        if name == "group":
                            if not negative and not has_rows(section):
                                clamps(section, t, 0)
                        for j in range(STEP):
                            r, q = divmod(j, STEP // PAIR)
                            tile = t * PAIR + (first_tile(section) + r)
                            if has_tail(section) and j == 0:
                                tail_scale_diag(section, t, pair, link)
                            if has_rows(section):
                                for part in ROW_PLAN[q] if not negative else []:
                                    if part == "holes":
                                        row_holes(tile).then_inc(row_used, 1)
                                    elif part == "bounds":
                                        if name == "group":
                                            clamps(section, t, j)
                                    elif part == "diagonal":
                                        row_diag(tile, r)
                                    else:
                                        row_logits(tile, r, *part)
                                if negative and q == 0:
                                    link(row_holes(tile))
                                if negative and q < HEADS:
                                    row_max_negative(tile, r, q, link)
                                if negative and q == HEADS:
                                    dve.sem_inc(row_used, 1)
                                    row_diag(tile, r)
                            residual_first = has_rows(section)
                            if has_tail(section) and j == STEP - 1 and residual_first:
                                tail_residual(section, t, pair, link)
                            if name == "group":
                                column_units(section, t, j, negative, link)
                                in_plan = has_rows(section) and (j + 1) % len(ROW_PLAN) == 0
                                if not negative and j < STEP - 1 and not in_plan:
                                    clamps(section, t, j + 1)
                            if has_tail(section):
                                if j == 1:
                                    tail_scale(section, t)
                                    if has_own(section):
                                        tail_scale_diag(section, t, pair + TURNS, link)
                                if j == 4:
                                    tail_candidate(section, t, link)
                                if j == 5:
                                    tail_state(pair, link)
                                if j == STEP - 1:
                                    if not residual_first:
                                        tail_residual(section, t, pair, link)
                                    tail_norm(pair)

                    ROW_LINKS = {False: 0, True: PAIR * (1 + HEADS * 2 * (1 + 3 * ROWHALF // PART))}
                    COLUMN_LINKS = {False: 0, True: HEAD_UNITS * 5 * (GROUP // PART)}
                    TAIL_LINKS = 2 + 2 + 3 + 2

                    def program(negative):
                        done = 1
                        for section in range(len(SECTIONS)):
                            name, g, _ = SECTIONS[section]
                            per_turn = (has_rows(section) * ROW_LINKS[negative] + (name == "group") * COLUMN_LINKS[negative]
                                        + has_tail(section) * TAIL_LINKS + has_own(section) * 2)
                            with turns(dve) as t:
                                link = chain(t * per_turn + done)
                                turn(section, t, negative, link)
                                assert link.local[0] == per_turn, (link.local, per_turn)
                            done += TURNS * per_turn

                    nc.vector.tensor_scalar(e_col[:, :], neg_e_col[:, :], -1.0, None, ALU.mult)
                    nc.vector.tensor_scalar(third_eye[:, :], eye_sb[:, :], 1.0 / HEADS, None, ALU.mult).then_inc(constants2, 1)
                    dve.sem_inc(row_used, 1)
                    dve.sem_inc(eminus_used, 1)
                    dve.sem_inc(weight_used, WEIGHTS)
                    dve.sem_inc(product_ready, WEIGHTS)
                    dve.sem_inc(dve_step2, 1)
                    dve.sem_inc(node_ready, 1)
                    for b in range(2):
                        dve.sem_inc(misc_read[b], 1)
                    dve.wait_ge(constants2, 1)
                    dve.wait_ge(d_loaded, 16)
                    on_negatives(dve, program)

                    steps = [0]

                    def link(ins):
                        steps[0] += 1
                        ins.then_inc(dve_step3, 1)
                        dve.wait_ge(dve_step3, steps[0])

                    def last_candidate(h):
                        arg = half(last_arg, h)
                        dve.wait_ge(last_gates, 4 * h + 3)
                        link(nc.vector.tensor_scalar(arg, ps_m[h][:, :], bias[:, 3, 2:3], 0.5, ALU.add, ALU.mult))
                        dve.wait_ge(last_rz, 2 * h + 1)
                        link(nc.vector.scalar_tensor_tensor(arg, half(last_r, h), 1.0, arg, ALU.add, ALU.mult))
                        dve.wait_ge(last_gates, 4 * h + 4)
                        nc.vector.scalar_tensor_tensor(arg, ps_u[2][h][:, :], bias[:, 2, 2:3], arg, ALU.add, ALU.add)\
                          .then_inc(last_arg_ready, 1)

                    def last_output(h):
                        node, n = half(last_node, h), half(last_n, h)
                        dve.wait_ge(last_n_ready, h + 1)
                        link(nc.vector.tensor_tensor(node, half(last_state, h), n, ALU.subtract))
                        dve.wait_ge(last_rz, 2 * h + 2)
                        link(nc.vector.scalar_tensor_tensor(node, half(last_z, h), 1.0, node, ALU.add, ALU.mult))
                        link(nc.vector.scalar_tensor_tensor(node, node, 0.5, n, ALU.mult, ALU.add))
                        nc.vector.tensor_tensor(node, node, half(last_edge, h), ALU.add).then_inc(last_node_ready, 1)

                    def last_residual(h):
                        dve.wait_ge(last_turned, h + 1)
                        for i in range(h * HTILES, (h + 1) * HTILES):
                            r = i - h * HTILES
                            ins = nc.vector.scalar_tensor_tensor(
                                last_y[:, i, :], ps_u[0][h][:, r * P:(r + 1) * P], d_sb[:, LAST_TILE + i:LAST_TILE + i + 1],
                                x_sb[:, LAST_TILE + i, :], ALU.mult, ALU.add)
                        link(ins)
                        for i in range(h * HTILES, (h + 1) * HTILES):
                            ins = nc.vector.bn_stats(last_moments[:, i, :], last_y[:, i, :])
                        link(ins)
                        for i in range(h * HTILES, (h + 1) * HTILES):
                            ins = nc.vector.bn_aggr(last_mean_var[:, i, :], last_moments[:, i, :])
                        link(ins)
                        nc.vector.tensor_scalar(tiles_of(last_var_eps, h), tiles_of(last_mean_var, h)[:, :, 1], EPS, None, ALU.add)\
                          .then_inc(last_var, 1)

                    def last_norm(h):
                        dve.wait_ge(last_rstd_ready, h + 1)
                        for i in range(h * HTILES, (h + 1) * HTILES):
                            ins = nc.vector.tensor_scalar(last_normal[:, i, :], last_y[:, i, :], last_mean_var[:, i, 0:1],
                                                          last_rstd[:, i:i + 1], ALU.subtract, ALU.mult)
                        ins.then_inc(last_normed, 1)

                    dve.wait_ge(heads_closed, GROUPS * HEADS * HALVES)
                    dve.wait_ge(logits_used, TILES * HEADS * 2 + LOGIT_SLOTS)
                    dve.wait_ge(last_loaded, 32)
                    for b in range(2):
                        dve.wait_ge(misc_read[b], LAST_READ[b])
                    for h in range(HALVES):
                        for k in range(HEADS):
                            ins = nc.vector.tensor_tensor(half(heads[:, k, :], h), ps_u[k][h][:, :], half(own_scale[:, k, :], h),
                                                          ALU.mult)
                        ins.then_inc(last_scaled, 1)
                    last_candidate(0)
                    last_output(0)
                    last_candidate(1)
                    last_residual(0)
                    last_output(1)
                    last_norm(0)
                    last_residual(1)
                    last_norm(1)


_OUTS = [((N, H), "float32")]


def kernel(**inputs):
    import numpy as _np
    import concourse.bacc as _bacc
    from concourse import mybir as _mybir
    from concourse.bass_utils import run_bass_kernel_spmd as _run

    c = _np.ascontiguousarray
    pre = "L0_gnn_"
    adj, x = _np.asarray(inputs["adj"]), _np.asarray(inputs["x"])
    gate_biases = [_np.asarray(inputs[pre + n]).reshape(3, H).T for n in ("edge_bih", "edge_bhh", "node_bih", "node_bhh")]
    row_pick = _np.zeros((2 * UCOLS, EROWS), _np.float32)
    for k in range(HEADS):
        for s in range(SPLITS):
            first = 1 + s * EROWS + 2 * k
            row_pick[[first, UCOLS + first + 1], k] = -1.0
            row_pick[[first + 1, UCOLS + first], HEADS + k] = -1.0
    keep = _np.ones((P, KEEP, P), _np.float32)
    keep[:, GROUPS - 1, :] -= _np.eye(P, dtype=_np.float32)
    w = _np.asarray(inputs[pre + "gat_W"])
    arrays = {
        "x": c(x), "x_t": c(x.T), "adj": c(adj),
        "adj_t": c(adj.T.reshape(N, GROUPS, GROUP).transpose(1, 0, 2)).reshape(GROUPS * TILES, P, GROUP),
        "w": c(w), "w_t": c(w.transpose(0, 2, 1)),
        "a_t": c(_np.asarray(inputs[pre + "gat_a"]).reshape(EROWS, H).T),
        "edge_wih": c(_np.asarray(inputs[pre + "edge_Wih"]).T), "edge_whh": c(_np.asarray(inputs[pre + "edge_Whh"]).T),
        "node_wih": c(_np.asarray(inputs[pre + "node_Wih"]).T), "node_whh": c(_np.asarray(inputs[pre + "node_Whh"]).T),
        "biases": c(_np.concatenate(gate_biases, axis=1)),
        "row_pick": row_pick, "bc_pick": c(_np.repeat(row_pick[:, :HEADS, None], P, axis=2)),
        "eye": _np.eye(P, dtype=_np.float32), "keep": keep,
    }
    nc = _bacc.Bacc("TRN2", target_bir_lowering=False, num_devices=1, dynamic_dma_scratch_size=1024)
    args = [nc.dram_tensor(f"in_{n}", a.shape, _mybir.dt.from_np(a.dtype), kind="ExternalInput").ap() for n, a in arrays.items()]
    for i, (shape, dtype) in enumerate(_OUTS):
        args.append(nc.dram_tensor(f"out_{i}", shape, _mybir.dt.from_np(_np.dtype(dtype)), kind="ExternalOutput").ap())
    gnn_kernel(nc, *args)
    r = _run(nc, [{f"in_{n}": a for n, a in arrays.items()}], core_ids=[0])
    return r.results[0]["out_0"]
```
